# Optimizing a Trainium2 kernel written in Bass

```python
import numpy as np
import jax
import jax.numpy as jnp

def _softmax(x, axis=-1):
    return jax.nn.softmax(x, axis=axis)

def _gelu(x):
    return jax.nn.gelu(x, approximate=True)

def _silu(x):
    return jax.nn.silu(x)

def _sigmoid(x):
    return jax.nn.sigmoid(x)

def _layernorm(x, axis=-1, eps=1e-05):
    m = jnp.mean(x, axis=axis, keepdims=True)
    v = jnp.var(x, axis=axis, keepdims=True)
    return (x - m) / jnp.sqrt(v + eps)

def _scatter_add(tgt, idx, src, axis=0):
    return tgt.at[idx].add(src)

def _segment_sum(src, seg, n):
    return jax.ops.segment_sum(src, seg, n)
kernel_name = 'mk_perceiver_d1_seqx_r4_5be24a'

def setup_inputs(seed: int=0):
    np.random.seed(seed)
    _w = jnp.asarray

    def _rec_inputs():
        import jax
        import jax.numpy as jnp
        _rk = jax.random.key(seed)
        x = 7.22e-05 + 1 * jax.random.normal(jax.random.fold_in(_rk, 1), (4, 256, 256), jnp.float32)
        _lenS = 256 - jax.random.randint(jax.random.fold_in(_rk, 7), (4,), 0, max(1, 256 // 4) + 1, jnp.int32)
        _lenS2 = 4096 - jax.random.randint(jax.random.fold_in(_rk, 8), (4,), 0, max(1, 4096 // 4) + 1, jnp.int32)
        _ctx_1024P = jax.random.normal(jax.random.fold_in(_rk, 11), (4, 16, 256), jnp.float32)
        _ctx_1024c = jax.random.dirichlet(jax.random.fold_in(_rk, 511), 0.3 * jnp.ones((16,), jnp.float32), (4, 4096))
        _ctx_1024t = jnp.einsum('bsk,bkd->bsd', _ctx_1024c, _ctx_1024P)
        _ctx_1024t = _ctx_1024t * jax.lax.rsqrt(jnp.mean(jnp.square(_ctx_1024t)) + 1e-12) * 0.953939
        ctx_1024 = 4.13588e-05 + 0.999923 * (_ctx_1024t + 0.3 * jax.random.normal(jax.random.fold_in(_rk, 611), (4, 4096, 256), jnp.float32))
        return (x, ctx_1024)
    x, ctx_1024 = _rec_inputs()

    def _L0_xattn_setup():
        import jax, jax.numpy as jnp
        import numpy as np
        C = 256
        B, SQ, SKV = (4, 512, 512)
        key = jax.random.key(seed)
        ks = jax.random.split(key, 10)
        s = 1.0 / np.sqrt(C)
        return {'x': jax.random.normal(ks[0], (B, SQ, C), jnp.float32), 'content_embeddings': jax.random.normal(ks[1], (B, SKV, C), jnp.float32), 'Wq': jax.random.normal(ks[2], (C, C), jnp.float32) * s, 'bq': jnp.zeros((C,), jnp.float32), 'Wk': jax.random.normal(ks[3], (C, C), jnp.float32) * s, 'bk': jnp.zeros((C,), jnp.float32), 'Wv': jax.random.normal(ks[4], (C, C), jnp.float32) * s, 'bv': jnp.zeros((C,), jnp.float32), 'Wo': jax.random.normal(ks[5], (C, C), jnp.float32) * s, 'bo': jnp.zeros((C,), jnp.float32)}
    _L0_xattn_all = _L0_xattn_setup()
    _L0_xattn_in = {k: v for k, v in _L0_xattn_all.items() if k in ('Wq', 'bq', 'Wk', 'bk', 'Wv', 'bv', 'Wo', 'bo')}
    del _L0_xattn_all

    def _L0_attn_setup():
        import jax, jax.numpy as jnp
        import numpy as np
        NUM_HEADS = 16
        FOCUS_FACTOR = 1.6
        HEAD_REGION = {0: 0, 1: 1, 2: 2}

        def _region_multipliers(seq_len: int, num_heads: int, factor: float) -> jnp.ndarray:
            first_end = max(1, seq_len // 3)
            second_end = max(first_end + 1, 2 * seq_len // 3)
            pos = jnp.arange(seq_len)
            regions = [pos < first_end, (pos >= first_end) & (pos < second_end), pos >= second_end]
            mult = np.ones((num_heads, seq_len), dtype=np.float32)
            mult = jnp.asarray(mult)
            for h, r in HEAD_REGION.items():
                if h < num_heads:
                    mult = mult.at[h].set(1.0 + (factor - 1.0) * regions[r].astype(jnp.float32))
            return mult
        key = jax.random.key(seed)
        k1, k2, k3, k4, k5 = jax.random.split(key, 5)
        B, S, D = (2, 512, 256)
        return {'hidden_states': jax.random.normal(k1, (B, S, D), dtype=jnp.float32), 'c_attn_w': jax.random.normal(k2, (D, 3 * D), dtype=jnp.float32) * 0.02, 'c_attn_b': jax.random.normal(k3, (3 * D,), dtype=jnp.float32) * 0.02, 'c_proj_w': jax.random.normal(k4, (D, D), dtype=jnp.float32) * 0.02, 'c_proj_b': jax.random.normal(k5, (D,), dtype=jnp.float32) * 0.02}
    _L0_attn_all = _L0_attn_setup()
    _L0_attn_in = {k: v for k, v in _L0_attn_all.items() if k in ('c_attn_w', 'c_attn_b', 'c_proj_w', 'c_proj_b')}
    del _L0_attn_all

    def _L0_ffn_setup():
        import jax, jax.numpy as jnp
        import numpy as np
        T, Z, D_DIM = (8, 512, 256)
        N_EXP, P_SLOT, H = (64, 32, 256)
        LN_EPS = 1e-05
        key = jax.random.key(seed)
        k = jax.random.split(key, 5)
        s = 0.02
        return {'x': jax.random.normal(k[0], (T, Z, D_DIM), dtype=jnp.float32), 'phi_w': jax.random.normal(k[1], (N_EXP * P_SLOT, D_DIM), dtype=jnp.float32) * s, 'phi_b': jax.random.normal(k[2], (N_EXP * P_SLOT,), dtype=jnp.float32) * s, 'expert_w': jax.random.normal(k[3], (N_EXP, D_DIM, H), dtype=jnp.float32) * s, 'expert_b': jax.random.normal(k[4], (N_EXP, H), dtype=jnp.float32) * s}
    _L0_ffn_all = _L0_ffn_setup()
    _L0_ffn_in = {k: v for k, v in _L0_ffn_all.items() if k in ('phi_w', 'phi_b', 'expert_w', 'expert_b')}
    del _L0_ffn_all
    return {'x': x, 'ctx_1024': ctx_1024, 'L0_xattn_Wq': _L0_xattn_in['Wq'], 'L0_xattn_bq': _L0_xattn_in['bq'], 'L0_xattn_Wk': _L0_xattn_in['Wk'], 'L0_xattn_bk': _L0_xattn_in['bk'], 'L0_xattn_Wv': _L0_xattn_in['Wv'], 'L0_xattn_bv': _L0_xattn_in['bv'], 'L0_xattn_Wo': _L0_xattn_in['Wo'], 'L0_xattn_bo': _L0_xattn_in['bo'], 'L0_attn_c_attn_w': _L0_attn_in['c_attn_w'], 'L0_attn_c_attn_b': _L0_attn_in['c_attn_b'], 'L0_attn_c_proj_w': _L0_attn_in['c_proj_w'], 'L0_attn_c_proj_b': _L0_attn_in['c_proj_b'], 'L0_ffn_phi_w': _L0_ffn_in['phi_w'], 'L0_ffn_phi_b': _L0_ffn_in['phi_b'], 'L0_ffn_expert_w': _L0_ffn_in['expert_w'], 'L0_ffn_expert_b': _L0_ffn_in['expert_b']}

def reference(x, ctx_1024, L0_xattn_Wq, L0_xattn_bq, L0_xattn_Wk, L0_xattn_bk, L0_xattn_Wv, L0_xattn_bv, L0_xattn_Wo, L0_xattn_bo, L0_attn_c_attn_w, L0_attn_c_attn_b, L0_attn_c_proj_w, L0_attn_c_proj_b, L0_ffn_phi_w, L0_ffn_phi_b, L0_ffn_expert_w, L0_ffn_expert_b):
    import jax
    import jax.numpy as jnp

    def _L0_xattn_ref(x, content_embeddings, Wq, bq, Wk, bk, Wv, bv, Wo, bo):
        import jax, jax.numpy as jnp
        import numpy as np
        C = 256
        B, SQ, SKV = (4, 512, 512)
        queries = x @ Wq.T + bq
        keys = content_embeddings @ Wk.T + bk
        values = content_embeddings @ Wv.T + bv
        scale = 1.0 / jnp.sqrt(jnp.asarray(C, x.dtype))
        scores = jnp.einsum('bqc,bkc->bqk', queries, keys) * scale
        attn = jax.nn.softmax(scores, axis=-1)
        attended = jnp.einsum('bqk,bkc->bqc', attn, values)
        out = x + attended
        return out @ Wo.T + bo

    def _L0_attn_ref(hidden_states, c_attn_w, c_attn_b, c_proj_w, c_proj_b):
        import jax, jax.numpy as jnp
        import numpy as np
        NUM_HEADS = 16
        FOCUS_FACTOR = 1.6
        HEAD_REGION = {0: 0, 1: 1, 2: 2}

        def _region_multipliers(seq_len: int, num_heads: int, factor: float) -> jnp.ndarray:
            first_end = max(1, seq_len // 3)
            second_end = max(first_end + 1, 2 * seq_len // 3)
            pos = jnp.arange(seq_len)
            regions = [pos < first_end, (pos >= first_end) & (pos < second_end), pos >= second_end]
            mult = np.ones((num_heads, seq_len), dtype=np.float32)
            mult = jnp.asarray(mult)
            for h, r in HEAD_REGION.items():
                if h < num_heads:
                    mult = mult.at[h].set(1.0 + (factor - 1.0) * regions[r].astype(jnp.float32))
            return mult
        B, S, D = hidden_states.shape
        H = NUM_HEADS
        hd = D // H
        qkv = hidden_states @ c_attn_w + c_attn_b
        q, k, v = jnp.split(qkv, 3, axis=-1)

        def _reshape(x):
            return x.reshape(B, S, H, hd).transpose(0, 2, 1, 3)
        q, k, v = (_reshape(q), _reshape(k), _reshape(v))
        scores = jnp.einsum('bhqd,bhkd->bhqk', q, k) / jnp.sqrt(jnp.float32(hd))
        causal = jnp.tril(jnp.ones((S, S), dtype=bool))
        mask_value = jnp.finfo(scores.dtype).min
        scores = jnp.where(causal[None, None], scores, mask_value)
        attn = jax.nn.softmax(scores, axis=-1)
        mult = _region_multipliers(S, H, FOCUS_FACTOR)
        scaled = attn * mult[None, :, None, :]
        scaled = scaled / jnp.sum(scaled, axis=-1, keepdims=True)
        div_heads = jnp.zeros((H,), dtype=bool)
        for h in HEAD_REGION:
            if h < H:
                div_heads = div_heads.at[h].set(True)
        attn = jnp.where(div_heads[None, :, None, None], scaled, attn)
        out = jnp.einsum('bhqk,bhkd->bhqd', attn, v)
        out = out.transpose(0, 2, 1, 3).reshape(B, S, D)
        out = out @ c_proj_w + c_proj_b
        return out

    def _L0_ffn_ref(x, phi_w, phi_b, expert_w, expert_b):
        import jax, jax.numpy as jnp
        import numpy as np
        T, Z, D_DIM = (8, 512, 256)
        N_EXP, P_SLOT, H = (64, 32, 256)
        LN_EPS = 1e-05
        t, z, d = x.shape
        n = expert_w.shape[0]
        p = phi_w.shape[0] // n
        logits = (jnp.einsum('tzd,ed->tze', x, phi_w) + phi_b).reshape(t, z, n, p)
        D = jax.nn.softmax(logits, axis=3)
        C = jax.nn.softmax(logits, axis=2)
        X_tilde = jnp.einsum('tznp,tzd->npd', D, x)
        X_tilde = jnp.clip(X_tilde, -33000.0, 65000.0)
        mu = jnp.mean(X_tilde, axis=-1, keepdims=True)
        var = jnp.mean(jnp.square(X_tilde - mu), axis=-1, keepdims=True)
        X_tilde = (X_tilde - mu) * jax.lax.rsqrt(var + LN_EPS)
        X_tilde = jnp.tanh(X_tilde)
        Y_tilde = jnp.einsum('npd,ndH->npH', X_tilde, expert_w) + expert_b[:, None, :]
        Y = jnp.einsum('tznp,npH->tzH', C, Y_tilde)
        return Y
    x = x + _L0_xattn_ref(_layernorm(x, axis=-1), ctx_1024, L0_xattn_Wq, L0_xattn_bq, L0_xattn_Wk, L0_xattn_bk, L0_xattn_Wv, L0_xattn_bv, L0_xattn_Wo, L0_xattn_bo)
    x = x + _L0_attn_ref(_layernorm(x, axis=-1), L0_attn_c_attn_w, L0_attn_c_attn_b, L0_attn_c_proj_w, L0_attn_c_proj_b)
    x = x + _L0_ffn_ref(_layernorm(x, axis=-1), L0_ffn_phi_w, L0_ffn_phi_b, L0_ffn_expert_w, L0_ffn_expert_b)
    return x

_drawn_inputs = setup_inputs


def setup_inputs(seed=0):
    import zlib

    import numpy as np

    out = dict(_drawn_inputs(seed))
    spreads = {'L0_xattn_bq': (0.0, 0.361),
     'L0_xattn_bk': (0.0, 2.0),
     'L0_xattn_bv': (0.0, 0.1),
     'L0_xattn_bo': (0.0, 0.1)}
    factors = {'L0_attn_c_attn_b': 4.386, 'L0_ffn_phi_b': 35.003}
    for name, (base, spread) in spreads.items():
        noise = np.random.default_rng([zlib.crc32(name.encode()), seed]).standard_normal(out[name].shape)
        drawn = base * np.exp(spread * noise) if base else spread * noise
        out[name] = jnp.asarray(drawn.astype(out[name].dtype))
    for name, factor in factors.items():
        out[name] = (out[name] * factor).astype(out[name].dtype)
    return out
```

```python
from contextlib import ExitStack

import concourse.bass as bass
from concourse import mybir

P = 128
B, S, D = 4, 256, 256
NCTX = 4096
TT = B * S // P
QT = S // P
DH = D // P
CH = 512
J = CH // P
SLOTS = 4
NCH = NCTX // CH
LN_EPS = 1e-5

F32 = mybir.dt.float32
F32R = mybir.dt.float32r
BF16 = mybir.dt.bfloat16
ALU = mybir.AluOpType
ACT = mybir.ActivationFunctionType
AX = mybir.AxisListType


def at_least(eng, sem, value):
    if not isinstance(value, int) or value > 0:
        eng.wait_ge(sem, value)


def half_wait(k):
    return k // 2 + 1


def cross_attention(nc, x_sb, ident, x, ctx, Wq, bq, Wk, bk, Wv, bv, Wo, bo):
    SCALE = 1.0 / 16.0
    with ExitStack() as st:
        def sb(name, shape, dt=F32):
            return st.enter_context(nc.sbuf_tensor(name, shape, dt))

        def sem(name):
            return st.enter_context(nc.semaphore(name))

        ctx_in_sb = sb("ctx_stage", [P, SLOTS, J * D])
        ctx_hi = sb("ctx_hi", [P, NCH * J * D], F32R)
        ctx_lo = sb("ctx_lo", [P, NCH * J * D], F32R)
        scores = sb("scores", [P, QT, NCTX])
        ctxT_hi = sb("ctxT_hi", [P, 2, DH, CH], F32R)
        ctxT_lo = sb("ctxT_lo", [P, 2, DH, CH], F32R)
        probs = sb("probs", [P, 2, QT, CH])
        pT_hi = sb("pT_hi", [P, 2, QT, CH], F32R)
        pT_lo = sb("pT_lo", [P, 2, QT, CH], F32R)
        qk_hi = sb("qk_hi", [P, DH, B * S], F32R)
        qk_lo = sb("qk_lo", [P, DH, B * S], F32R)
        h_nat = sb("h_nat", [P, TT, D])
        hT = sb("hT", [P, DH, B * S])
        qT = scores[:, 0, 0:DH * B * S].rearrange("p (a t) -> p a t", a=DH)
        w_nat = {w: scores[:, 1, k * DH * D:(k + 1) * DH * D].rearrange("p (a d) -> p a d", a=DH)
                 for k, w in enumerate("qkvo")}
        qk_hi_b = sb("qk_hi_b", [P, DH, S], F32R)
        qk_lo_b = sb("qk_lo_b", [P, DH, S], F32R)
        wT = {w: sb(f"wT_{w}", [P, DH, D]) for w in "qvo"}
        bias = {w: sb(f"b_{w}", [P, DH]) for w in "qkv"}
        bo_all = sb("bo_all", [P, D])
        stats = sb("stats", [P, TT, 6])
        mv = sb("mv", [P, TT, 2])
        ve = sb("ve", [P, TT])
        rstd = sb("rstd", [P, TT])
        power = sb("power", [P, TT])
        qbk = sb("qbk", [P, TT])
        cmax = sb("cmax", [P, QT, NCH])
        rowmax = sb("rowmax", [P, QT])
        negmax = sb("negmax", [P, QT])
        csum = sb("csum", [P, QT, NCH])
        rowsum = sb("rowsum", [P, QT])
        rinv = sb("rinv", [P, QT])
        att = h_nat
        attT = qT
        zT = hT

        bank = [st.enter_context(nc.psum_tensor(f"ps{i}", [P, 512], F32)) for i in range(8)]
        pT, pS, pE, pO = bank[0:2], bank[2:4], bank[4:6], bank[6:8]

        x_in, w_in, ident_ok = sem("x_in"), sem("w_in"), sem("ident_ok")
        st_v, mv_v, ve_v, rstd_g, h_v, pow_g = sem("st_v"), sem("mv_v"), sem("ve_v"), sem("rstd_g"), sem("h_v"), sem("pow_g")
        xbo_g = sem("xbo_g")
        pro_mm, pro_v, pro_a, qklo_v = sem("pro_mm"), sem("pro_v"), sem("pro_a"), sem("qklo_v")
        ctx_in = [sem(f"ctx_in{k}") for k in range(SLOTS)]
        ctxhi_v, split_g, qkb_v = sem("ctxhi_v"), sem("split_g"), sem("qkb_v")
        ctxT_mm, ctxThi_a, ctxTlo_v = sem("ctxT_mm"), sem("ctxThi_a"), sem("ctxTlo_v")
        scores_mm, scores_v = sem("scores_mm"), sem("scores_v")
        max_v, negmax_v = sem("max_v"), sem("negmax_v")
        exp_a = sem("exp_a")
        probsT_mm, probsThi_a, probsTlo_v = sem("probsT_mm"), sem("probsThi_a"), sem("probsTlo_v")
        pv_mm = sem("pv_mm")
        sum_v, rinv_v, att_v = sem("sum_v"), sem("rinv_v"), sem("att_v")
        epi_mm, epi_v, epi_a = sem("epi_mm"), sem("epi_v"), sem("epi_a")

        ST_W = 0
        ST_H = ST_W + 3
        ST_Q = ST_H + 4
        ST_QK = ST_Q + 4
        ST_QB = ST_QK + 4
        HALF = B * S // 2

        def arrivals(b, c):
            return 16 * (NCH // SLOTS * b + c // SLOTS + 1)

        block = st.enter_context(nc.Block())

        @block.sync
        def _(sp):
            sp.dma_start(x_sb[:], x.rearrange("b (q p) d -> p (b q) d", p=P)).then_inc(x_in, 16)
            for w, a in (("q", Wq), ("k", Wk), ("v", Wv), ("o", Wo)):
                sp.dma_start(w_nat[w][:], a.rearrange("(j p) d -> p j d", p=P)).then_inc(w_in, 16)
            for w, a in (("q", bq), ("k", bk), ("v", bv)):
                sp.dma_start(bias[w][:], a.rearrange("(j p) -> p j", p=P),
                             allow_slow_non_contiguous=True).then_inc(w_in, 16)
            sp.dma_start(bo_all[:], bo.rearrange("(a d) -> a d", a=1).broadcast_to([P, D])).then_inc(w_in, 16)

            chunks = ctx.rearrange("b s d -> (b s) d").rearrange("(g s p j) d -> p g s (j d)", s=SLOTS, p=P, j=J)

            def load(g, s):
                n = SLOTS * g + s
                at_least(sp, split_g, n - SLOTS + 1)
                sp.dma_start(ctx_in_sb[:, s, :],
                             chunks[:, bass.ds(g, 1), s, :].rearrange("p g e -> p (g e)")).then_inc(ctx_in[s], 16)

            for s in range(SLOTS):
                load(0, s)
            with sp.Fori(1, B * NCH // SLOTS) as g:
                for s in range(SLOTS):
                    load(g, s)

        @block.gpsimd
        def _(pool):
            nc.gpsimd.memset(ident[:], 0.0).then_inc(ident_ok, 1)
            nc.gpsimd.memset(power[:], -0.5).then_inc(pow_g, 1)
            pool.wait_ge(ident_ok, 1)
            nc.gpsimd.affine_select(out=ident[:], in_=ident[:], compare_op=ALU.not_equal, fill=1.0, base=0,
                                    pattern=[[-1, P]], channel_multiplier=1).then_inc(ident_ok, 1)
            pool.wait_ge(pow_g, 1)
            pool.wait_ge(ve_v, 1)
            nc.gpsimd.tensor_tensor(rstd[:], ve[:], power[:], ALU.pow).then_inc(rstd_g, 1)
            pool.wait_ge(w_in, 128)
            pool.wait_ge(h_v, TT)
            nc.gpsimd.tensor_tensor(x_sb[:], x_sb[:], bo_all[:].unsqueeze(1).broadcast_to([P, TT, D]),
                                    ALU.add).then_inc(xbo_g, 1)

            with pool.Fori(0, B) as b:
                for c in range(NCH):
                    cols = slice(c * J * D, (c + 1) * J * D)
                    pool.wait_ge(ctxhi_v, NCH * b + c + 1)
                    pool.wait_ge(ctxT_mm, DH * (NCH * b + c + 1))
                    nc.gpsimd.tensor_tensor(ctx_lo[:, cols], ctx_in_sb[:, c % SLOTS, :], ctx_hi[:, cols].bitcast(F32),
                                            ALU.subtract).then_inc(split_g, 1)

        @block.tensor
        def _(pe):
            def bank_free(k):
                if k >= 4:
                    pe.wait_ge(pro_a if k % 2 else pro_v, half_wait(k - 4))

            pe.wait_ge(w_in, 128)
            pe.wait_ge(ident_ok, 2)
            for k, w in enumerate("qvo"):
                for ci in range(DH):
                    for co in range(DH):
                        last = nc.tensor.transpose(bank[k][:, ci * D + co * P:][:, :P],
                                                   w_nat[w][:, co, ci * P:(ci + 1) * P], ident[:])
                last.then_inc(pro_mm, 1)
            pe.wait_ge(h_v, TT)
            for s in range(4):
                k = ST_H + s
                bank_free(k)
                for t in range(4):
                    last = nc.tensor.transpose(bank[k % 4][:, t * P:(t + 1) * P],
                                               h_nat[:, (s % 2) * 4 + t, (s // 2) * P:(s // 2 + 1) * P], ident[:])
                last.then_inc(pro_mm, 1)
            pe.wait_ge(pro_v, half_wait(ST_Q - 1 if (ST_Q - 1) % 2 == 0 else ST_Q - 2))
            pe.wait_ge(pro_a, half_wait(ST_Q - 1 if (ST_Q - 1) % 2 else ST_Q - 2))
            for s in range(4):
                k = ST_Q + s
                for c in range(DH):
                    last = nc.tensor.matmul(bank[k % 4][:], wT["q"][:, c, (s // 2) * P:(s // 2 + 1) * P],
                                            hT[:, c, (s % 2) * HALF:(s % 2 + 1) * HALF], start=c == 0, stop=c == 1)
                last.then_inc(pro_mm, 1)
            pe.wait_ge(pro_v, half_wait(ST_QK - 1 if (ST_QK - 1) % 2 == 0 else ST_QK - 2))
            pe.wait_ge(pro_a, half_wait(ST_QK - 1 if (ST_QK - 1) % 2 else ST_QK - 2))
            for s in range(4):
                k = ST_QK + s
                for c in range(DH):
                    last = nc.tensor.matmul(bank[k % 4][:], w_nat["k"][:, c, (s // 2) * P:(s // 2 + 1) * P],
                                            qT[:, c, (s % 2) * HALF:(s % 2 + 1) * HALF], start=c == 0, stop=c == 1)
                last.then_inc(pro_mm, 1)
            for t in range(TT):
                for c in range(DH):
                    last = nc.tensor.matmul(bank[4][:, t:t + 1], qT[:, c, t * P:(t + 1) * P], bias["k"][:, c:c + 1],
                                            start=c == 0, stop=c == 1)
            last.then_inc(pro_mm, 1)
            pe.wait_ge(qklo_v, 4)
            pe.wait_ge(pro_v, 1 + half_wait(ST_Q - 1))

            def transpose_ctx(b, c):
                n = NCH * b + c
                pe.wait_ge(ctx_in[c % SLOTS], arrivals(b, c))
                for dh in range(DH):
                    at_least(pe, ctxTlo_v, 2 * n + dh - 1)
                    for j in range(J):
                        last = nc.tensor.transpose(pT[dh][:, j * P:(j + 1) * P],
                                                   ctx_in_sb[:, c % SLOTS, j * D + dh * P:][:, :P], ident[:])
                    last.then_inc(ctxT_mm, 1)

            def score(b, c):
                n = NCH * b + c
                pe.wait_ge(ctxTlo_v, 2 * n + 2)
                for q in range(QT):
                    at_least(pe, scores_v, 2 * n + q - 1)
                    step = 0
                    for a, k in ((qk_hi_b, ctxT_hi), (qk_lo_b, ctxT_hi), (qk_hi_b, ctxT_lo)):
                        for dh in range(DH):
                            last = nc.tensor.matmul(pS[q][:], a[:, dh, q * P:(q + 1) * P], k[:, c % 2, dh, :],
                                                    start=step == 0, stop=step == 5)
                            step += 1
                    last.then_inc(scores_mm, 1)

            def transpose_probs(b, c):
                m = NCH * b + c
                for q in range(QT):
                    pe.wait_ge(exp_a, 2 * m + q + 1)
                    if c:
                        pe.wait_ge(probsTlo_v, 2 * m + q - 1)
                    for j in range(J):
                        last = nc.tensor.transpose(pE[q][:, j * P:(j + 1) * P],
                                                   probs[:, c % 2, q, j * P:(j + 1) * P], ident[:])
                    last.then_inc(probsT_mm, 1)

            def mix(b, c, scoring):
                m = NCH * b + c
                pe.wait_ge(probsTlo_v, 2 * m + 2)
                pe.wait_ge(split_g, m + 1)
                if c == 0 and not scoring:
                    pe.wait_ge(att_v, QT * b)
                for q in range(QT):
                    for j in range(J):
                        hi = ctx_hi[:, (c * J + j) * D:(c * J + j + 1) * D]
                        lo = ctx_lo[:, (c * J + j) * D:(c * J + j + 1) * D]
                        cols = slice(j * P, (j + 1) * P)
                        nc.tensor.matmul(pO[q][:, 0:D], pT_hi[:, c % 2, q, cols], hi, start=c == 0 and j == 0, stop=False)
                        nc.tensor.matmul(pO[q][:, 0:D], pT_hi[:, c % 2, q, cols], lo, start=False, stop=False)
                        last = nc.tensor.matmul(pO[q][:, 0:D], pT_lo[:, c % 2, q, cols], hi, start=False,
                                                stop=c == NCH - 1 and j == J - 1)
                last.then_inc(pv_mm, 1)

            def batch(b, scoring, mixing):
                if scoring:
                    transpose_ctx(b, 0)
                    pe.wait_ge(qkb_v, 2 * b + 2)
                if mixing:
                    transpose_probs(b - 1, 0)
                for c in range(NCH):
                    if scoring:
                        score(b, c)
                        if c < NCH - 1:
                            transpose_ctx(b, c + 1)
                    if mixing:
                        mix(b - 1, c, scoring)
                        if c < NCH - 1:
                            transpose_probs(b - 1, c + 1)

            batch(0, True, False)
            with pe.Fori(1, B) as b:
                batch(b, True, True)
            batch(B, False, True)

            pe.wait_ge(att_v, TT)
            for k in range(4):
                for t in range(4):
                    last = nc.tensor.transpose(bank[k][:, t * P:(t + 1) * P],
                                               att[:, (k % 2) * 4 + t, (k // 2) * P:(k // 2 + 1) * P], ident[:])
                last.then_inc(epi_mm, 1)
            pe.wait_ge(epi_v, 2)
            pe.wait_ge(epi_a, 2)
            for k in range(4):
                for c in range(DH):
                    last = nc.tensor.matmul(bank[k][:], wT["v"][:, c, (k // 2) * P:(k // 2 + 1) * P],
                                            attT[:, c, (k % 2) * HALF:(k % 2 + 1) * HALF], start=c == 0, stop=c == 1)
                last.then_inc(epi_mm, 1)
            pe.wait_ge(epi_v, 2 + 4)
            for k in range(TT):
                for c in range(DH):
                    last = nc.tensor.matmul(bank[k][:, 0:D], zT[:, c, k * P:(k + 1) * P], wT["o"][:, c, :],
                                            start=c == 0, stop=c == 1)
                last.then_inc(epi_mm, 1)

        @block.scalar
        def _(act):
            act.wait_ge(w_in, 128)
            nc.scalar.wait_ge(pro_mm, 2)
            nc.scalar.copy(wT["v"][:].rearrange("p a b -> p (a b)"), bank[1][:]).then_inc(pro_a, 1)
            for s in range(4):
                k = ST_H + s
                if k % 2:
                    act.wait_ge(pro_mm, k + 1)
                    nc.scalar.copy(hT[:, s // 2, (s % 2) * HALF:(s % 2 + 1) * HALF], bank[k % 4][:]).then_inc(pro_a, 1)
            for s in range(4):
                k = ST_Q + s
                if k % 2:
                    act.wait_ge(pro_mm, k + 1)
                    nc.scalar.activation(qT[:, s // 2, (s % 2) * HALF:(s % 2 + 1) * HALF], bank[k % 4][:], ACT.Identity,
                                         bias=bias["q"][:, s // 2:s // 2 + 1]).then_inc(pro_a, 1)
            for s in range(4):
                k = ST_QK + s
                act.wait_ge(pro_mm, k + 1)
                nc.scalar.copy(qk_hi[:, s // 2, (s % 2) * HALF:(s % 2 + 1) * HALF], bank[k % 4][:]).then_inc(pro_a, 1)

            def ctx_high(b, c):
                n = NCH * b + c
                at_least(act, scores_mm, 2 * n - 2)
                for dh in range(DH):
                    act.wait_ge(ctxT_mm, 2 * n + dh + 1)
                    nc.scalar.copy(ctxT_hi[:, c % 2, dh, :], pT[dh][:]).then_inc(ctxThi_a, 1)

            def exps(b, c):
                m = NCH * b + c
                act.wait_ge(negmax_v, b + 1)
                if c == 0:
                    act.wait_ge(sum_v, b + 1)
                for q in range(QT):
                    if c >= 2:
                        act.wait_ge(probsT_mm, 2 * m + q - 3)
                    nc.scalar.activation(probs[:, c % 2, q, :], scores[:, q, c * CH:(c + 1) * CH], ACT.Exp,
                                         bias=negmax[:, q:q + 1], scale=SCALE,
                                         accum_out=csum[:, q, c:c + 1]).then_inc(exp_a, 1)

            def probs_high(b, c):
                m = NCH * b + c
                for q in range(QT):
                    act.wait_ge(probsT_mm, 2 * m + q + 1)
                    nc.scalar.copy(pT_hi[:, c % 2, q, :], pE[q][:]).then_inc(probsThi_a, 1)

            def batch(b, scoring, mixing):
                if mixing:
                    exps(b - 1, 0)
                if scoring:
                    ctx_high(b, 0)
                if mixing:
                    probs_high(b - 1, 0)
                for c in range(NCH - 1):
                    if scoring:
                        ctx_high(b, c + 1)
                    if mixing:
                        exps(b - 1, c + 1)
                        probs_high(b - 1, c + 1)

            batch(0, True, False)
            with act.Fori(1, B) as b:
                batch(b, True, True)
            batch(B, False, True)

            for k in (1, 3):
                act.wait_ge(epi_mm, k + 1)
                nc.scalar.copy(attT[:, k // 2, (k % 2) * HALF:(k % 2 + 1) * HALF], bank[k][:]).then_inc(epi_a, 1)

        @block.vector
        def _(dve):
            dve.wait_ge(x_in, 16)
            for t in range(TT):
                nc.vector.bn_stats(stats[:, t, :], x_sb[:, t, :]).then_inc(st_v, 1)
            for t in range(TT):
                dve.wait_ge(st_v, t + 1)
                nc.vector.bn_aggr(mv[:, t, :], stats[:, t, :]).then_inc(mv_v, 1)
            dve.wait_ge(mv_v, TT)
            nc.vector.tensor_scalar(ve[:], mv[:, :, 1], LN_EPS, None, ALU.add).then_inc(ve_v, 1)
            dve.wait_ge(rstd_g, 1)
            for t in range(TT):
                nc.vector.tensor_scalar(h_nat[:, t, :], x_sb[:, t, :], mv[:, t, 0:1], rstd[:, t:t + 1],
                                        ALU.subtract, ALU.mult).then_inc(h_v, 1)
            for k, w in ((0, "q"), (2, "o")):
                dve.wait_ge(pro_mm, k + 1)
                nc.vector.tensor_copy(wT[w][:].rearrange("p a b -> p (a b)"), bank[k][:]).then_inc(pro_v, 1)
            for s in range(4):
                k = ST_H + s
                if k % 2 == 0:
                    dve.wait_ge(pro_mm, k + 1)
                    nc.vector.tensor_copy(hT[:, s // 2, (s % 2) * HALF:(s % 2 + 1) * HALF], bank[k % 4][:]).then_inc(pro_v, 1)
            dve.wait_ge(w_in, 128)
            for s in range(4):
                k = ST_Q + s
                if k % 2 == 0:
                    dve.wait_ge(pro_mm, k + 1)
                    nc.vector.tensor_scalar(qT[:, s // 2, (s % 2) * HALF:(s % 2 + 1) * HALF], bank[k % 4][:],
                                            bias["q"][:, s // 2:s // 2 + 1], None, ALU.add).then_inc(pro_v, 1)
            for s in range(4):
                cols = slice((s % 2) * HALF, (s % 2 + 1) * HALF)
                dve.wait_ge(pro_a, half_wait(ST_Q - 1 if (ST_Q - 1) % 2 else ST_Q - 2) + 2 + s + 1)
                nc.vector.tensor_tensor(qk_lo[:, s // 2, cols], bank[(ST_QK + s) % 4][:],
                                        qk_hi[:, s // 2, cols].bitcast(F32), ALU.subtract).then_inc(qklo_v, 1)
            dve.wait_ge(pro_mm, ST_QB + 1)
            nc.vector.tensor_copy(qbk[:], bank[4][:, 0:TT]).then_inc(pro_v, 1)
            dve.wait_ge(pro_v, 1 + half_wait(ST_Q - 1))
            dve.wait_ge(qklo_v, 4)
            nc.vector.memset(rowsum[:], 0.0).then_inc(sum_v, 1)

            def ctx_low(b, c):
                n = NCH * b + c
                for dh in range(DH):
                    dve.wait_ge(ctxThi_a, 2 * n + dh + 1)
                    nc.vector.tensor_tensor(ctxT_lo[:, c % 2, dh, :], pT[dh][:], ctxT_hi[:, c % 2, dh, :].bitcast(F32),
                                            ALU.subtract).then_inc(ctxTlo_v, 1)

            def ctx_high(b, c):
                n = NCH * b + c
                dve.wait_ge(ctx_in[c % SLOTS], arrivals(b, c))
                at_least(dve, pv_mm, n - NCH + 1)
                nc.vector.tensor_copy(ctx_hi[:, c * J * D:(c + 1) * J * D], ctx_in_sb[:, c % SLOTS, :]).then_inc(ctxhi_v, 1)

            def scores_out(b, c):
                n = NCH * b + c
                for q in range(QT):
                    dve.wait_ge(scores_mm, 2 * n + q + 1)
                    at_least(dve, exp_a, 2 * n + q + 1 - QT * NCH)
                    nc.vector.tensor_scalar(scores[:, q, c * CH:(c + 1) * CH], pS[q][:], qbk[:, bass.ds(b * QT + q, 1)], None,
                                            ALU.add, ALU.max,
                                            accum_out=cmax[:, q, c:c + 1]).then_inc(scores_v, 1)

            def probs_low(b, c):
                m = NCH * b + c
                for q in range(QT):
                    dve.wait_ge(probsThi_a, 2 * m + q + 1)
                    nc.vector.tensor_tensor(pT_lo[:, c % 2, q, :], pE[q][:], pT_hi[:, c % 2, q, :].bitcast(F32),
                                            ALU.subtract).then_inc(probsTlo_v, 1)

            def maxima(b):
                dve.wait_ge(scores_v, QT * NCH * (b + 1))
                nc.vector.reduce_max(rowmax[:], cmax[:], axis=AX.X).then_inc(max_v, 1)
                dve.wait_ge(max_v, b + 1)
                nc.vector.tensor_scalar(negmax[:], rowmax[:], -SCALE, None, ALU.mult).then_inc(negmax_v, 1)

            def normalise(b):
                dve.wait_ge(exp_a, QT * NCH * (b + 1))
                nc.vector.reduce_sum(rowsum[:], csum[:], axis=AX.X).then_inc(sum_v, 1)
                dve.wait_ge(sum_v, b + 2)
                nc.vector.reciprocal(rinv[:], rowsum[:]).then_inc(rinv_v, 1)
                dve.wait_ge(rinv_v, b + 1)
                dve.wait_ge(pv_mm, NCH * (b + 1))
                for q in range(QT):
                    nc.vector.tensor_scalar(att[:].rearrange("p t d -> p (t d)")[:, bass.ds((b * QT + q) * D, D)], pO[q][:, 0:D],
                                            rinv[:, q:q + 1], None, ALU.mult).then_inc(att_v, 1)

            def batch(b, scoring, mixing):
                if scoring:
                    at_least(dve, scores_mm, QT * NCH * b)
                    for part, of_all in ((qk_hi_b, qk_hi), (qk_lo_b, qk_lo)):
                        nc.vector.tensor_copy(part[:], of_all[:, :, bass.ds(b * S, S)].bitcast(F32)).then_inc(qkb_v, 1)
                    ctx_low(b, 0)
                if mixing:
                    probs_low(b - 1, 0)
                for c in range(NCH):
                    if scoring:
                        scores_out(b, c)
                        if c < NCH - 1:
                            ctx_low(b, c + 1)
                        else:
                            maxima(b)
                        if c:
                            ctx_high(b, c - 1)
                    if mixing and c < NCH - 1:
                        probs_low(b - 1, c + 1)
                if scoring:
                    ctx_high(b, NCH - 1)
                if mixing:
                    normalise(b - 1)

            batch(0, True, False)
            with dve.Fori(1, B) as b:
                batch(b, True, True)
            batch(B, False, True)

            for k in (0, 2):
                dve.wait_ge(epi_mm, k + 1)
                nc.vector.tensor_copy(attT[:, k // 2, (k % 2) * HALF:(k % 2 + 1) * HALF], bank[k][:]).then_inc(epi_v, 1)
            for k in range(4):
                cols = slice((k % 2) * HALF, (k % 2 + 1) * HALF)
                dve.wait_ge(epi_mm, 4 + k + 1)
                nc.vector.scalar_tensor_tensor(out=zT[:, k // 2, cols], in0=bank[k][:], scalar=bias["v"][:, k // 2:k // 2 + 1],
                                               in1=hT[:, k // 2, cols], op0=ALU.add, op1=ALU.add).then_inc(epi_v, 1)
            dve.wait_ge(xbo_g, 1)
            for k in range(TT):
                dve.wait_ge(epi_mm, 8 + k + 1)
                nc.vector.tensor_tensor(x_sb[:, k, :], bank[k][:, 0:D], x_sb[:, k, :], ALU.add).then_inc(epi_v, 1)


def layernorm_stats(dve, nc, x_sb, stats, mv, ve, stats_v, mv_v, ve_v):
    for t in range(TT):
        nc.vector.bn_stats(stats[:, t, :], x_sb[:, t, :]).then_inc(stats_v, 1)
    for t in range(TT):
        dve.wait_ge(stats_v, t + 1)
        nc.vector.bn_aggr(mv[:, t, :], stats[:, t, :]).then_inc(mv_v, 1)
    dve.wait_ge(mv_v, TT)
    nc.vector.tensor_scalar(ve[:], mv[:, :, 1], LN_EPS, None, ALU.add).then_inc(ve_v, 1)


def self_attention(nc, x_sb, ident, c_attn_w, c_attn_b, c_proj_w, c_proj_b):
    NH = 16
    HD = D // NH
    GH = 4
    NG = NH // GH
    HPH = P // HD
    FIRST_END = S // 3
    SECOND_END = 2 * S // 3
    FOCUS = 1.6
    SCALE = HD ** -0.5
    MASKED = -3.0e38
    HALF = B * S // 2
    with ExitStack() as st:
        def sb(name, shape, dt=F32):
            return st.enter_context(nc.sbuf_tensor(name, shape, dt))

        def sem(name):
            return st.enter_context(nc.semaphore(name))

        w_qkv = sb("w_qkv", [P, DH, 3 * D])
        w_proj = sb("w_proj", [P, DH, D])
        b_qk = sb("b_qk2", [P, 2 * DH])
        b_v = sb("b_v2", [P, D])
        b_proj = sb("b_proj2", [P, D])
        stats = sb("stats2", [P, TT, 6])
        mv = sb("mv2", [P, TT, 2])
        ve = sb("ve2", [P, TT])
        rstd = sb("rstd2", [P, TT])
        power = sb("power2", [P, TT])
        h_nat = sb("h2_nat", [P, TT, D])
        hT = sb("h2T", [P, DH, B * S])
        qkT = sb("qkT2", [P, 2 * DH, B * S])
        v_all = sb("v_all", [P, TT, D])
        v_pad = sb("v_pad", [P, QT, NH, P])
        q_pad = sb("q_pad", [P, 2, GH, S])
        head_rows = sb("head_rows", [P, HPH])
        ident_bf = sb("ident_bf", [P, P], BF16)
        causal = sb("causal", [P, S], BF16)
        focus = sb("focus", [P, 3, S])
        eA = sb("eA", [P, 2, GH, P])
        eB = sb("eB", [P, 2, GH, S])
        gmax = sb("gmax", [P, 2, 2 * GH])
        nmax = sb("nmax", [P, 2, 2 * GH])
        esum = sb("esum", [P, 2, 2 * GH])
        rinv = sb("rinv2", [P, 2, 2 * GH])
        pT = sb("pT2", [P, 2, 3, 512])
        oT = sb("oT2", [P, DH, B * S])

        bank = [st.enter_context(nc.psum_tensor(f"pq{i}", [P, 512], F32)) for i in range(8)]
        psA, psB, psT, psO = bank[0], bank[1:3], bank[3:6], bank[6:8]

        w_in = sem("w2_in")
        stats_v, mv_v, ve_v, rstd_g, h_v = sem("stats2_v"), sem("mv2_v"), sem("ve2_v"), sem("rstd2_g"), sem("h2_v")
        const_g, rows_g, consts_g, xb_g = sem("const2_g"), sem("rows2_g"), sem("consts2_g"), sem("xb2_g")
        pro_mm, pro_v, pro_a = sem("pro2_mm"), sem("pro2_v"), sem("pro2_a")
        vpad_g, qpad_v = sem("vpad_g"), sem("qpad_v")
        s_mm, gmax_v, nmax_v, exp_a = sem("s2_mm"), sem("gmax_v"), sem("nmax_v"), sem("exp2_a")
        focus_v, fsum_v, rinv_v, norm_g = sem("focus_v"), sem("fsum_v"), sem("rinv2_v"), sem("norm_g")
        t_mm, pT_a, pT_v, av_mm, o_a = sem("t2_mm"), sem("pT_a"), sem("pT_v"), sem("av_mm"), sem("o_a")
        out_mm, out_v = sem("out2_mm"), sem("out2_v")

        ST_H = 0
        ST_QK = 4
        ST_V = 12

        block = st.enter_context(nc.Block())

        @block.sync
        def _(sp):
            sp.dma_start(w_qkv[:], c_attn_w.rearrange("(j p) n -> p j n", p=P)).then_inc(w_in, 16)
            sp.dma_start(w_proj[:], c_proj_w.rearrange("(j p) n -> p j n", p=P)).then_inc(w_in, 16)
            sp.dma_start(b_qk[:], c_attn_b[0:2 * D].rearrange("(j p) -> p j", p=P),
                         allow_slow_non_contiguous=True).then_inc(w_in, 16)
            sp.dma_start(b_v[:], c_attn_b[2 * D:3 * D].rearrange("(a d) -> a d", a=1).broadcast_to([P, D])).then_inc(w_in, 16)
            sp.dma_start(b_proj[:], c_proj_b.rearrange("(a d) -> a d", a=1).broadcast_to([P, D])).then_inc(w_in, 16)

        @block.gpsimd
        def _(pool):
            nc.gpsimd.memset(power[:], -0.5).then_inc(const_g, 1)
            nc.gpsimd.memset(head_rows[:], 1.0).then_inc(const_g, 1)
            nc.gpsimd.memset(causal[:], 0.0).then_inc(const_g, 1)
            nc.gpsimd.memset(focus[:], 1.0).then_inc(const_g, 1)
            pool.wait_ge(const_g, 1)
            pool.wait_ge(ve_v, 1)
            nc.gpsimd.tensor_tensor(rstd[:], ve[:], power[:], ALU.pow).then_inc(rstd_g, 1)
            pool.wait_ge(const_g, 4)
            nc.gpsimd.affine_select(out=head_rows[:], in_=head_rows[:], compare_op=ALU.is_ge, fill=0.0, base=0,
                                    pattern=[[-HD, HPH]], channel_multiplier=1).then_inc(rows_g, 1)
            nc.gpsimd.affine_select(out=causal[:, P:S], in_=causal[:, P:S], compare_op=ALU.is_ge, fill=MASKED, base=0,
                                    pattern=[[-1, P]], channel_multiplier=1).then_inc(consts_g, 1)
            nc.gpsimd.tensor_copy(ident_bf[:], ident[:]).then_inc(consts_g, 1)
            nc.gpsimd.memset(focus[:, 0, 0:FIRST_END], FOCUS).then_inc(consts_g, 1)
            nc.gpsimd.memset(focus[:, 1, FIRST_END:SECOND_END], FOCUS).then_inc(consts_g, 1)
            nc.gpsimd.memset(focus[:, 2, SECOND_END:S], FOCUS).then_inc(consts_g, 1)
            pool.wait_ge(rows_g, 1)
            nc.gpsimd.affine_select(out=head_rows[:], in_=head_rows[:], compare_op=ALU.is_ge, fill=0.0, base=HD - 1,
                                    pattern=[[HD, HPH]], channel_multiplier=-1).then_inc(rows_g, 1)
            nc.gpsimd.memset(v_pad[:], 0.0).then_inc(rows_g, 1)
            pool.wait_ge(w_in, 80)
            pool.wait_ge(h_v, TT)
            nc.gpsimd.tensor_tensor(x_sb[:], x_sb[:], b_proj[:].unsqueeze(1).broadcast_to([P, TT, D]),
                                    ALU.add).then_inc(xb_g, 1)
            pool.wait_ge(rows_g, 3)
            pool.wait_ge(pro_v, 10)
            pool.wait_ge(pro_a, 6)

            def pad_values(b):
                at_least(pool, av_mm, NG * b)
                for kt in range(QT):
                    for half in range(DH):
                        first = (half * HPH) * P
                        diagonal = v_pad[:, kt, :, :].rearrange("p h c -> p (h c)")[:, first:first + HPH * P]
                        diagonal = bass.AP(diagonal.tensor, diagonal.offset, [diagonal.ap[0], [P + HD, HPH], [1, HD]])
                        nc.gpsimd.tensor_copy(diagonal, v_all[:].rearrange("p t d -> p (t d)")[
                            :, bass.ds((b * QT + kt) * D + half * P, P)].rearrange("p (h c) -> p h c", h=HPH)).then_inc(vpad_g, 1)

            def normalise(b, g):
                pool.wait_ge(rinv_v, NG * b + g + 1)
                nc.gpsimd.tensor_tensor(eA[:, g % 2, :, :], eA[:, g % 2, :, :],
                                        rinv[:, g % 2, 0:GH].unsqueeze(2).broadcast_to([P, GH, P]), ALU.mult).then_inc(norm_g, 1)
                nc.gpsimd.tensor_tensor(eB[:, g % 2, :, :], eB[:, g % 2, :, :],
                                        rinv[:, g % 2, GH:].unsqueeze(2).broadcast_to([P, GH, S]), ALU.mult).then_inc(norm_g, 1)

            pad_values(0)
            normalise(0, 0)

            def batch(b, last):
                for g in range(NG):
                    if g + 1 < NG:
                        normalise(b, g + 1)
                    elif not last:
                        normalise(b + 1, 0)
                if not last:
                    pad_values(b + 1)

            with pool.Fori(0, B - 1) as b:
                batch(b, False)
            batch(B - 1, True)

        @block.tensor
        def _(pe):
            def bank_free(k):
                if k >= 4:
                    pe.wait_ge(pro_a if k % 2 else pro_v, half_wait(k - 4))

            pe.wait_ge(h_v, TT)
            for s in range(4):
                k = ST_H + s
                for t in range(4):
                    last = nc.tensor.transpose(bank[k % 4][:, t * P:(t + 1) * P],
                                               h_nat[:, (s % 2) * 4 + t, (s // 2) * P:(s // 2 + 1) * P], ident[:])
                last.then_inc(pro_mm, 1)
            pe.wait_ge(w_in, 80)
            pe.wait_ge(pro_v, 2)
            pe.wait_ge(pro_a, 2)
            for s in range(8):
                k = ST_QK + s
                bank_free(k)
                for c in range(DH):
                    last = nc.tensor.matmul(bank[k % 4][:], w_qkv[:, c, (s // 2) * P:(s // 2 + 1) * P],
                                            hT[:, c, (s % 2) * HALF:(s % 2 + 1) * HALF], start=c == 0, stop=c == 1)
                last.then_inc(pro_mm, 1)
            for s in range(4):
                k = ST_V + s
                bank_free(k)
                for t in range(2):
                    for c in range(DH):
                        last = nc.tensor.matmul(bank[k % 4][:, t * D:(t + 1) * D],
                                                hT[:, c, (2 * s + t) * P:(2 * s + t + 1) * P], w_qkv[:, c, 2 * D:3 * D],
                                                start=c == 0, stop=c == 1)
                last.then_inc(pro_mm, 1)
            pe.wait_ge(consts_g, 5)
            pe.wait_ge(pro_v, 10)
            pe.wait_ge(pro_a, 6)

            def score(b, g):
                G = NG * b + g
                half = g * GH // HPH
                keys = qkT[:, DH + half, :]
                pe.wait_ge(qpad_v, G + 1)
                at_least(pe, exp_a, 2 * GH * G)
                nc.tensor.matmul(psA[:], ident_bf[:], causal[:, P:S].unsqueeze(1).broadcast_to([P, GH, P]), start=True, stop=False)
                for h in range(GH):
                    last = nc.tensor.matmul(psA[:, h * P:(h + 1) * P], q_pad[:, g % 2, h, 0:P],
                                            keys[:, bass.ds(b * S, P)], start=False, stop=h == GH - 1)
                last.then_inc(s_mm, 1)
                for r in range(2):
                    nc.tensor.matmul(psB[r][:], ident_bf[:], causal[:].unsqueeze(1).broadcast_to([P, 2, S]), start=True, stop=False)
                    for h in range(2):
                        last = nc.tensor.matmul(psB[r][:, h * S:(h + 1) * S], q_pad[:, g % 2, 2 * r + h, P:S],
                                                keys[:, bass.ds(b * S, S)], start=False, stop=h == 1)
                    last.then_inc(s_mm, 1)

            def transpose(b, g):
                G = NG * b + g
                pe.wait_ge(norm_g, 2 * G + 2)
                for h in range(GH):
                    to = psT[h // 2][:, (h % 2) * S:(h % 2 + 1) * S]
                    nc.tensor.transpose(to[:, 0:P], eA[:, g % 2, h, :], ident[:])
                    last = nc.tensor.transpose(to[:, P:S], eB[:, g % 2, h, 0:P], ident[:])
                    if h % 2:
                        last.then_inc(t_mm, 1)
                for h in range(GH):
                    last = nc.tensor.transpose(psT[2][:, h * P:(h + 1) * P], eB[:, g % 2, h, P:S], ident[:])
                last.then_inc(t_mm, 1)

            def mix(b, g):
                G = NG * b + g
                half = g * GH // HPH
                if g == 0:
                    pe.wait_ge(vpad_g, 4 * b + 4)
                pe.wait_ge(pT_a, G + 1)
                pe.wait_ge(pT_v, 2 * G + 2)
                for h in range(GH):
                    head = g * GH + h
                    nc.tensor.matmul(psO[half][:, 0:S], v_pad[:, 0, head, :], pT[:, g % 2, h // 2, (h % 2) * S:(h % 2 + 1) * S],
                                     start=head % HPH == 0, stop=False)
                    last = nc.tensor.matmul(psO[half][:, P:S], v_pad[:, 1, head, :], pT[:, g % 2, 2, h * P:(h + 1) * P],
                                            start=False, stop=head % HPH == HPH - 1)
                last.then_inc(av_mm, 1)

            score(0, 0)

            def batch(b, last):
                for g in range(NG):
                    if g + 1 < NG:
                        score(b, g + 1)
                    elif not last:
                        score(b + 1, 0)
                    transpose(b, g)
                    mix(b, g)

            with pe.Fori(0, B - 1) as b:
                batch(b, False)
            batch(B - 1, True)
            pe.wait_ge(o_a, DH * B)
            for t in range(TT):
                if t < 2:
                    bk = psO[t]
                else:
                    bk = bank[t - 2]
                for c in range(DH):
                    last = nc.tensor.matmul(bk[:, 0:D], oT[:, c, t * P:(t + 1) * P], w_proj[:, c, :], start=c == 0, stop=c == 1)
                last.then_inc(out_mm, 1)

        @block.scalar
        def _(act):
            for s in (1, 3):
                act.wait_ge(pro_mm, ST_H + s + 1)
                nc.scalar.copy(hT[:, s // 2, (s % 2) * HALF:(s % 2 + 1) * HALF], bank[s][:]).then_inc(pro_a, 1)
            act.wait_ge(w_in, 80)
            for s in range(1, 8, 2):
                act.wait_ge(pro_mm, ST_QK + s + 1)
                nc.scalar.activation(qkT[:, s // 2, (s % 2) * HALF:(s % 2 + 1) * HALF], bank[(ST_QK + s) % 4][:], ACT.Identity,
                                     bias=b_qk[:, s // 2:s // 2 + 1]).then_inc(pro_a, 1)

            def exps_early(b, g):
                act.wait_ge(nmax_v, 2 * (NG * b + g) + 1)
                for h in range(GH):
                    nc.scalar.activation(eA[:, g % 2, h, :], psA[:, h * P:(h + 1) * P], ACT.Exp, bias=nmax[:, g % 2, h:h + 1],
                                         scale=SCALE, accum_out=esum[:, g % 2, h:h + 1]).then_inc(exp_a, 1)

            def exps_late(b, g):
                act.wait_ge(nmax_v, 2 * (NG * b + g) + 2)
                for h in range(GH):
                    nc.scalar.activation(eB[:, g % 2, h, :], psB[h // 2][:, (h % 2) * S:(h % 2 + 1) * S], ACT.Exp,
                                         bias=nmax[:, g % 2, GH + h:GH + h + 1], scale=SCALE,
                                         accum_out=esum[:, g % 2, GH + h:GH + h + 1]).then_inc(exp_a, 1)

            def transposed(b, g):
                act.wait_ge(t_mm, 3 * (NG * b + g) + 1)
                nc.scalar.copy(pT[:, g % 2, 0, :], psT[0][:]).then_inc(pT_a, 1)

            exps_early(0, 0)
            exps_late(0, 0)

            def batch(b, last):
                for g in range(NG):
                    nb, ng = (b, g + 1) if g + 1 < NG else (b + 1, 0)
                    more = g + 1 < NG or not last
                    if more:
                        exps_early(nb, ng)
                    transposed(b, g)
                    if more:
                        exps_late(nb, ng)
                    if (g + 1) * GH % HPH == 0:
                        half = g * GH // HPH
                        act.wait_ge(av_mm, NG * b + g + 1)
                        nc.scalar.copy(oT[:, half, bass.ds(b * S, S)], psO[half][:, 0:S]).then_inc(o_a, 1)

            with act.Fori(0, B - 1) as b:
                batch(b, False)
            batch(B - 1, True)

        @block.vector
        def _(dve):
            layernorm_stats(dve, nc, x_sb, stats, mv, ve, stats_v, mv_v, ve_v)
            dve.wait_ge(rstd_g, 1)
            for t in range(TT):
                nc.vector.tensor_scalar(h_nat[:, t, :], x_sb[:, t, :], mv[:, t, 0:1], rstd[:, t:t + 1],
                                        ALU.subtract, ALU.mult).then_inc(h_v, 1)
            for s in (0, 2):
                dve.wait_ge(pro_mm, ST_H + s + 1)
                nc.vector.tensor_copy(hT[:, s // 2, (s % 2) * HALF:(s % 2 + 1) * HALF], bank[s][:]).then_inc(pro_v, 1)
            dve.wait_ge(w_in, 80)
            for s in range(0, 8, 2):
                dve.wait_ge(pro_mm, ST_QK + s + 1)
                nc.vector.tensor_scalar(qkT[:, s // 2, (s % 2) * HALF:(s % 2 + 1) * HALF], bank[(ST_QK + s) % 4][:],
                                        b_qk[:, s // 2:s // 2 + 1], None, ALU.add).then_inc(pro_v, 1)
            for s in range(4):
                dve.wait_ge(pro_mm, ST_V + s + 1)
                nc.vector.tensor_tensor(v_all[:, 2 * s:2 * s + 2, :], bank[(ST_V + s) % 4][:].rearrange("p (t d) -> p t d", t=2),
                                        b_v[:].unsqueeze(1).broadcast_to([P, 2, D]), ALU.add).then_inc(pro_v, 1)

            def maxima(b, g):
                G = NG * b + g
                dve.wait_ge(s_mm, 3 * G + 1)
                nc.vector.reduce_max(gmax[:, g % 2, 0:GH], psA[:].rearrange("p (h k) -> p h k", h=GH), axis=AX.X).then_inc(gmax_v, 1)
                dve.wait_ge(gmax_v, 3 * G + 1)
                nc.vector.tensor_scalar(nmax[:, g % 2, 0:GH], gmax[:, g % 2, 0:GH], -SCALE, None, ALU.mult).then_inc(nmax_v, 1)
                for r in range(2):
                    dve.wait_ge(s_mm, 3 * G + 2 + r)
                    nc.vector.reduce_max(gmax[:, g % 2, GH + 2 * r:GH + 2 * r + 2], psB[r][:].rearrange("p (h k) -> p h k", h=2),
                                         axis=AX.X).then_inc(gmax_v, 1)
                dve.wait_ge(gmax_v, 3 * G + 3)
                nc.vector.tensor_scalar(nmax[:, g % 2, GH:], gmax[:, g % 2, GH:], -SCALE, None, ALU.mult).then_inc(nmax_v, 1)

            def weights(b, g):
                G = NG * b + g
                dve.wait_ge(exp_a, 2 * GH * (G + 1))
                if g == 0:
                    dve.wait_ge(consts_g, 5)
                    nc.vector.tensor_tensor(eA[:, 0, 0:3, :], eA[:, 0, 0:3, :], focus[:, :, 0:P], ALU.mult).then_inc(focus_v, 1)
                    nc.vector.tensor_tensor(eB[:, 0, 0:3, :], eB[:, 0, 0:3, :], focus[:], ALU.mult).then_inc(focus_v, 1)
                    dve.wait_ge(focus_v, 2 * b + 2)
                    nc.vector.reduce_sum(esum[:, 0, 0:3], eA[:, 0, 0:3, :], axis=AX.X).then_inc(fsum_v, 1)
                    nc.vector.reduce_sum(esum[:, 0, GH:GH + 3], eB[:, 0, 0:3, :], axis=AX.X).then_inc(fsum_v, 1)
                    dve.wait_ge(fsum_v, 2 * b + 2)
                nc.vector.reciprocal(rinv[:, g % 2, :], esum[:, g % 2, :]).then_inc(rinv_v, 1)

            def transposed(b, g):
                G = NG * b + g
                for r in range(1, 3):
                    dve.wait_ge(t_mm, 3 * G + r + 1)
                    nc.vector.tensor_copy(pT[:, g % 2, r, :], psT[r][:]).then_inc(pT_v, 1)

            def pad_queries(b, g):
                at_least(dve, s_mm, 3 * (NG * b + g - 1))
                half = g * GH // HPH
                rows = head_rows[:, (g * GH) % HPH:(g * GH) % HPH + GH]
                nc.vector.tensor_tensor(q_pad[:, g % 2, :, :],
                                        qkT[:, half, bass.ds(b * S, S)].unsqueeze(1).broadcast_to([P, GH, S]),
                                        rows.unsqueeze(2).broadcast_to([P, GH, S]), ALU.mult).then_inc(qpad_v, 1)

            dve.wait_ge(rows_g, 2)
            dve.wait_ge(pro_v, 10)
            dve.wait_ge(pro_a, 6)
            pad_queries(0, 0)
            pad_queries(0, 1)
            maxima(0, 0)
            weights(0, 0)

            def batch(b, last):
                for g in range(NG):
                    nb, ng = (b, g + 1) if g + 1 < NG else (b + 1, 0)
                    more = g + 1 < NG or not last
                    if more:
                        maxima(nb, ng)
                    if g + 2 < NG:
                        pad_queries(b, g + 2)
                    elif not last:
                        pad_queries(b + 1, g + 2 - NG)
                    transposed(b, g)
                    if more:
                        weights(nb, ng)

            with dve.Fori(0, B - 1) as b:
                batch(b, False)
            batch(B - 1, True)
            dve.wait_ge(xb_g, 1)
            for t in range(TT):
                bk = psO[t] if t < 2 else bank[t - 2]
                dve.wait_ge(out_mm, t + 1)
                nc.vector.tensor_tensor(x_sb[:, t, :], bk[:, 0:D], x_sb[:, t, :], ALU.add).then_inc(out_v, 1)


def soft_moe(nc, x_sb, ident, phi_w, phi_b, expert_w, expert_b, out):
    NE, NS, HID = expert_w.shape[0], phi_w.shape[0] // expert_w.shape[0], expert_w.shape[2]
    SL = NE * NS
    ST = SL // P
    EPT = P // NS
    LB = SL // 512
    WS = 3
    LOW, HIGH = -33000.0, 65000.0
    HALF = B * S // 2
    with ExitStack() as st:
        def sb(name, shape, dt=F32):
            return st.enter_context(nc.sbuf_tensor(name, shape, dt))

        def sem(name):
            return st.enter_context(nc.semaphore(name))

        disp = sb("disp", [P, TT, SL])
        combT = sb("combT", [P, ST, B * S])
        phiT = sb("phiT", [P, DH, SL])
        stage = sb("stage", [P, 2 * SL + DH * B * S])
        h_nat = sb("h3_nat", [P, TT, D])
        hT_t = sb("h3T_tile", [P, 2, DH, P])
        ones = sb("ones3", [P, P], BF16)
        phib = sb("phib", [P, SL], BF16)
        dwork = sb("dwork", [P, SL])
        stats = sb("stats3", [P, TT, 6])
        mv = sb("mv3", [P, TT, 2])
        ve = sb("ve3", [P, TT])
        rstd = sb("rstd3", [P, TT])
        power = sb("power3", [P, TT])
        sstats = sb("sstats", [P, 2, 6])
        smv = sb("smv", [P, 2, 2])
        sve = sb("sve", [P, 2])
        srstd = sb("srstd", [P, 2])
        snmr = sb("snmr", [P, 2])
        dmax = sb("dmax", [P, NE])
        dsum = sb("dsum", [P, NE])
        dinv = sb("dinv", [P, NE])
        cmax = sb("cmax3", [P, 2, NS])
        csum = sb("csum3", [P, NS])
        cinv = sb("cinv", [P, 2, NS])

        logits = stage[:, 0:2 * SL].rearrange("p (r s) -> p r s", r=2)
        hT = stage[:, 2 * SL:].rearrange("p (a t) -> p a t", a=DH)
        xc, xh, xhT = (stage[:, 2 * SL + k * 2 * D:2 * SL + (k + 1) * 2 * D].rearrange("p (r d) -> p r d", r=2) for k in range(3))
        xhT = xhT.rearrange("p r (c s) -> p r c s", c=DH)
        dflat = disp[:].rearrange("p t s -> p (t s)")
        phi_nat = dflat[:, 0:ST * D].rearrange("p (k d) -> p k d", k=ST)
        pb = [dflat[:, ST * D + k * SL:ST * D + (k + 1) * SL] for k in range(3)]
        mixed = phiT[:].rearrange("p a s -> p (a s)").rearrange("p (k d) -> p k d", k=ST)
        w_exp = [a.rearrange("p (n c h) -> p n c h", n=EPT, c=DH)
                 for a in (stage[:, 0:SL], stage[:, SL:2 * SL], dwork[:])]

        bank = [st.enter_context(nc.psum_tensor(f"pf{i}", [P, 512], F32)) for i in range(8)]
        psL, psC = bank[0:4], bank[4:6]
        psX, psE, psT = bank[0:2], bank[2:4], bank[4:6]
        psY = bank[6:8] + bank[0:6]

        phi_in, pb_in, w_in, eb_in = sem("phi_in"), sem("pb_in"), [sem(f"w3_in{k}") for k in range(WS)], sem("eb_in")
        stats_v, mv_v, ve_v, rstd_g, h_v = sem("stats3_v"), sem("mv3_v"), sem("ve3_v"), sem("rstd3_g"), sem("h3_v")
        const_g, ones_v, phib_v, left_v = sem("const3_g"), sem("ones_v"), sem("phib_v"), sem("left_v")
        pro_mm, pro_v, pro_a = sem("pro3_mm"), sem("pro3_v"), sem("pro3_a")
        hTt_v, L_mm, L_a = sem("hTt_v"), sem("L_mm"), sem("L_a")
        cmax_v, csub_g, cexp_a, csum_v, cinv_v, cmul_g = (sem(n) for n in ("cmax3_v", "csub_g", "cexp_a", "csum3_v", "cinv_v", "cmul_g"))
        dmax_v, dsub_v, dexp_a, dsum_v, dinv_v, dmul_v = (sem(n) for n in ("dmax_v", "dsub_v", "dexp_a", "dsum_v", "dinv_v", "dmul_v"))
        cT_mm, cT_a = sem("cT_mm"), sem("cT_a")
        xs_mm, clip_v, sst_v, smv_v, sve_v, srstd_g, snmr_v, tanh_a = (sem(n) for n in (
            "xs_mm", "clip_v", "sst_v", "smv_v", "sve_v", "srstd_g", "snmr_v", "tanh_a"))
        xT_mm, xT_a, e_mm, mixed_v = sem("xT_mm"), sem("xT_a"), sem("e_mm"), sem("mixed_v")
        y_mm, y_v, out_done = sem("y_mm"), sem("y_v"), sem("out_done")

        ST_PHI = 0
        ST_H = 2 * LB

        def by_expert(a):
            return a.rearrange("p (n s) -> p n s", s=NS)

        def by_slot(a):
            return a.rearrange("p (n s) -> p s n", s=NS)

        block = st.enter_context(nc.Block())

        @block.sync
        def _(sp):
            sp.dma_start(phi_nat, phi_w.rearrange("(k p) d -> p k d", p=P)).then_inc(phi_in, 16)
            sp.dma_start(pb[0], phi_b.rearrange("(a s) -> a s", a=1).broadcast_to([P, SL])).then_inc(pb_in, 16)
            experts = expert_w.rearrange("(k n) (c p) h -> k p n c h", n=EPT, p=P)

            def load(k):
                sp.dma_start(w_exp[k % WS], experts[k]).then_inc(w_in[k % WS], 16)

            sp.wait_ge(L_mm, LB * TT)
            for j in range(EPT):
                sp.dma_start(mixed[j * NS:(j + 1) * NS, :, :],
                             expert_b.rearrange("(k n) h -> n k h", n=EPT)[j:j + 1].broadcast_to([NS, ST, HID])).then_inc(eb_in, 16)
            sp.wait_ge(dmul_v, TT)
            sp.wait_ge(cT_mm, LB * TT)
            for k in range(ST):
                if k >= WS:
                    sp.wait_ge(e_mm, k - WS + 1)
                load(k)
            rows = out.rearrange("b (q p) d -> (b q) p d", p=P)
            for t in range(TT):
                sp.wait_ge(y_v, t + 1)
                sp.dma_start(rows[t], x_sb[:, t, :]).then_inc(out_done, 16)
            sp.wait_ge(out_done, 16 * TT)

        @block.gpsimd
        def _(pool):
            nc.gpsimd.memset(power[:], -0.5).then_inc(const_g, 1)
            pool.wait_ge(const_g, 1)
            pool.wait_ge(ve_v, 1)
            nc.gpsimd.tensor_tensor(rstd[:], ve[:], power[:], ALU.pow).then_inc(rstd_g, 1)

            def combine(i, r):
                t = 2 * i + r
                c = by_slot(logits[:, r, :])
                pool.wait_ge(cmax_v, t + 1)
                pool.wait_ge(dsub_v, t + 1)
                nc.gpsimd.tensor_tensor(c, c, cmax[:, r, :].unsqueeze(2).broadcast_to([P, NS, NE]), ALU.subtract).then_inc(csub_g, 1)
                pool.wait_ge(cinv_v, t + 1)
                nc.gpsimd.tensor_tensor(c, c, cinv[:, r, :].unsqueeze(2).broadcast_to([P, NS, NE]), ALU.mult).then_inc(cmul_g, 1)

            with pool.Fori(0, TT // 2) as i:
                combine(i, 0)
                combine(i, 1)
            for s in range(ST):
                pool.wait_ge(sve_v, s + 1)
                nc.gpsimd.tensor_tensor(srstd[:, s % 2:s % 2 + 1], sve[:, s % 2:s % 2 + 1], power[:, 0:1], ALU.pow).then_inc(srstd_g, 1)

        @block.tensor
        def _(pe):
            def bank_free(k):
                if k >= 4:
                    pe.wait_ge(pro_a if k % 2 else pro_v, half_wait(k - 4))

            pe.wait_ge(phi_in, 16)
            for s in range(2 * LB):
                k = ST_PHI + s
                bank_free(k)
                for j in range(4):
                    last = nc.tensor.transpose(bank[k % 4][:, j * P:(j + 1) * P],
                                               phi_nat[:, (s % LB) * 4 + j, (s // LB) * P:(s // LB + 1) * P], ident[:])
                last.then_inc(pro_mm, 1)
            pe.wait_ge(h_v, TT)
            for s in range(4):
                k = ST_H + s
                bank_free(k)
                for t in range(4):
                    last = nc.tensor.transpose(bank[k % 4][:, t * P:(t + 1) * P],
                                               h_nat[:, (s % 2) * 4 + t, (s // 2) * P:(s // 2 + 1) * P], ident[:])
                last.then_inc(pro_mm, 1)
            pe.wait_ge(pro_v, (ST_H + 4) // 2)
            pe.wait_ge(pro_a, (ST_H + 4) // 2)
            pe.wait_ge(ones_v, 4)
            pe.wait_ge(phib_v, 3)

            def logit(i, r):
                t = 2 * i + r
                pe.wait_ge(hTt_v, t + 1)
                for j in range(LB):
                    at_least(pe, L_a, LB * (t - 1) + j + 1)
                    cols = slice(j * 512, (j + 1) * 512)
                    nc.tensor.matmul(psL[j][:], ones[0:96, :], phib[0:96, cols], start=True, stop=False)
                    for c in range(DH):
                        last = nc.tensor.matmul(psL[j][:], hT_t[:, r, c, :], phiT[:, c, cols], start=False, stop=c == 1)
                    last.then_inc(L_mm, 1)

            def transpose_combine(i, r):
                t = 2 * i + r
                pe.wait_ge(cmul_g, t + 1)
                for k in range(LB):
                    at_least(pe, cT_a, LB * t + max(k - 1, 0))
                    for j in range(4):
                        last = nc.tensor.transpose(psC[k % 2][:, j * P:(j + 1) * P],
                                                   logits[:, r, (4 * k + j) * P:(4 * k + j + 1) * P], ident[:])
                    last.then_inc(cT_mm, 1)

            logit(0, 0)

            def pair(i, last=False):
                logit(i, 1)
                transpose_combine(i, 0)
                if not last:
                    logit(i + 1, 0)
                transpose_combine(i, 1)

            pair(0)
            with pe.Fori(1, TT // 2 - 1) as i:
                pair(i)
            pair(TT // 2 - 1, True)

            def slot_inputs(s):
                if s >= 2:
                    pe.wait_ge(clip_v, s - 1)
                for t in range(TT):
                    last = nc.tensor.matmul(psX[s % 2][:, 0:D], disp[:, t, s * P:(s + 1) * P], h_nat[:, t, :],
                                            start=t == 0, stop=t == TT - 1)
                last.then_inc(xs_mm, 1)

            def transpose_inputs(s):
                pe.wait_ge(tanh_a, s + 1)
                at_least(pe, xT_a, s - 1)
                for c in range(DH):
                    last = nc.tensor.transpose(psT[s % 2][:, c * P:(c + 1) * P], xh[:, s % 2, c * P:(c + 1) * P], ident[:])
                last.then_inc(xT_mm, 1)

            def experts(s):
                pe.wait_ge(xT_a, s + 1)
                pe.wait_ge(w_in[s % WS], 16 * (s // WS + 1))
                at_least(pe, mixed_v, s - 1)
                for n in range(EPT):
                    rows = slice(n * NS, (n + 1) * NS)
                    for c in range(DH):
                        last = nc.tensor.matmul(psE[s % 2][rows, 0:HID], xhT[:, s % 2, c, rows], w_exp[s % WS][:, n, c, :],
                                                start=c == 0, stop=c == 1)
                last.then_inc(e_mm, 1)

            pe.wait_ge(dmul_v, TT)
            pe.wait_ge(cT_a, LB * TT)
            slot_inputs(0)
            for s in range(ST):
                if s + 1 < ST:
                    slot_inputs(s + 1)
                transpose_inputs(s)
                if s:
                    experts(s - 1)
            experts(ST - 1)
            pe.wait_ge(mixed_v, ST)
            for t in range(TT):
                for s in range(ST):
                    last = nc.tensor.matmul(psY[t][:, 0:HID], combT[:, s, t * P:(t + 1) * P], mixed[:, s, :],
                                            start=s == 0, stop=s == ST - 1)
                last.then_inc(y_mm, 1)

        @block.scalar
        def _(act):
            for s in range(1, 2 * LB, 2):
                act.wait_ge(pro_mm, ST_PHI + s + 1)
                nc.scalar.copy(phiT[:, s // LB, (s % LB) * 512:(s % LB + 1) * 512], bank[s % 4][:]).then_inc(pro_a, 1)
            for s in (1, 3):
                act.wait_ge(pro_mm, ST_H + s + 1)
                nc.scalar.copy(hT[:, s // 2, (s % 2) * HALF:(s % 2 + 1) * HALF], bank[(ST_H + s) % 4][:]).then_inc(pro_a, 1)

            def logits_out(i, r):
                t = 2 * i + r
                at_least(act, cT_mm, LB * (t - 1))
                for j in range(LB):
                    act.wait_ge(L_mm, LB * t + j + 1)
                    nc.scalar.copy(logits[:, r, j * 512:(j + 1) * 512], psL[j][:]).then_inc(L_a, 1)

            def exps(i, r):
                t = 2 * i + r
                act.wait_ge(dsub_v, t + 1)
                nc.scalar.activation(dwork[:], dwork[:], ACT.Exp).then_inc(dexp_a, 1)
                act.wait_ge(csub_g, t + 1)
                nc.scalar.activation(logits[:, r, :], logits[:, r, :], ACT.Exp).then_inc(cexp_a, 1)

            def combine_out(i, r):
                t = 2 * i + r
                for k in range(LB):
                    act.wait_ge(cT_mm, LB * t + k + 1)
                    nc.scalar.copy(combT[:, 4 * k:4 * k + 4, bass.ds(t * P, P)],
                                   psC[k % 2][:].rearrange("p (j q) -> p j q", j=4)).then_inc(cT_a, 1)

            logits_out(0, 0)

            def pair(i, last=False):
                logits_out(i, 1)
                exps(i, 0)
                combine_out(i, 0)
                if not last:
                    logits_out(i + 1, 0)
                exps(i, 1)
                combine_out(i, 1)

            pair(0)
            with act.Fori(1, TT // 2 - 1) as i:
                pair(i)
            pair(TT // 2 - 1, True)

            for s in range(ST):
                act.wait_ge(snmr_v, s + 1)
                at_least(act, xT_mm, s - 1)
                nc.scalar.activation(xh[:, s % 2, :], xc[:, s % 2, :], ACT.Tanh, bias=snmr[:, s % 2:s % 2 + 1],
                                     scale=srstd[:, s % 2:s % 2 + 1]).then_inc(tanh_a, 1)
                act.wait_ge(xT_mm, s + 1)
                at_least(act, e_mm, s - 1)
                nc.scalar.copy(xhT[:, s % 2, :, :].rearrange("p c s -> p (c s)"), psT[s % 2][:, 0:DH * P]).then_inc(xT_a, 1)

        @block.vector
        def _(dve):
            layernorm_stats(dve, nc, x_sb, stats, mv, ve, stats_v, mv_v, ve_v)
            dve.wait_ge(rstd_g, 1)
            for t in range(TT):
                nc.vector.tensor_scalar(h_nat[:, t, :], x_sb[:, t, :], mv[:, t, 0:1], rstd[:, t:t + 1],
                                        ALU.subtract, ALU.mult).then_inc(h_v, 1)
            nc.vector.memset(ones[:], 0.0).then_inc(ones_v, 1)
            dve.wait_ge(ones_v, 1)
            for r in range(3):
                nc.vector.memset(ones[32 * r:32 * r + 1, :], 1.0).then_inc(ones_v, 1)
            dve.wait_ge(pb_in, 16)
            for r in range(3):
                rows = slice(0, 96 - 32 * r)
                nc.vector.tensor_copy(phib[rows, :], pb[r][rows, :]).then_inc(phib_v, 1)
                if r < 2:
                    rows = slice(0, 64 - 32 * r)
                    dve.wait_ge(phib_v, r + 1)
                    nc.vector.tensor_tensor(pb[r + 1][rows, :], pb[r][rows, :], phib[rows, :], ALU.subtract).then_inc(left_v, 1)
                    dve.wait_ge(left_v, r + 1)
            for s in range(0, 2 * LB, 2):
                dve.wait_ge(pro_mm, ST_PHI + s + 1)
                nc.vector.tensor_copy(phiT[:, s // LB, (s % LB) * 512:(s % LB + 1) * 512], bank[s % 4][:]).then_inc(pro_v, 1)
            for s in (0, 2):
                dve.wait_ge(pro_mm, ST_H + s + 1)
                nc.vector.tensor_copy(hT[:, s // 2, (s % 2) * HALF:(s % 2 + 1) * HALF], bank[(ST_H + s) % 4][:]).then_inc(pro_v, 1)
            dve.wait_ge(pro_v, (ST_H + 4) // 2)
            dve.wait_ge(pro_a, (ST_H + 4) // 2)
            dve.wait_ge(phib_v, 3)

            def tile_operand(i, r):
                t = 2 * i + r
                at_least(dve, L_mm, LB * (t - 1))
                nc.vector.tensor_copy(hT_t[:, r, :, :], hT[:, :, bass.ds(t * P, P)]).then_inc(hTt_v, 1)

            def softmaxes(i, r):
                t = 2 * i + r
                work = by_expert(dwork[:])
                dve.wait_ge(L_a, LB * (t + 1))
                nc.vector.reduce_max(cmax[:, r, :], by_slot(logits[:, r, :]), axis=AX.X).then_inc(cmax_v, 1)
                nc.vector.reduce_max(dmax[:], by_expert(logits[:, r, :]), axis=AX.X).then_inc(dmax_v, 1)
                dve.wait_ge(dmax_v, t + 1)
                at_least(dve, dmul_v, t)
                nc.vector.tensor_tensor(work, by_expert(logits[:, r, :]), dmax[:].unsqueeze(2).broadcast_to([P, NE, NS]),
                                        ALU.subtract).then_inc(dsub_v, 1)
                dve.wait_ge(dexp_a, t + 1)
                nc.vector.reduce_sum(dsum[:], work, axis=AX.X).then_inc(dsum_v, 1)
                dve.wait_ge(dsum_v, t + 1)
                nc.vector.reciprocal(dinv[:], dsum[:]).then_inc(dinv_v, 1)
                dve.wait_ge(dinv_v, t + 1)
                nc.vector.tensor_tensor(by_expert(dflat[:, bass.ds(t * SL, SL)]), work,
                                        dinv[:].unsqueeze(2).broadcast_to([P, NE, NS]), ALU.mult).then_inc(dmul_v, 1)
                dve.wait_ge(cexp_a, t + 1)
                nc.vector.reduce_sum(csum[:], by_slot(logits[:, r, :]), axis=AX.X).then_inc(csum_v, 1)
                dve.wait_ge(csum_v, t + 1)
                nc.vector.reciprocal(cinv[:, r, :], csum[:]).then_inc(cinv_v, 1)

            tile_operand(0, 0)

            def pair(i, last=False):
                tile_operand(i, 1)
                softmaxes(i, 0)
                if not last:
                    tile_operand(i + 1, 0)
                softmaxes(i, 1)

            pair(0)
            with dve.Fori(1, TT // 2 - 1) as i:
                pair(i)
            pair(TT // 2 - 1, True)

            def inputs(s):
                r = s % 2
                dve.wait_ge(xs_mm, s + 1)
                at_least(dve, tanh_a, s - 1)
                nc.vector.tensor_scalar(xc[:, r, :], psX[r][:, 0:D], LOW, HIGH, ALU.max, ALU.min).then_inc(clip_v, 1)
                dve.wait_ge(clip_v, s + 1)
                nc.vector.bn_stats(sstats[:, r, :], xc[:, r, :]).then_inc(sst_v, 1)
                dve.wait_ge(sst_v, s + 1)
                nc.vector.bn_aggr(smv[:, r, :], sstats[:, r, :]).then_inc(smv_v, 1)
                dve.wait_ge(smv_v, s + 1)
                nc.vector.tensor_scalar(sve[:, r:r + 1], smv[:, r, 1:2], LN_EPS, None, ALU.add).then_inc(sve_v, 1)
                dve.wait_ge(srstd_g, s + 1)
                nc.vector.tensor_scalar(snmr[:, r:r + 1], smv[:, r, 0:1], -1.0, srstd[:, r:r + 1],
                                        ALU.mult, ALU.mult).then_inc(snmr_v, 1)

            def outputs(s):
                dve.wait_ge(e_mm, s + 1)
                nc.vector.tensor_tensor(mixed[:, s, :], psE[s % 2][:, 0:HID], mixed[:, s, :], ALU.add).then_inc(mixed_v, 1)

            dve.wait_ge(eb_in, 16 * EPT)
            for s in range(ST):
                inputs(s)
                if s >= 2:
                    outputs(s - 2)
            outputs(ST - 2)
            outputs(ST - 1)
            for t in range(TT):
                dve.wait_ge(y_mm, t + 1)
                nc.vector.tensor_tensor(x_sb[:, t, :], psY[t][:, 0:HID], x_sb[:, t, :], ALU.add).then_inc(y_v, 1)


def perceiver_block(nc, x, ctx, Wq, bq, Wk, bk, Wv, bv, Wo, bo, c_attn_w, c_attn_b, c_proj_w, c_proj_b,
                    phi_w, phi_b, expert_w, expert_b, out):
    with ExitStack() as st:
        x_sb = st.enter_context(nc.sbuf_tensor("x_sb", [P, TT, D], F32))
        ident = st.enter_context(nc.sbuf_tensor("ident", [P, P], F32))
        cross_attention(nc, x_sb, ident, x, ctx, Wq, bq, Wk, bk, Wv, bv, Wo, bo)
        self_attention(nc, x_sb, ident, c_attn_w, c_attn_b, c_proj_w, c_proj_b)
        soft_moe(nc, x_sb, ident, phi_w, phi_b, expert_w, expert_b, out)


_INS = ["x", "ctx_1024", "L0_xattn_Wq", "L0_xattn_bq", "L0_xattn_Wk", "L0_xattn_bk", "L0_xattn_Wv", "L0_xattn_bv",
        "L0_xattn_Wo", "L0_xattn_bo", "L0_attn_c_attn_w", "L0_attn_c_attn_b", "L0_attn_c_proj_w", "L0_attn_c_proj_b",
        "L0_ffn_phi_w", "L0_ffn_phi_b", "L0_ffn_expert_w", "L0_ffn_expert_b"]


def kernel(**inputs):
    import numpy as np
    import concourse.bacc as bacc
    from concourse.bass_utils import run_bass_kernel_spmd

    nc = bacc.Bacc("TRN2", target_bir_lowering=False, num_devices=1)
    arrays, args = {}, []
    for name in _INS:
        a = np.ascontiguousarray(inputs[name])
        arrays[f"in_{name}_dram"] = a
        args.append(nc.dram_tensor(f"in_{name}_dram", a.shape, mybir.dt.from_np(a.dtype), kind="ExternalInput").ap())
    out = nc.dram_tensor("out_dram", (B, S, D), F32, kind="ExternalOutput").ap()
    perceiver_block(nc, *args, out)
    r = run_bass_kernel_spmd(nc, [arrays], core_ids=[0])
    return r.results[0]["out_dram"]
```

```python
from contextlib import ExitStack

import concourse.bass as bass
from concourse import mybir

P = 128
B, S, D = 4, 256, 256
NCTX = 4096
TT = B * S // P
QT = S // P
DH = D // P
CH = 512
J = CH // P
SLOTS = 4
NCH = NCTX // CH
LN_EPS = 1e-5

F32 = mybir.dt.float32
F32R = mybir.dt.float32r
BF16 = mybir.dt.bfloat16
ALU = mybir.AluOpType
ACT = mybir.ActivationFunctionType
AX = mybir.AxisListType


def at_least(eng, sem, value):
    if not isinstance(value, int) or value > 0:
        eng.wait_ge(sem, value)


def half_wait(k):
    return k // 2 + 1


def cross_attention(nc, x_sb, ident, x, ctx, Wq, bq, Wk, bk, Wv, bv, Wo, bo):
    SCALE = 1.0 / 16.0
    with ExitStack() as st:
        def sb(name, shape, dt=F32):
            return st.enter_context(nc.sbuf_tensor(name, shape, dt))

        def sem(name):
            return st.enter_context(nc.semaphore(name))

        ctx_in_sb = sb("ctx_stage", [P, SLOTS, J * D])
        ctx_hi = sb("ctx_hi", [P, NCH * J * D], F32R)
        ctx_lo = sb("ctx_lo", [P, NCH * J * D], F32R)
        scores = sb("scores", [P, QT, NCTX])
        ctxT_hi = sb("ctxT_hi", [P, 2, DH, CH], F32R)
        ctxT_lo = sb("ctxT_lo", [P, 2, DH, CH], F32R)
        probs = sb("probs", [P, 2, QT, CH])
        pT_hi = sb("pT_hi", [P, 2, QT, CH], F32R)
        pT_lo = sb("pT_lo", [P, 2, QT, CH], F32R)
        qk_hi = sb("qk_hi", [P, DH, B * S], F32R)
        qk_lo = sb("qk_lo", [P, DH, B * S], F32R)
        h_nat = sb("h_nat", [P, TT, D])
        hT = sb("hT", [P, DH, B * S])
        qT = scores[:, 0, 0:DH * B * S].rearrange("p (a t) -> p a t", a=DH)
        w_nat = {w: scores[:, 1, k * DH * D:(k + 1) * DH * D].rearrange("p (a d) -> p a d", a=DH)
                 for k, w in enumerate("qkvo")}
        qk_hi_b = sb("qk_hi_b", [P, DH, S], F32R)
        qk_lo_b = sb("qk_lo_b", [P, DH, S], F32R)
        wT = {w: sb(f"wT_{w}", [P, DH, D]) for w in "qvo"}
        bias = {w: sb(f"b_{w}", [P, DH]) for w in "qkv"}
        bo_all = sb("bo_all", [P, D])
        stats = sb("stats", [P, TT, 6])
        mv = sb("mv", [P, TT, 2])
        ve = sb("ve", [P, TT])
        rstd = sb("rstd", [P, TT])
        power = sb("power", [P, TT])
        qbk = sb("qbk", [P, TT])
        cmax = sb("cmax", [P, QT, NCH])
        rowmax = sb("rowmax", [P, QT])
        negmax = sb("negmax", [P, QT])
        csum = sb("csum", [P, QT, NCH])
        rowsum = sb("rowsum", [P, QT])
        rinv = sb("rinv", [P, QT])
        att = h_nat
        attT = qT
        zT = hT

        bank = [st.enter_context(nc.psum_tensor(f"ps{i}", [P, 512], F32)) for i in range(8)]
        pT, pS, pE, pO = bank[0:2], bank[2:4], bank[4:6], bank[6:8]

        x_in, w_in, ident_ok = sem("x_in"), sem("w_in"), sem("ident_ok")
        st_v, mv_v, ve_v, rstd_g, h_v, pow_g = sem("st_v"), sem("mv_v"), sem("ve_v"), sem("rstd_g"), sem("h_v"), sem("pow_g")
        xbo_g = sem("xbo_g")
        pro_mm, pro_v, pro_a, qklo_v = sem("pro_mm"), sem("pro_v"), sem("pro_a"), sem("qklo_v")
        ctx_in = [sem(f"ctx_in{k}") for k in range(SLOTS)]
        ctxhi_v, split_g, qkb_v = sem("ctxhi_v"), sem("split_g"), sem("qkb_v")
        ctxT_mm, ctxThi_a, ctxTlo_v = sem("ctxT_mm"), sem("ctxThi_a"), sem("ctxTlo_v")
        scores_mm, scores_v = sem("scores_mm"), sem("scores_v")
        max_v, negmax_v = sem("max_v"), sem("negmax_v")
        exp_a = sem("exp_a")
        probsT_mm, probsThi_a, probsTlo_v = sem("probsT_mm"), sem("probsThi_a"), sem("probsTlo_v")
        pv_mm = sem("pv_mm")
        sum_v, rinv_v, att_v = sem("sum_v"), sem("rinv_v"), sem("att_v")
        epi_mm, epi_v, epi_a = sem("epi_mm"), sem("epi_v"), sem("epi_a")

        ST_W = 0
        ST_H = ST_W + 3
        ST_Q = ST_H + 4
        ST_QK = ST_Q + 4
        ST_QB = ST_QK + 4
        HALF = B * S // 2

        def arrivals(b, c):
            return 16 * (NCH // SLOTS * b + c // SLOTS + 1)

        block = st.enter_context(nc.Block())

        @block.sync
        def _(sp):
            sp.dma_start(x_sb[:], x.rearrange("b (q p) d -> p (b q) d", p=P)).then_inc(x_in, 16)
            for w, a in (("q", Wq), ("k", Wk), ("v", Wv), ("o", Wo)):
                sp.dma_start(w_nat[w][:], a.rearrange("(j p) d -> p j d", p=P)).then_inc(w_in, 16)
            for w, a in (("q", bq), ("k", bk), ("v", bv)):
                sp.dma_start(bias[w][:], a.rearrange("(j p) -> p j", p=P),
                             allow_slow_non_contiguous=True).then_inc(w_in, 16)
            sp.dma_start(bo_all[:], bo.rearrange("(a d) -> a d", a=1).broadcast_to([P, D])).then_inc(w_in, 16)

            chunks = ctx.rearrange("b s d -> (b s) d").rearrange("(g s p j) d -> p g s (j d)", s=SLOTS, p=P, j=J)

            def load(g, s):
                n = SLOTS * g + s
                at_least(sp, split_g, n - SLOTS + 1)
                sp.dma_start(ctx_in_sb[:, s, :],
                             chunks[:, bass.ds(g, 1), s, :].rearrange("p g e -> p (g e)")).then_inc(ctx_in[s], 16)

            for s in range(SLOTS):
                load(0, s)
            with sp.Fori(1, B * NCH // SLOTS) as g:
                for s in range(SLOTS):
                    load(g, s)

        @block.gpsimd
        def _(pool):
            nc.gpsimd.memset(ident[:], 0.0).then_inc(ident_ok, 1)
            nc.gpsimd.memset(power[:], -0.5).then_inc(pow_g, 1)
            pool.wait_ge(ident_ok, 1)
            nc.gpsimd.affine_select(out=ident[:], in_=ident[:], compare_op=ALU.not_equal, fill=1.0, base=0,
                                    pattern=[[-1, P]], channel_multiplier=1).then_inc(ident_ok, 1)
            pool.wait_ge(pow_g, 1)
            pool.wait_ge(ve_v, 1)
            nc.gpsimd.tensor_tensor(rstd[:], ve[:], power[:], ALU.pow).then_inc(rstd_g, 1)
            pool.wait_ge(w_in, 128)
            pool.wait_ge(h_v, TT)
            nc.gpsimd.tensor_tensor(x_sb[:], x_sb[:], bo_all[:].unsqueeze(1).broadcast_to([P, TT, D]),
                                    ALU.add).then_inc(xbo_g, 1)

            with pool.Fori(0, B) as b:
                for c in range(NCH):
                    cols = slice(c * J * D, (c + 1) * J * D)
                    pool.wait_ge(ctxhi_v, NCH * b + c + 1)
                    pool.wait_ge(ctxT_mm, DH * (NCH * b + c + 1))
                    nc.gpsimd.tensor_tensor(ctx_lo[:, cols], ctx_in_sb[:, c % SLOTS, :], ctx_hi[:, cols].bitcast(F32),
                                            ALU.subtract).then_inc(split_g, 1)

        @block.tensor
        def _(pe):
            def bank_free(k):
                if k >= 4:
                    pe.wait_ge(pro_a if k % 2 else pro_v, half_wait(k - 4))

            pe.wait_ge(w_in, 128)
            pe.wait_ge(ident_ok, 2)
            for k, w in enumerate("qvo"):
                for ci in range(DH):
                    for co in range(DH):
                        last = nc.tensor.transpose(bank[k][:, ci * D + co * P:][:, :P],
                                                   w_nat[w][:, co, ci * P:(ci + 1) * P], ident[:])
                last.then_inc(pro_mm, 1)
            pe.wait_ge(h_v, TT)
            for s in range(4):
                k = ST_H + s
                bank_free(k)
                for t in range(4):
                    last = nc.tensor.transpose(bank[k % 4][:, t * P:(t + 1) * P],
                                               h_nat[:, (s % 2) * 4 + t, (s // 2) * P:(s // 2 + 1) * P], ident[:])
                last.then_inc(pro_mm, 1)
            pe.wait_ge(pro_v, half_wait(ST_Q - 1 if (ST_Q - 1) % 2 == 0 else ST_Q - 2))
            pe.wait_ge(pro_a, half_wait(ST_Q - 1 if (ST_Q - 1) % 2 else ST_Q - 2))
            for s in range(4):
                k = ST_Q + s
                for c in range(DH):
                    last = nc.tensor.matmul(bank[k % 4][:], wT["q"][:, c, (s // 2) * P:(s // 2 + 1) * P],
                                            hT[:, c, (s % 2) * HALF:(s % 2 + 1) * HALF], start=c == 0, stop=c == 1)
                last.then_inc(pro_mm, 1)
            pe.wait_ge(pro_v, half_wait(ST_QK - 1 if (ST_QK - 1) % 2 == 0 else ST_QK - 2))
            pe.wait_ge(pro_a, half_wait(ST_QK - 1 if (ST_QK - 1) % 2 else ST_QK - 2))
            for s in range(4):
                k = ST_QK + s
                for c in range(DH):
                    last = nc.tensor.matmul(bank[k % 4][:], w_nat["k"][:, c, (s // 2) * P:(s // 2 + 1) * P],
                                            qT[:, c, (s % 2) * HALF:(s % 2 + 1) * HALF], start=c == 0, stop=c == 1)
                last.then_inc(pro_mm, 1)
            for t in range(TT):
                for c in range(DH):
                    last = nc.tensor.matmul(bank[4][:, t:t + 1], qT[:, c, t * P:(t + 1) * P], bias["k"][:, c:c + 1],
                                            start=c == 0, stop=c == 1)
            last.then_inc(pro_mm, 1)
            pe.wait_ge(qklo_v, 4)
            pe.wait_ge(pro_v, 1 + half_wait(ST_Q - 1))

            def transpose_ctx(b, c):
                n = NCH * b + c
                pe.wait_ge(ctx_in[c % SLOTS], arrivals(b, c))
                for dh in range(DH):
                    at_least(pe, ctxTlo_v, 2 * n + dh - 1)
                    for j in range(J):
                        last = nc.tensor.transpose(pT[dh][:, j * P:(j + 1) * P],
                                                   ctx_in_sb[:, c % SLOTS, j * D + dh * P:][:, :P], ident[:])
                    last.then_inc(ctxT_mm, 1)

            def score(b, c):
                n = NCH * b + c
                pe.wait_ge(ctxTlo_v, 2 * n + 2)
                for q in range(QT):
                    at_least(pe, scores_v, 2 * n + q - 1)
                    step = 0
                    for a, k in ((qk_hi_b, ctxT_hi), (qk_lo_b, ctxT_hi), (qk_hi_b, ctxT_lo)):
                        for dh in range(DH):
                            last = nc.tensor.matmul(pS[q][:], a[:, dh, q * P:(q + 1) * P], k[:, c % 2, dh, :],
                                                    start=step == 0, stop=step == 5)
                            step += 1
                    last.then_inc(scores_mm, 1)

            def transpose_probs(b, c):
                m = NCH * b + c
                for q in range(QT):
                    pe.wait_ge(exp_a, 2 * m + q + 1)
                    if c:
                        pe.wait_ge(probsTlo_v, 2 * m + q - 1)
                    for j in range(J):
                        last = nc.tensor.transpose(pE[q][:, j * P:(j + 1) * P],
                                                   probs[:, c % 2, q, j * P:(j + 1) * P], ident[:])
                    last.then_inc(probsT_mm, 1)

            def mix(b, c, scoring):
                m = NCH * b + c
                pe.wait_ge(probsTlo_v, 2 * m + 2)
                pe.wait_ge(split_g, m + 1)
                if c == 0 and not scoring:
                    pe.wait_ge(att_v, QT * b)
                for q in range(QT):
                    for j in range(J):
                        hi = ctx_hi[:, (c * J + j) * D:(c * J + j + 1) * D]
                        lo = ctx_lo[:, (c * J + j) * D:(c * J + j + 1) * D]
                        cols = slice(j * P, (j + 1) * P)
                        nc.tensor.matmul(pO[q][:, 0:D], pT_hi[:, c % 2, q, cols], hi, start=c == 0 and j == 0, stop=False)
                        nc.tensor.matmul(pO[q][:, 0:D], pT_hi[:, c % 2, q, cols], lo, start=False, stop=False)
                        last = nc.tensor.matmul(pO[q][:, 0:D], pT_lo[:, c % 2, q, cols], hi, start=False,
                                                stop=c == NCH - 1 and j == J - 1)
                last.then_inc(pv_mm, 1)

            def batch(b, scoring, mixing):
                if scoring:
                    transpose_ctx(b, 0)
                    pe.wait_ge(qkb_v, 2 * b + 2)
                if mixing:
                    transpose_probs(b - 1, 0)
                for c in range(NCH):
                    if scoring:
                        score(b, c)
                        if c < NCH - 1:
                            transpose_ctx(b, c + 1)
                    if mixing:
                        mix(b - 1, c, scoring)
                        if c < NCH - 1:
                            transpose_probs(b - 1, c + 1)

            batch(0, True, False)
            with pe.Fori(1, B) as b:
                batch(b, True, True)
            batch(B, False, True)

            pe.wait_ge(att_v, TT)
            for k in range(4):
                for t in range(4):
                    last = nc.tensor.transpose(bank[k][:, t * P:(t + 1) * P],
                                               att[:, (k % 2) * 4 + t, (k // 2) * P:(k // 2 + 1) * P], ident[:])
                last.then_inc(epi_mm, 1)
            pe.wait_ge(epi_v, 2)
            pe.wait_ge(epi_a, 2)
            for k in range(4):
                for c in range(DH):
                    last = nc.tensor.matmul(bank[k][:], wT["v"][:, c, (k // 2) * P:(k // 2 + 1) * P],
                                            attT[:, c, (k % 2) * HALF:(k % 2 + 1) * HALF], start=c == 0, stop=c == 1)
                last.then_inc(epi_mm, 1)
            pe.wait_ge(epi_v, 2 + 4)
            for k in range(TT):
                for c in range(DH):
                    last = nc.tensor.matmul(bank[k][:, 0:D], zT[:, c, k * P:(k + 1) * P], wT["o"][:, c, :],
                                            start=c == 0, stop=c == 1)
                last.then_inc(epi_mm, 1)

        @block.scalar
        def _(act):
            act.wait_ge(w_in, 128)
            nc.scalar.wait_ge(pro_mm, 2)
            nc.scalar.copy(wT["v"][:].rearrange("p a b -> p (a b)"), bank[1][:]).then_inc(pro_a, 1)
            for s in range(4):
                k = ST_H + s
                if k % 2:
                    act.wait_ge(pro_mm, k + 1)
                    nc.scalar.copy(hT[:, s // 2, (s % 2) * HALF:(s % 2 + 1) * HALF], bank[k % 4][:]).then_inc(pro_a, 1)
            for s in range(4):
                k = ST_Q + s
                if k % 2:
                    act.wait_ge(pro_mm, k + 1)
                    nc.scalar.activation(qT[:, s // 2, (s % 2) * HALF:(s % 2 + 1) * HALF], bank[k % 4][:], ACT.Identity,
                                         bias=bias["q"][:, s // 2:s // 2 + 1]).then_inc(pro_a, 1)
            for s in range(4):
                k = ST_QK + s
                act.wait_ge(pro_mm, k + 1)
                nc.scalar.copy(qk_hi[:, s // 2, (s % 2) * HALF:(s % 2 + 1) * HALF], bank[k % 4][:]).then_inc(pro_a, 1)

            def ctx_high(b, c):
                n = NCH * b + c
                at_least(act, scores_mm, 2 * n - 2)
                for dh in range(DH):
                    act.wait_ge(ctxT_mm, 2 * n + dh + 1)
                    nc.scalar.copy(ctxT_hi[:, c % 2, dh, :], pT[dh][:]).then_inc(ctxThi_a, 1)

            def exps(b, c):
                m = NCH * b + c
                act.wait_ge(negmax_v, b + 1)
                if c == 0:
                    act.wait_ge(sum_v, b + 1)
                for q in range(QT):
                    if c >= 2:
                        act.wait_ge(probsT_mm, 2 * m + q - 3)
                    nc.scalar.activation(probs[:, c % 2, q, :], scores[:, q, c * CH:(c + 1) * CH], ACT.Exp,
                                         bias=negmax[:, q:q + 1], scale=SCALE,
                                         accum_out=csum[:, q, c:c + 1]).then_inc(exp_a, 1)

            def probs_high(b, c):
                m = NCH * b + c
                for q in range(QT):
                    act.wait_ge(probsT_mm, 2 * m + q + 1)
                    nc.scalar.copy(pT_hi[:, c % 2, q, :], pE[q][:]).then_inc(probsThi_a, 1)

            def batch(b, scoring, mixing):
                if mixing:
                    exps(b - 1, 0)
                if scoring:
                    ctx_high(b, 0)
                if mixing:
                    probs_high(b - 1, 0)
                for c in range(NCH - 1):
                    if scoring:
                        ctx_high(b, c + 1)
                    if mixing:
                        exps(b - 1, c + 1)
                        probs_high(b - 1, c + 1)

            batch(0, True, False)
            with act.Fori(1, B) as b:
                batch(b, True, True)
            batch(B, False, True)

            for k in (1, 3):
                act.wait_ge(epi_mm, k + 1)
                nc.scalar.copy(attT[:, k // 2, (k % 2) * HALF:(k % 2 + 1) * HALF], bank[k][:]).then_inc(epi_a, 1)

        @block.vector
        def _(dve):
            dve.wait_ge(x_in, 16)
            for t in range(TT):
                nc.vector.bn_stats(stats[:, t, :], x_sb[:, t, :]).then_inc(st_v, 1)
            for t in range(TT):
                dve.wait_ge(st_v, t + 1)
                nc.vector.bn_aggr(mv[:, t, :], stats[:, t, :]).then_inc(mv_v, 1)
            dve.wait_ge(mv_v, TT)
            nc.vector.tensor_scalar(ve[:], mv[:, :, 1], LN_EPS, None, ALU.add).then_inc(ve_v, 1)
            dve.wait_ge(rstd_g, 1)
            for t in range(TT):
                nc.vector.tensor_scalar(h_nat[:, t, :], x_sb[:, t, :], mv[:, t, 0:1], rstd[:, t:t + 1],
                                        ALU.subtract, ALU.mult).then_inc(h_v, 1)
            for k, w in ((0, "q"), (2, "o")):
                dve.wait_ge(pro_mm, k + 1)
                nc.vector.tensor_copy(wT[w][:].rearrange("p a b -> p (a b)"), bank[k][:]).then_inc(pro_v, 1)
            for s in range(4):
                k = ST_H + s
                if k % 2 == 0:
                    dve.wait_ge(pro_mm, k + 1)
                    nc.vector.tensor_copy(hT[:, s // 2, (s % 2) * HALF:(s % 2 + 1) * HALF], bank[k % 4][:]).then_inc(pro_v, 1)
            dve.wait_ge(w_in, 128)
            for s in range(4):
                k = ST_Q + s
                if k % 2 == 0:
                    dve.wait_ge(pro_mm, k + 1)
                    nc.vector.tensor_scalar(qT[:, s // 2, (s % 2) * HALF:(s % 2 + 1) * HALF], bank[k % 4][:],
                                            bias["q"][:, s // 2:s // 2 + 1], None, ALU.add).then_inc(pro_v, 1)
            for s in range(4):
                cols = slice((s % 2) * HALF, (s % 2 + 1) * HALF)
                dve.wait_ge(pro_a, half_wait(ST_Q - 1 if (ST_Q - 1) % 2 else ST_Q - 2) + 2 + s + 1)
                nc.vector.tensor_tensor(qk_lo[:, s // 2, cols], bank[(ST_QK + s) % 4][:],
                                        qk_hi[:, s // 2, cols].bitcast(F32), ALU.subtract).then_inc(qklo_v, 1)
            dve.wait_ge(pro_mm, ST_QB + 1)
            nc.vector.tensor_copy(qbk[:], bank[4][:, 0:TT]).then_inc(pro_v, 1)
            dve.wait_ge(pro_v, 1 + half_wait(ST_Q - 1))
            dve.wait_ge(qklo_v, 4)
            nc.vector.memset(rowsum[:], 0.0).then_inc(sum_v, 1)

            def ctx_low(b, c):
                n = NCH * b + c
                for dh in range(DH):
                    dve.wait_ge(ctxThi_a, 2 * n + dh + 1)
                    nc.vector.tensor_tensor(ctxT_lo[:, c % 2, dh, :], pT[dh][:], ctxT_hi[:, c % 2, dh, :].bitcast(F32),
                                            ALU.subtract).then_inc(ctxTlo_v, 1)

            def ctx_high(b, c):
                n = NCH * b + c
                dve.wait_ge(ctx_in[c % SLOTS], arrivals(b, c))
                at_least(dve, pv_mm, n - NCH + 1)
                nc.vector.tensor_copy(ctx_hi[:, c * J * D:(c + 1) * J * D], ctx_in_sb[:, c % SLOTS, :]).then_inc(ctxhi_v, 1)

            def scores_out(b, c):
                n = NCH * b + c
                for q in range(QT):
                    dve.wait_ge(scores_mm, 2 * n + q + 1)
                    at_least(dve, exp_a, 2 * n + q + 1 - QT * NCH)
                    nc.vector.tensor_scalar(scores[:, q, c * CH:(c + 1) * CH], pS[q][:], qbk[:, bass.ds(b * QT + q, 1)], None,
                                            ALU.add, ALU.max,
                                            accum_out=cmax[:, q, c:c + 1]).then_inc(scores_v, 1)

            def probs_low(b, c):
                m = NCH * b + c
                for q in range(QT):
                    dve.wait_ge(probsThi_a, 2 * m + q + 1)
                    nc.vector.tensor_tensor(pT_lo[:, c % 2, q, :], pE[q][:], pT_hi[:, c % 2, q, :].bitcast(F32),
                                            ALU.subtract).then_inc(probsTlo_v, 1)

            def maxima(b):
                dve.wait_ge(scores_v, QT * NCH * (b + 1))
                nc.vector.reduce_max(rowmax[:], cmax[:], axis=AX.X).then_inc(max_v, 1)
                dve.wait_ge(max_v, b + 1)
                nc.vector.tensor_scalar(negmax[:], rowmax[:], -SCALE, None, ALU.mult).then_inc(negmax_v, 1)

            def normalise(b):
                dve.wait_ge(exp_a, QT * NCH * (b + 1))
                nc.vector.reduce_sum(rowsum[:], csum[:], axis=AX.X).then_inc(sum_v, 1)
                dve.wait_ge(sum_v, b + 2)
                nc.vector.reciprocal(rinv[:], rowsum[:]).then_inc(rinv_v, 1)
                dve.wait_ge(rinv_v, b + 1)
                dve.wait_ge(pv_mm, NCH * (b + 1))
                for q in range(QT):
                    nc.vector.tensor_scalar(att[:].rearrange("p t d -> p (t d)")[:, bass.ds((b * QT + q) * D, D)], pO[q][:, 0:D],
                                            rinv[:, q:q + 1], None, ALU.mult).then_inc(att_v, 1)

            def batch(b, scoring, mixing):
                if scoring:
                    at_least(dve, scores_mm, QT * NCH * b)
                    for part, of_all in ((qk_hi_b, qk_hi), (qk_lo_b, qk_lo)):
                        nc.vector.tensor_copy(part[:], of_all[:, :, bass.ds(b * S, S)].bitcast(F32)).then_inc(qkb_v, 1)
                    ctx_low(b, 0)
                if mixing:
                    probs_low(b - 1, 0)
                for c in range(NCH):
                    if scoring:
                        scores_out(b, c)
                        if c < NCH - 1:
                            ctx_low(b, c + 1)
                        else:
                            maxima(b)
                        if c:
                            ctx_high(b, c - 1)
                    if mixing and c < NCH - 1:
                        probs_low(b - 1, c + 1)
                if scoring:
                    ctx_high(b, NCH - 1)
                if mixing:
                    normalise(b - 1)

            batch(0, True, False)
            with dve.Fori(1, B) as b:
                batch(b, True, True)
            batch(B, False, True)

            for k in (0, 2):
                dve.wait_ge(epi_mm, k + 1)
                nc.vector.tensor_copy(attT[:, k // 2, (k % 2) * HALF:(k % 2 + 1) * HALF], bank[k][:]).then_inc(epi_v, 1)
            for k in range(4):
                cols = slice((k % 2) * HALF, (k % 2 + 1) * HALF)
                dve.wait_ge(epi_mm, 4 + k + 1)
                nc.vector.scalar_tensor_tensor(out=zT[:, k // 2, cols], in0=bank[k][:], scalar=bias["v"][:, k // 2:k // 2 + 1],
                                               in1=hT[:, k // 2, cols], op0=ALU.add, op1=ALU.add).then_inc(epi_v, 1)
            dve.wait_ge(xbo_g, 1)
            for k in range(TT):
                dve.wait_ge(epi_mm, 8 + k + 1)
                nc.vector.tensor_tensor(x_sb[:, k, :], bank[k][:, 0:D], x_sb[:, k, :], ALU.add).then_inc(epi_v, 1)


def layernorm_stats(dve, nc, x_sb, stats, mv, ve, stats_v, mv_v, ve_v):
    for t in range(TT):
        nc.vector.bn_stats(stats[:, t, :], x_sb[:, t, :]).then_inc(stats_v, 1)
    for t in range(TT):
        dve.wait_ge(stats_v, t + 1)
        nc.vector.bn_aggr(mv[:, t, :], stats[:, t, :]).then_inc(mv_v, 1)
    dve.wait_ge(mv_v, TT)
    nc.vector.tensor_scalar(ve[:], mv[:, :, 1], LN_EPS, None, ALU.add).then_inc(ve_v, 1)


def self_attention(nc, x_sb, ident, c_attn_w, c_attn_b, c_proj_w, c_proj_b):
    NH = 16
    HD = D // NH
    GH = 4
    NG = NH // GH
    HPH = P // HD
    FIRST_END = S // 3
    SECOND_END = 2 * S // 3
    FOCUS = 1.6
    SCALE = HD ** -0.5
    MASKED = -3.0e38
    HALF = B * S // 2
    with ExitStack() as st:
        def sb(name, shape, dt=F32):
            return st.enter_context(nc.sbuf_tensor(name, shape, dt))

        def sem(name):
            return st.enter_context(nc.semaphore(name))

        w_qkv = sb("w_qkv", [P, DH, 3 * D])
        w_proj = sb("w_proj", [P, DH, D])
        b_qk = sb("b_qk2", [P, 2 * DH])
        b_v = sb("b_v2", [P, D])
        b_proj = sb("b_proj2", [P, D])
        stats = sb("stats2", [P, TT, 6])
        mv = sb("mv2", [P, TT, 2])
        ve = sb("ve2", [P, TT])
        rstd = sb("rstd2", [P, TT])
        power = sb("power2", [P, TT])
        h_nat = sb("h2_nat", [P, TT, D])
        hT = sb("h2T", [P, DH, B * S])
        qkT = sb("qkT2", [P, 2 * DH, B * S])
        v_all = sb("v_all", [P, TT, D])
        v_pad = sb("v_pad", [P, QT, NH, P])
        q_pad = sb("q_pad", [P, 2, GH, S])
        head_rows = sb("head_rows", [P, HPH])
        ident_bf = sb("ident_bf", [P, P], BF16)
        causal = sb("causal", [P, P], BF16)
        focus = sb("focus", [P, 3, S])
        eA = sb("eA", [P, 2, GH, P])
        eB = sb("eB", [P, 2, GH, S])
        gmax = sb("gmax", [P, 2, 2 * GH])
        nmax = sb("nmax", [P, 2, 2 * GH])
        esum = sb("esum", [P, 2, 2 * GH])
        rinv = sb("rinv2", [P, 2, 2 * GH])
        pT = sb("pT2", [P, 2, 3, 512])
        oT = sb("oT2", [P, DH, B * S])

        bank = [st.enter_context(nc.psum_tensor(f"pq{i}", [P, 512], F32)) for i in range(8)]
        psS, psT, psO = bank[0:4], bank[4:7], bank[7]

        HEADS_DONE = (0, GH, GH + 2)

        def following(b, g, n):
            return (b + (g + n) // NG, (g + n) % NG) if g + n >= NG else (b, g + n)

        def columns(g, part):
            return psS[(3 * g + part) % 4]

        w_in = sem("w2_in")
        stats_v, mv_v, ve_v, rstd_g, h_v = sem("stats2_v"), sem("mv2_v"), sem("ve2_v"), sem("rstd2_g"), sem("h2_v")
        const_g, rows_g, consts_g, xb_g = sem("const2_g"), sem("rows2_g"), sem("consts2_g"), sem("xb2_g")
        pro_mm, pro_v, pro_a = sem("pro2_mm"), sem("pro2_v"), sem("pro2_a")
        vpad_g, qpad_v = sem("vpad_g"), sem("qpad_v")
        s_mm, gmax_v, nmax_v, exp_a = sem("s2_mm"), sem("gmax_v"), sem("nmax_v"), sem("exp2_a")
        focus_v, fsum_v, rinv_v, norm_g = sem("focus_v"), sem("fsum_v"), sem("rinv2_v"), sem("norm_g")
        t_mm, pT_a, pT_v, av_mm, o_a = sem("t2_mm"), sem("pT_a"), sem("pT_v"), sem("av_mm"), sem("o_a")
        out_mm, out_v = sem("out2_mm"), sem("out2_v")

        ST_H = 0
        ST_QK = 4
        ST_V = 12
        QK_TILES = (0, 2, 1, 3)

        def stage_bank(k):
            return bank[k] if k < ST_QK else bank[4 + k % 4]

        def qk_stage(s):
            return QK_TILES[s % 4], slice(s // 4 * HALF, (s // 4 + 1) * HALF)

        block = st.enter_context(nc.Block())

        @block.sync
        def _(sp):
            sp.dma_start(w_qkv[:], c_attn_w.rearrange("(j p) n -> p j n", p=P)).then_inc(w_in, 16)
            sp.dma_start(w_proj[:], c_proj_w.rearrange("(j p) n -> p j n", p=P)).then_inc(w_in, 16)
            sp.dma_start(b_qk[:], c_attn_b[0:2 * D].rearrange("(j p) -> p j", p=P),
                         allow_slow_non_contiguous=True).then_inc(w_in, 16)
            sp.dma_start(b_v[:], c_attn_b[2 * D:3 * D].rearrange("(a d) -> a d", a=1).broadcast_to([P, D])).then_inc(w_in, 16)
            sp.dma_start(b_proj[:], c_proj_b.rearrange("(a d) -> a d", a=1).broadcast_to([P, D])).then_inc(w_in, 16)

        @block.gpsimd
        def _(pool):
            nc.gpsimd.memset(power[:], -0.5).then_inc(const_g, 1)
            nc.gpsimd.memset(head_rows[:], 1.0).then_inc(const_g, 1)
            nc.gpsimd.memset(causal[:], 0.0).then_inc(const_g, 1)
            nc.gpsimd.memset(focus[:], 1.0).then_inc(const_g, 1)
            pool.wait_ge(const_g, 1)
            pool.wait_ge(ve_v, 1)
            nc.gpsimd.tensor_tensor(rstd[:], ve[:], power[:], ALU.pow).then_inc(rstd_g, 1)
            pool.wait_ge(const_g, 4)
            nc.gpsimd.affine_select(out=head_rows[:], in_=head_rows[:], compare_op=ALU.is_ge, fill=0.0, base=0,
                                    pattern=[[-HD, HPH]], channel_multiplier=1).then_inc(rows_g, 1)
            nc.gpsimd.affine_select(out=causal[:], in_=causal[:], compare_op=ALU.is_ge, fill=MASKED, base=0,
                                    pattern=[[-1, P]], channel_multiplier=1).then_inc(consts_g, 1)
            nc.gpsimd.tensor_copy(ident_bf[:], ident[:]).then_inc(consts_g, 1)
            nc.gpsimd.memset(focus[:, 0, 0:FIRST_END], FOCUS).then_inc(consts_g, 1)
            nc.gpsimd.memset(focus[:, 1, FIRST_END:SECOND_END], FOCUS).then_inc(consts_g, 1)
            nc.gpsimd.memset(focus[:, 2, SECOND_END:S], FOCUS).then_inc(consts_g, 1)
            pool.wait_ge(rows_g, 1)
            nc.gpsimd.affine_select(out=head_rows[:], in_=head_rows[:], compare_op=ALU.is_ge, fill=0.0, base=HD - 1,
                                    pattern=[[HD, HPH]], channel_multiplier=-1).then_inc(rows_g, 1)
            nc.gpsimd.memset(v_pad[:], 0.0).then_inc(rows_g, 1)
            pool.wait_ge(w_in, 80)
            pool.wait_ge(h_v, TT)
            nc.gpsimd.tensor_tensor(x_sb[:], x_sb[:], b_proj[:].unsqueeze(1).broadcast_to([P, TT, D]),
                                    ALU.add).then_inc(xb_g, 1)

            def pad_values(b):
                at_least(pool, av_mm, NG * b)
                for kt in range(QT):
                    for half in range(DH):
                        first = (half * HPH) * P
                        diagonal = v_pad[:, kt, :, :].rearrange("p h c -> p (h c)")[:, first:first + HPH * P]
                        diagonal = bass.AP(diagonal.tensor, diagonal.offset, [diagonal.ap[0], [P + HD, HPH], [1, HD]])
                        nc.gpsimd.tensor_copy(diagonal, v_all[:].rearrange("p t d -> p (t d)")[
                            :, bass.ds((b * QT + kt) * D + half * P, P)].rearrange("p (h c) -> p h c", h=HPH)).then_inc(vpad_g, 1)

            def normalise(b, g):
                pool.wait_ge(rinv_v, 2 * (NG * b + g) + 1)
                nc.gpsimd.tensor_tensor(eA[:, g % 2, :, :], eA[:, g % 2, :, :],
                                        rinv[:, g % 2, 0:GH].unsqueeze(2).broadcast_to([P, GH, P]), ALU.mult).then_inc(norm_g, 1)
                pool.wait_ge(rinv_v, 2 * (NG * b + g) + 2)
                nc.gpsimd.tensor_tensor(eB[:, g % 2, :, :], eB[:, g % 2, :, :],
                                        rinv[:, g % 2, GH:].unsqueeze(2).broadcast_to([P, GH, S]), ALU.mult).then_inc(norm_g, 1)

            normalise(0, 0)
            pool.wait_ge(rows_g, 3)
            pool.wait_ge(pro_v, 10)
            pad_values(0)

            def batch(b, last):
                for g in range(NG):
                    if g + 1 < NG:
                        normalise(b, g + 1)
                    elif not last:
                        normalise(b + 1, 0)
                if not last:
                    pad_values(b + 1)

            with pool.Fori(0, B - 1) as b:
                batch(b, False)
            batch(B - 1, True)

        @block.tensor
        def _(pe):
            def bank_free(k):
                if k >= 4:
                    pe.wait_ge(pro_a if k % 2 else pro_v, half_wait(k - 4))

            for s in range(4):
                k = ST_H + s
                pe.wait_ge(h_v, (s // 2 + 1) * 4)
                for t in range(4):
                    last = nc.tensor.transpose(stage_bank(k)[:, t * P:(t + 1) * P],
                                               h_nat[:, (s // 2) * 4 + t, (s % 2) * P:(s % 2 + 1) * P], ident[:])
                last.then_inc(pro_mm, 1)

            def project_qk(s):
                k = ST_QK + s
                rows, tokens = qk_stage(s)
                bank_free(k)
                for c in range(DH):
                    last = nc.tensor.matmul(stage_bank(k)[:], w_qkv[:, c, rows * P:(rows + 1) * P], hT[:, c, tokens],
                                            start=c == 0, stop=c == 1)
                last.then_inc(pro_mm, 1)

            def project_v(s):
                k = ST_V + s
                bank_free(k)
                for t in range(2):
                    for c in range(DH):
                        last = nc.tensor.matmul(stage_bank(k)[:, t * D:(t + 1) * D],
                                                hT[:, c, (2 * s + t) * P:(2 * s + t + 1) * P], w_qkv[:, c, 2 * D:3 * D],
                                                start=c == 0, stop=c == 1)
                last.then_inc(pro_mm, 1)

            def score(b, g, part):
                G = NG * b + g
                half = g * GH // HPH
                keys = qkT[:, DH + half, :]
                to = columns(g, part)
                if part == 0:
                    pe.wait_ge(qpad_v, G + 1)
                    at_least(pe, exp_a, 2 * GH * (G - 1))
                    for h in range(GH):
                        nc.tensor.matmul(to[:, h * P:(h + 1) * P], q_pad[:, g % 2, h, 0:P],
                                         keys[:, bass.ds(b * S, P)], start=h == 0, stop=False)
                    last = nc.tensor.matmul(to[:], ident_bf[:], causal[:].unsqueeze(1).broadcast_to([P, GH, P]), start=False, stop=True)
                else:
                    at_least(pe, exp_a, 2 * GH * (G - 1) + HEADS_DONE[part])
                    for h in range(2):
                        nc.tensor.matmul(to[:, h * S:(h + 1) * S], q_pad[:, g % 2, 2 * (part - 1) + h, P:S],
                                         keys[:, bass.ds(b * S, S)], start=h == 0, stop=False)
                    last = nc.tensor.matmul(to[:].rearrange("p (h k) -> p h k", h=2)[:, :, P:S], ident_bf[:],
                                            causal[:].unsqueeze(1).broadcast_to([P, 2, P]), start=False, stop=True)
                last.then_inc(s_mm, 1)

            def transpose(b, g):
                G = NG * b + g
                pe.wait_ge(norm_g, 2 * G + 2)
                for h in range(GH):
                    to = psT[h // 2][:, (h % 2) * S:(h % 2 + 1) * S]
                    nc.tensor.transpose(to[:, 0:P], eA[:, g % 2, h, :], ident[:])
                    last = nc.tensor.transpose(to[:, P:S], eB[:, g % 2, h, 0:P], ident[:])
                    if h % 2:
                        last.then_inc(t_mm, 1)
                for h in range(GH):
                    last = nc.tensor.transpose(psT[2][:, h * P:(h + 1) * P], eB[:, g % 2, h, P:S], ident[:])
                last.then_inc(t_mm, 1)

            def mix(b, g):
                G = NG * b + g
                half = g * GH // HPH
                if g == 0:
                    pe.wait_ge(vpad_g, 4 * b + 4)
                pe.wait_ge(pT_a, G + 1)
                pe.wait_ge(pT_v, 2 * G + 2)
                for h in range(GH):
                    head = g * GH + h
                    nc.tensor.matmul(psO[:, half * S:(half + 1) * S], v_pad[:, 0, head, :], pT[:, g % 2, h // 2, (h % 2) * S:(h % 2 + 1) * S],
                                     start=head % HPH == 0, stop=False)
                    last = nc.tensor.matmul(psO[:, half * S + P:(half + 1) * S], v_pad[:, 1, head, :], pT[:, g % 2, 2, h * P:(h + 1) * P],
                                            start=False, stop=head % HPH == HPH - 1)
                last.then_inc(av_mm, 1)

            pe.wait_ge(w_in, 80)
            pe.wait_ge(pro_v, 1)
            pe.wait_ge(pro_a, 1)
            for s in range(4):
                project_qk(s)
            pe.wait_ge(consts_g, 5)
            pe.wait_ge(pro_v, 2)
            pe.wait_ge(pro_a, 3)
            for part in range(3):
                score(0, 0, part)
            score(0, 1, 0)
            for s in range(4, 8):
                project_qk(s)
            for s in range(4):
                project_v(s)
            pe.wait_ge(pro_a, 6)
            pe.wait_ge(pro_v, 10)

            def batch(b, last):
                for g in range(NG):
                    if g + 1 < NG or not last:
                        score(*following(b, g, 1), 1)
                        score(*following(b, g, 1), 2)
                    transpose(b, g)
                    if g + 2 < NG or not last:
                        score(*following(b, g, 2), 0)
                    mix(b, g)

            with pe.Fori(0, B - 1) as b:
                batch(b, False)
            batch(B - 1, True)
            pe.wait_ge(o_a, DH * B)
            for t in range(TT):
                for c in range(DH):
                    last = nc.tensor.matmul(bank[t][:, 0:D], oT[:, c, t * P:(t + 1) * P], w_proj[:, c, :], start=c == 0, stop=c == 1)
                last.then_inc(out_mm, 1)

        @block.scalar
        def _(act):
            def project_qk(s):
                rows, tokens = qk_stage(s)
                act.wait_ge(pro_mm, ST_QK + s + 1)
                nc.scalar.activation(qkT[:, rows, tokens], stage_bank(ST_QK + s)[:], ACT.Identity,
                                     bias=b_qk[:, rows:rows + 1]).then_inc(pro_a, 1)

            for s in (1, 3):
                act.wait_ge(pro_mm, ST_H + s + 1)
                nc.scalar.copy(hT[:, s % 2, (s // 2) * HALF:(s // 2 + 1) * HALF], stage_bank(s)[:]).then_inc(pro_a, 1)
            act.wait_ge(w_in, 80)
            project_qk(1)
            project_qk(3)

            def exps(b, g, part):
                act.wait_ge(nmax_v, 3 * (NG * b + g) + part + 1)
                if part == 0:
                    for h in range(GH):
                        nc.scalar.activation(eA[:, g % 2, h, :], columns(g, part)[:, h * P:(h + 1) * P], ACT.Exp,
                                             bias=nmax[:, g % 2, h:h + 1], scale=SCALE,
                                             accum_out=esum[:, g % 2, h:h + 1]).then_inc(exp_a, 1)
                else:
                    for i in range(2):
                        h = 2 * (part - 1) + i
                        nc.scalar.activation(eB[:, g % 2, h, :], columns(g, part)[:, i * S:(i + 1) * S], ACT.Exp,
                                             bias=nmax[:, g % 2, GH + h:GH + h + 1], scale=SCALE,
                                             accum_out=esum[:, g % 2, GH + h:GH + h + 1]).then_inc(exp_a, 1)

            def transposed(b, g):
                act.wait_ge(t_mm, 3 * (NG * b + g) + 1)
                nc.scalar.copy(pT[:, g % 2, 0, :], psT[0][:]).then_inc(pT_a, 1)

            for part in range(3):
                exps(0, 0, part)
            project_qk(5)
            exps(0, 1, 0)
            project_qk(7)

            def batch(b, last):
                for g in range(NG):
                    if g + 1 < NG or not last:
                        exps(*following(b, g, 1), 1)
                        exps(*following(b, g, 1), 2)
                    transposed(b, g)
                    if g + 2 < NG or not last:
                        exps(*following(b, g, 2), 0)
                    if (g + 1) * GH % HPH == 0:
                        half = g * GH // HPH
                        act.wait_ge(av_mm, NG * b + g + 1)
                        nc.scalar.copy(oT[:, half, bass.ds(b * S, S)], psO[:, half * S:(half + 1) * S]).then_inc(o_a, 1)

            with act.Fori(0, B - 1) as b:
                batch(b, False)
            batch(B - 1, True)

        @block.vector
        def _(dve):
            layernorm_stats(dve, nc, x_sb, stats, mv, ve, stats_v, mv_v, ve_v)
            dve.wait_ge(rstd_g, 1)
            for t in range(TT):
                nc.vector.tensor_scalar(h_nat[:, t, :], x_sb[:, t, :], mv[:, t, 0:1], rstd[:, t:t + 1],
                                        ALU.subtract, ALU.mult).then_inc(h_v, 1)
            def project_qk(s):
                rows, tokens = qk_stage(s)
                dve.wait_ge(pro_mm, ST_QK + s + 1)
                nc.vector.tensor_scalar(qkT[:, rows, tokens], stage_bank(ST_QK + s)[:], b_qk[:, rows:rows + 1], None,
                                        ALU.add).then_inc(pro_v, 1)

            for s in (0, 2):
                dve.wait_ge(pro_mm, ST_H + s + 1)
                nc.vector.tensor_copy(hT[:, s % 2, (s // 2) * HALF:(s // 2 + 1) * HALF], stage_bank(s)[:]).then_inc(pro_v, 1)
            dve.wait_ge(w_in, 80)

            def maxima(b, g, part):
                unit = 3 * (NG * b + g) + part
                heads = GH if part == 0 else 2
                first = (0, GH, GH + 2)[part]
                dve.wait_ge(s_mm, unit + 1)
                nc.vector.reduce_max(gmax[:, g % 2, first:first + heads], columns(g, part)[:].rearrange("p (h k) -> p h k", h=heads),
                                     axis=AX.X).then_inc(gmax_v, 1)
                dve.wait_ge(gmax_v, unit + 1)
                nc.vector.tensor_scalar(nmax[:, g % 2, first:first + heads], gmax[:, g % 2, first:first + heads], -SCALE, None,
                                        ALU.mult).then_inc(nmax_v, 1)

            def invert_sums(b, g, late):
                G = NG * b + g
                e = (eA, eB)[late]
                first = late * GH
                dve.wait_ge(exp_a, 2 * GH * G + (late + 1) * GH)
                if g == 0:
                    dve.wait_ge(consts_g, 5)
                    nc.vector.tensor_tensor(e[:, 0, 0:3, :], e[:, 0, 0:3, :], focus[:, :, 0:(late + 1) * P], ALU.mult).then_inc(focus_v, 1)
                    dve.wait_ge(focus_v, 2 * b + late + 1)
                    nc.vector.reduce_sum(esum[:, 0, first:first + 3], e[:, 0, 0:3, :], axis=AX.X).then_inc(fsum_v, 1)
                    dve.wait_ge(fsum_v, 2 * b + late + 1)
                nc.vector.reciprocal(rinv[:, g % 2, first:first + GH], esum[:, g % 2, first:first + GH]).then_inc(rinv_v, 1)

            def transposed(b, g):
                G = NG * b + g
                for r in range(1, 3):
                    dve.wait_ge(t_mm, 3 * G + r + 1)
                    nc.vector.tensor_copy(pT[:, g % 2, r, :], psT[r][:]).then_inc(pT_v, 1)

            def pad_queries(b, g):
                at_least(dve, s_mm, 3 * (NG * b + g - 1))
                half = g * GH // HPH
                rows = head_rows[:, (g * GH) % HPH:(g * GH) % HPH + GH]
                nc.vector.tensor_tensor(q_pad[:, g % 2, :, :],
                                        qkT[:, half, bass.ds(b * S, S)].unsqueeze(1).broadcast_to([P, GH, S]),
                                        rows.unsqueeze(2).broadcast_to([P, GH, S]), ALU.mult).then_inc(qpad_v, 1)

            project_qk(0)
            dve.wait_ge(rows_g, 2)
            dve.wait_ge(pro_v, 3)
            pad_queries(0, 0)
            project_qk(2)
            pad_queries(0, 1)
            for part in range(3):
                maxima(0, 0, part)
            invert_sums(0, 0, 0)
            maxima(0, 1, 0)
            project_qk(4)
            invert_sums(0, 0, 1)
            project_qk(6)
            dve.wait_ge(pro_v, 4)
            pad_queries(0, 2)
            for s in range(4):
                dve.wait_ge(pro_mm, ST_V + s + 1)
                nc.vector.tensor_tensor(v_all[:, 2 * s:2 * s + 2, :], stage_bank(ST_V + s)[:].rearrange("p (t d) -> p t d", t=2),
                                        b_v[:].unsqueeze(1).broadcast_to([P, 2, D]), ALU.add).then_inc(pro_v, 1)
            dve.wait_ge(pro_v, 6)

            def batch(b, last):
                for g in range(NG):
                    more = g + 1 < NG or not last
                    if more:
                        maxima(*following(b, g, 1), 1)
                        invert_sums(*following(b, g, 1), 0)
                        maxima(*following(b, g, 1), 2)
                    transposed(b, g)
                    if more:
                        invert_sums(*following(b, g, 1), 1)
                    if g + 2 < NG or not last:
                        maxima(*following(b, g, 2), 0)
                    if g + 3 < NG or not last:
                        pad_queries(*following(b, g, 3))

            with dve.Fori(0, B - 1) as b:
                batch(b, False)
            batch(B - 1, True)
            dve.wait_ge(xb_g, 1)
            for t in range(TT):
                dve.wait_ge(out_mm, t + 1)
                nc.vector.tensor_tensor(x_sb[:, t, :], bank[t][:, 0:D], x_sb[:, t, :], ALU.add).then_inc(out_v, 1)


def soft_moe(nc, x_sb, ident, phi_w, phi_b, expert_w, expert_b, out):
    NE, NS, HID = expert_w.shape[0], phi_w.shape[0] // expert_w.shape[0], expert_w.shape[2]
    SL = NE * NS
    ST = SL // P
    EPT = P // NS
    LB = SL // 512
    LR = 3
    WS = 4
    EARLY = 4
    LOW, HIGH = -33000.0, 65000.0
    HALF = B * S // 2
    with ExitStack() as st:
        def sb(name, shape, dt=F32):
            return st.enter_context(nc.sbuf_tensor(name, shape, dt))

        def sem(name):
            return st.enter_context(nc.semaphore(name))

        disp = sb("disp", [P, TT, SL])
        combT = sb("combT", [P, ST, B * S])
        phiT = sb("phiT", [P, DH, SL])
        logits = sb("logits", [P, LR, SL])
        h_nat = sb("h3_nat", [P, TT, D])
        xc = sb("xc", [P, 2, D])
        xh = sb("xh", [P, 2, D])
        xhT = sb("xhT", [P, 2, DH, P])
        ones = sb("ones3", [P, P], BF16)
        phib = sb("phib", [P, SL], BF16)
        dwork = sb("dwork", [P, SL])
        stats = sb("stats3", [P, TT, 6])
        mv = sb("mv3", [P, TT, 2])
        ve = sb("ve3", [P, TT])
        rstd = sb("rstd3", [P, TT])
        power = sb("power3", [P, TT])
        sstats = sb("sstats", [P, 2, 6])
        smv = sb("smv", [P, 2, 2])
        sve = sb("sve", [P, 2])
        srstd = sb("srstd", [P, 2])
        snmr = sb("snmr", [P, 2])
        dmax = sb("dmax", [P, NE])
        dsum = sb("dsum", [P, NE])
        dinv = sb("dinv", [P, NE])
        cmax = sb("cmax3", [P, NS])
        csum = sb("csum3", [P, NS])
        cinv = sb("cinv", [P, NS])

        dflat = disp[:].rearrange("p t s -> p (t s)")
        hT = disp[:, TT - 1, :].rearrange("p (a t) -> p a t", a=DH)
        phi_nat = dflat[:, 0:ST * D].rearrange("p (k d) -> p k d", k=ST)
        pb = [dflat[:, ST * D + k * SL:ST * D + (k + 1) * SL] for k in range(3)]
        mixed = phiT[:].rearrange("p a s -> p (a s)").rearrange("p (k d) -> p k d", k=ST)
        w_exp = [a.rearrange("p (n c h) -> p n c h", n=EPT, c=DH)
                 for a in (logits[:, 2, :], dwork[:], logits[:, 0, :], logits[:, 1, :])]

        bank = [st.enter_context(nc.psum_tensor(f"pf{i}", [P, 512], F32)) for i in range(8)]
        psL, psC = bank[0:4], bank[4:6]
        psE, psT = bank[2:4], bank[4:6]

        def psX(s):
            return bank[6 + s // 2][:, (s % 2) * D:(s % 2 + 1) * D] if s < EARLY else bank[s % 2][:, 0:D]

        psY = bank[6:8] + bank[0:6]

        phi_in, pb_in, w_in, eb_in = sem("phi_in"), sem("pb_in"), [sem(f"w3_in{k}") for k in range(WS)], sem("eb_in")
        stats_v, mv_v, ve_v, rstd_g, h_v = sem("stats3_v"), sem("mv3_v"), sem("ve3_v"), sem("rstd3_g"), sem("h3_v")
        const_g, ones_v, phib_v, left_v = sem("const3_g"), sem("ones_v"), sem("phib_v"), sem("left_v")
        pro_mm, pro_v, pro_a = sem("pro3_mm"), sem("pro3_v"), sem("pro3_a")
        L_mm, L_a = sem("L_mm"), sem("L_a")
        cmax_v, csub_g, cexp_a, csum_v, cinv_v, cmul_g = (sem(n) for n in ("cmax3_v", "csub_g", "cexp_a", "csum3_v", "cinv_v", "cmul_g"))
        dmax_v, dsub_v, dexp_a, dsum_v, dinv_v, dmul_v = (sem(n) for n in ("dmax_v", "dsub_v", "dexp_a", "dsum_v", "dinv_v", "dmul_v"))
        cT_mm, cT_a = sem("cT_mm"), sem("cT_a")
        xs_mm, clip_v, sst_v, smv_v, sve_v, srstd_g, snmr_v, tanh_a = (sem(n) for n in (
            "xs_mm", "clip_v", "sst_v", "smv_v", "sve_v", "srstd_g", "snmr_v", "tanh_a"))
        xT_mm, xT_a, e_mm, mixed_v = sem("xT_mm"), sem("xT_a"), sem("e_mm"), sem("mixed_v")
        y_mm, y_v, out_done = sem("y_mm"), sem("y_v"), sem("out_done")

        ST_PHI = 0
        ST_H = 2 * LB

        def by_expert(a):
            return a.rearrange("p (n s) -> p n s", s=NS)

        def by_slot(a):
            return a.rearrange("p (n s) -> p s n", s=NS)

        block = st.enter_context(nc.Block())

        @block.sync
        def _(sp):
            sp.dma_start(phi_nat, phi_w.rearrange("(k p) d -> p k d", p=P)).then_inc(phi_in, 16)
            sp.dma_start(pb[0], phi_b.rearrange("(a s) -> a s", a=1).broadcast_to([P, SL])).then_inc(pb_in, 16)
            experts = expert_w.rearrange("(k n) (c p) h -> k p n c h", n=EPT, p=P)

            def load(k):
                sp.dma_start(w_exp[k % WS], experts[k]).then_inc(w_in[k % WS], 16)

            sp.wait_ge(L_mm, LB * TT)
            for j in range(EPT):
                sp.dma_start(mixed[j * NS:(j + 1) * NS, :, :],
                             expert_b.rearrange("(k n) h -> n k h", n=EPT)[j:j + 1].broadcast_to([NS, ST, HID])).then_inc(eb_in, 16)
            freed = [(cT_mm, LB * (TT - 2)), (dmul_v, TT), (cT_mm, LB * (TT - 1)), (cT_mm, LB * TT)]
            for k in range(ST):
                if k < WS:
                    sp.wait_ge(*freed[k])
                else:
                    sp.wait_ge(e_mm, k - WS + 1)
                load(k)
            rows = out.rearrange("b (q p) d -> (b q) p d", p=P)
            for t in range(TT):
                sp.wait_ge(y_v, t + 1)
                sp.dma_start(rows[t], x_sb[:, t, :]).then_inc(out_done, 16)
            sp.wait_ge(out_done, 16 * TT)

        @block.gpsimd
        def _(pool):
            nc.gpsimd.memset(power[:], -0.5).then_inc(const_g, 1)
            pool.wait_ge(const_g, 1)
            pool.wait_ge(ve_v, 1)
            nc.gpsimd.tensor_tensor(rstd[:], ve[:], power[:], ALU.pow).then_inc(rstd_g, 1)

            def subtract(t):
                c = by_slot(logits[:, t % LR, :])
                pool.wait_ge(cmax_v, t + 1)
                pool.wait_ge(dsub_v, t + 1)
                nc.gpsimd.tensor_tensor(c, c, cmax[:].unsqueeze(2).broadcast_to([P, NS, NE]), ALU.subtract).then_inc(csub_g, 1)

            def divide(t):
                c = by_slot(logits[:, t % LR, :])
                pool.wait_ge(cinv_v, t + 1)
                nc.gpsimd.tensor_tensor(c, c, cinv[:].unsqueeze(2).broadcast_to([P, NS, NE]), ALU.mult).then_inc(cmul_g, 1)

            subtract(0)
            for t in range(1, TT):
                subtract(t)
                divide(t - 1)
            divide(TT - 1)
            for s in range(ST):
                pool.wait_ge(sve_v, s + 1)
                nc.gpsimd.tensor_tensor(srstd[:, s % 2:s % 2 + 1], sve[:, s % 2:s % 2 + 1], power[:, 0:1], ALU.pow).then_inc(srstd_g, 1)

        @block.tensor
        def _(pe):
            def bank_free(k):
                if k >= 4:
                    pe.wait_ge(pro_a if k % 2 else pro_v, half_wait(k - 4))

            pe.wait_ge(phi_in, 16)
            for s in range(2 * LB):
                k = ST_PHI + s
                bank_free(k)
                for j in range(4):
                    last = nc.tensor.transpose(bank[k % 4][:, j * P:(j + 1) * P],
                                               phi_nat[:, (s % LB) * 4 + j, (s // LB) * P:(s // LB + 1) * P], ident[:])
                last.then_inc(pro_mm, 1)
            pe.wait_ge(h_v, TT)
            for s in range(4):
                k = ST_H + s
                bank_free(k)
                for t in range(4):
                    last = nc.tensor.transpose(bank[k % 4][:, t * P:(t + 1) * P],
                                               h_nat[:, (s % 2) * 4 + t, (s // 2) * P:(s // 2 + 1) * P], ident[:])
                last.then_inc(pro_mm, 1)
            pe.wait_ge(pro_v, (ST_H + 4) // 2)
            pe.wait_ge(pro_a, (ST_H + 4) // 2)
            pe.wait_ge(ones_v, 4)
            pe.wait_ge(phib_v, 3)

            def logit(t, first, end):
                for j in range(first, end):
                    if t:
                        pe.wait_ge(L_a, LB * (t - 1) + j + 1)
                    cols = slice(j * 512, (j + 1) * 512)
                    nc.tensor.matmul(psL[j][:], ones[0:96, :], phib[0:96, cols], start=True, stop=False)
                    for c in range(DH):
                        last = nc.tensor.matmul(psL[j][:], hT[:, c, t * P:(t + 1) * P], phiT[:, c, cols],
                                                start=False, stop=c == DH - 1)
                    last.then_inc(L_mm, 1)

            def transpose_combine(t):
                pe.wait_ge(cmul_g, t + 1)
                for k in range(LB):
                    at_least(pe, cT_a, LB * t + k - 1)
                    for j in range(4):
                        last = nc.tensor.transpose(psC[k % 2][:, j * P:(j + 1) * P],
                                                   logits[:, t % LR, (4 * k + j) * P:(4 * k + j + 1) * P], ident[:])
                    last.then_inc(cT_mm, 1)

            def early_inputs(t):
                pe.wait_ge(dmul_v, t + 1)
                for s in range(EARLY):
                    last = nc.tensor.matmul(psX(s), disp[:, t, s * P:(s + 1) * P], h_nat[:, t, :],
                                            start=t == 0 and s % 2 == 0, stop=t == TT - 1, skip_group_check=True)
                if t == TT - 1:
                    last.then_inc(xs_mm, EARLY)

            logit(0, 0, LB)
            for t in range(TT):
                if t:
                    early_inputs(t - 1)
                if t + 1 < TT:
                    logit(t + 1, 0, LB // 2)
                if t >= 2:
                    transpose_combine(t - 2)
                if t + 1 < TT:
                    logit(t + 1, LB // 2, LB)

            def slot_inputs(s):
                if s >= EARLY + 2:
                    pe.wait_ge(clip_v, s - 1)
                for t in range(TT):
                    last = nc.tensor.matmul(psX(s), disp[:, t, s * P:(s + 1) * P], h_nat[:, t, :],
                                            start=t == 0, stop=t == TT - 1)
                last.then_inc(xs_mm, 1)

            def transpose_inputs(s):
                pe.wait_ge(tanh_a, s + 1)
                at_least(pe, xT_a, s - 1)
                for c in range(DH):
                    last = nc.tensor.transpose(psT[s % 2][:, c * P:(c + 1) * P], xh[:, s % 2, c * P:(c + 1) * P], ident[:])
                last.then_inc(xT_mm, 1)

            def experts(s):
                pe.wait_ge(xT_a, s + 1)
                pe.wait_ge(w_in[s % WS], 16 * (s // WS + 1))
                at_least(pe, mixed_v, s - 1)
                for n in range(EPT):
                    rows = slice(n * NS, (n + 1) * NS)
                    for c in range(DH):
                        last = nc.tensor.matmul(psE[s % 2][rows, 0:HID], xhT[:, s % 2, c, rows], w_exp[s % WS][:, n, c, :],
                                                start=c == 0, stop=c == 1)
                last.then_inc(e_mm, 1)

            early_inputs(TT - 1)
            pe.wait_ge(L_a, LB * TT)
            slot_inputs(EARLY)
            transpose_combine(TT - 2)
            slot_inputs(EARLY + 1)
            transpose_combine(TT - 1)
            pe.wait_ge(cT_a, LB * TT)
            for s in range(ST):
                if EARLY + 2 <= s + 1 < ST:
                    slot_inputs(s + 1)
                transpose_inputs(s)
                if s:
                    experts(s - 1)
            experts(ST - 1)
            pe.wait_ge(mixed_v, ST)
            for t in range(TT):
                for s in range(ST):
                    last = nc.tensor.matmul(psY[t][:, 0:HID], combT[:, s, t * P:(t + 1) * P], mixed[:, s, :],
                                            start=s == 0, stop=s == ST - 1)
                last.then_inc(y_mm, 1)

        @block.scalar
        def _(act):
            for s in range(1, 2 * LB, 2):
                act.wait_ge(pro_mm, ST_PHI + s + 1)
                nc.scalar.copy(phiT[:, s // LB, (s % LB) * 512:(s % LB + 1) * 512], bank[s % 4][:]).then_inc(pro_a, 1)
            for s in (1, 3):
                act.wait_ge(pro_mm, ST_H + s + 1)
                nc.scalar.copy(hT[:, s // 2, (s % 2) * HALF:(s % 2 + 1) * HALF], bank[(ST_H + s) % 4][:]).then_inc(pro_a, 1)

            def logits_out(t):
                if t >= LR:
                    act.wait_ge(cT_mm, LB * (t - LR + 1))
                for j in range(LB):
                    act.wait_ge(L_mm, LB * t + j + 1)
                    nc.scalar.copy(logits[:, t % LR, j * 512:(j + 1) * 512], psL[j][:]).then_inc(L_a, 1)

            def combine_out(t, first, end):
                for k in range(first, end):
                    act.wait_ge(cT_mm, LB * t + k + 1)
                    nc.scalar.copy(combT[:, 4 * k:4 * k + 4, t * P:(t + 1) * P],
                                   psC[k % 2][:].rearrange("p (j q) -> p j q", j=4)).then_inc(cT_a, 1)

            logits_out(0)
            for t in range(TT):
                if t >= 2:
                    combine_out(t - 2, 0, 2)
                act.wait_ge(dsub_v, t + 1)
                nc.scalar.activation(dwork[:], dwork[:], ACT.Exp).then_inc(dexp_a, 1)
                if t >= 2:
                    combine_out(t - 2, 2, LB)
                if t + 1 < TT:
                    logits_out(t + 1)
                act.wait_ge(csub_g, t + 1)
                nc.scalar.activation(logits[:, t % LR, :], logits[:, t % LR, :], ACT.Exp).then_inc(cexp_a, 1)
            for t in range(TT - 2, TT):
                combine_out(t, 0, LB)

            for s in range(ST):
                act.wait_ge(snmr_v, s + 1)
                at_least(act, xT_mm, s - 1)
                nc.scalar.activation(xh[:, s % 2, :], xc[:, s % 2, :], ACT.Tanh, bias=snmr[:, s % 2:s % 2 + 1],
                                     scale=srstd[:, s % 2:s % 2 + 1]).then_inc(tanh_a, 1)
                act.wait_ge(xT_mm, s + 1)
                at_least(act, e_mm, s - 1)
                nc.scalar.copy(xhT[:, s % 2, :, :].rearrange("p c s -> p (c s)"), psT[s % 2][:, 0:DH * P]).then_inc(xT_a, 1)

        @block.vector
        def _(dve):
            layernorm_stats(dve, nc, x_sb, stats, mv, ve, stats_v, mv_v, ve_v)
            dve.wait_ge(rstd_g, 1)
            for t in range(TT):
                nc.vector.tensor_scalar(h_nat[:, t, :], x_sb[:, t, :], mv[:, t, 0:1], rstd[:, t:t + 1],
                                        ALU.subtract, ALU.mult).then_inc(h_v, 1)
            nc.vector.memset(ones[:], 0.0).then_inc(ones_v, 1)
            dve.wait_ge(ones_v, 1)
            for r in range(3):
                nc.vector.memset(ones[32 * r:32 * r + 1, :], 1.0).then_inc(ones_v, 1)
            dve.wait_ge(pb_in, 16)
            for r in range(3):
                rows = slice(0, 96 - 32 * r)
                nc.vector.tensor_copy(phib[rows, :], pb[r][rows, :]).then_inc(phib_v, 1)
                if r < 2:
                    rows = slice(0, 64 - 32 * r)
                    dve.wait_ge(phib_v, r + 1)
                    nc.vector.tensor_tensor(pb[r + 1][rows, :], pb[r][rows, :], phib[rows, :], ALU.subtract).then_inc(left_v, 1)
                    dve.wait_ge(left_v, r + 1)
            for s in range(0, 2 * LB, 2):
                dve.wait_ge(pro_mm, ST_PHI + s + 1)
                nc.vector.tensor_copy(phiT[:, s // LB, (s % LB) * 512:(s % LB + 1) * 512], bank[s % 4][:]).then_inc(pro_v, 1)
            for s in (0, 2):
                dve.wait_ge(pro_mm, ST_H + s + 1)
                nc.vector.tensor_copy(hT[:, s // 2, (s % 2) * HALF:(s % 2 + 1) * HALF], bank[(ST_H + s) % 4][:]).then_inc(pro_v, 1)
            dve.wait_ge(pro_v, (ST_H + 4) // 2)
            dve.wait_ge(pro_a, (ST_H + 4) // 2)
            dve.wait_ge(phib_v, 3)

            def combine_sum(t):
                dve.wait_ge(cexp_a, t + 1)
                nc.vector.reduce_sum(csum[:], by_slot(logits[:, t % LR, :]), axis=AX.X).then_inc(csum_v, 1)
                dve.wait_ge(csum_v, t + 1)
                at_least(dve, cmul_g, t)
                nc.vector.reciprocal(cinv[:], csum[:]).then_inc(cinv_v, 1)

            for t in range(TT):
                row = logits[:, t % LR, :]
                work = by_expert(dwork[:])
                dve.wait_ge(L_a, LB * (t + 1))
                nc.vector.reduce_max(dmax[:], by_expert(row), axis=AX.X).then_inc(dmax_v, 1)
                at_least(dve, csub_g, t)
                nc.vector.reduce_max(cmax[:], by_slot(row), axis=AX.X).then_inc(cmax_v, 1)
                dve.wait_ge(dmax_v, t + 1)
                at_least(dve, dmul_v, t)
                nc.vector.tensor_tensor(work, by_expert(row), dmax[:].unsqueeze(2).broadcast_to([P, NE, NS]),
                                        ALU.subtract).then_inc(dsub_v, 1)
                if t:
                    combine_sum(t - 1)
                dve.wait_ge(dexp_a, t + 1)
                nc.vector.reduce_sum(dsum[:], work, axis=AX.X).then_inc(dsum_v, 1)
                dve.wait_ge(dsum_v, t + 1)
                nc.vector.reciprocal(dinv[:], dsum[:]).then_inc(dinv_v, 1)
                dve.wait_ge(dinv_v, t + 1)
                nc.vector.tensor_tensor(by_expert(disp[:, t, :]), work, dinv[:].unsqueeze(2).broadcast_to([P, NE, NS]),
                                        ALU.mult).then_inc(dmul_v, 1)
            combine_sum(TT - 1)

            def inputs(s):
                r = s % 2
                dve.wait_ge(xs_mm, s + 1)
                at_least(dve, tanh_a, s - 1)
                nc.vector.tensor_scalar(xc[:, r, :], psX(s), LOW, HIGH, ALU.max, ALU.min).then_inc(clip_v, 1)
                dve.wait_ge(clip_v, s + 1)
                nc.vector.bn_stats(sstats[:, r, :], xc[:, r, :]).then_inc(sst_v, 1)
                dve.wait_ge(sst_v, s + 1)
                nc.vector.bn_aggr(smv[:, r, :], sstats[:, r, :]).then_inc(smv_v, 1)
                dve.wait_ge(smv_v, s + 1)
                nc.vector.tensor_scalar(sve[:, r:r + 1], smv[:, r, 1:2], LN_EPS, None, ALU.add).then_inc(sve_v, 1)
                dve.wait_ge(srstd_g, s + 1)
                nc.vector.tensor_scalar(snmr[:, r:r + 1], smv[:, r, 0:1], -1.0, srstd[:, r:r + 1],
                                        ALU.mult, ALU.mult).then_inc(snmr_v, 1)

            def outputs(s):
                dve.wait_ge(e_mm, s + 1)
                nc.vector.tensor_tensor(mixed[:, s, :], psE[s % 2][:, 0:HID], mixed[:, s, :], ALU.add).then_inc(mixed_v, 1)

            dve.wait_ge(eb_in, 16 * EPT)
            for s in range(ST):
                inputs(s)
                if s >= 2:
                    outputs(s - 2)
            outputs(ST - 2)
            outputs(ST - 1)
            for t in range(TT):
                dve.wait_ge(y_mm, t + 1)
                nc.vector.tensor_tensor(x_sb[:, t, :], psY[t][:, 0:HID], x_sb[:, t, :], ALU.add).then_inc(y_v, 1)


def perceiver_block(nc, x, ctx, Wq, bq, Wk, bk, Wv, bv, Wo, bo, c_attn_w, c_attn_b, c_proj_w, c_proj_b,
                    phi_w, phi_b, expert_w, expert_b, out):
    with ExitStack() as st:
        x_sb = st.enter_context(nc.sbuf_tensor("x_sb", [P, TT, D], F32))
        ident = st.enter_context(nc.sbuf_tensor("ident", [P, P], F32))
        cross_attention(nc, x_sb, ident, x, ctx, Wq, bq, Wk, bk, Wv, bv, Wo, bo)
        self_attention(nc, x_sb, ident, c_attn_w, c_attn_b, c_proj_w, c_proj_b)
        soft_moe(nc, x_sb, ident, phi_w, phi_b, expert_w, expert_b, out)


_INS = ["x", "ctx_1024", "L0_xattn_Wq", "L0_xattn_bq", "L0_xattn_Wk", "L0_xattn_bk", "L0_xattn_Wv", "L0_xattn_bv",
        "L0_xattn_Wo", "L0_xattn_bo", "L0_attn_c_attn_w", "L0_attn_c_attn_b", "L0_attn_c_proj_w", "L0_attn_c_proj_b",
        "L0_ffn_phi_w", "L0_ffn_phi_b", "L0_ffn_expert_w", "L0_ffn_expert_b"]


def kernel(**inputs):
    import numpy as np
    import concourse.bacc as bacc
    from concourse.bass_utils import run_bass_kernel_spmd

    nc = bacc.Bacc("TRN2", target_bir_lowering=False, num_devices=1)
    arrays, args = {}, []
    for name in _INS:
        a = np.ascontiguousarray(inputs[name])
        arrays[f"in_{name}_dram"] = a
        args.append(nc.dram_tensor(f"in_{name}_dram", a.shape, mybir.dt.from_np(a.dtype), kind="ExternalInput").ap())
    out = nc.dram_tensor("out_dram", (B, S, D), F32, kind="ExternalOutput").ap()
    perceiver_block(nc, *args, out)
    r = run_bass_kernel_spmd(nc, [arrays], core_ids=[0])
    return r.results[0]["out_dram"]
```

```python
from contextlib import ExitStack

import concourse.bass as bass
from concourse import mybir

P = 128
B, S, D = 4, 256, 256
NCTX = 4096
TT = B * S // P
QT = S // P
DH = D // P
CH = 512
J = CH // P
SLOTS = 4
NCH = NCTX // CH
LN_EPS = 1e-5

F32 = mybir.dt.float32
F32R = mybir.dt.float32r
BF16 = mybir.dt.bfloat16
ALU = mybir.AluOpType
ACT = mybir.ActivationFunctionType
AX = mybir.AxisListType


def at_least(eng, sem, value):
    if not isinstance(value, int) or value > 0:
        eng.wait_ge(sem, value)


def next_address(nc):
    return -(-nc.sbuf_base // 32) * 32


def half_wait(k):
    return k // 2 + 1


def row_statistics(dve, nc, x_sb, x_stats, x_mv, t, done, count, stats_v, mv_v):
    dve.wait_ge(done, count)
    nc.vector.bn_stats(x_stats[:, t, :], x_sb[:, t, :]).then_inc(stats_v, 1)
    dve.wait_ge(stats_v, t + 1)
    nc.vector.bn_aggr(x_mv[:, t, :], x_stats[:, t, :]).then_inc(mv_v, 1)


def cross_attention(nc, x_sb, x_stats, x_mv, ident, x, ctx, Wq, bq, Wk, bk, Wv, bv, Wo, bo):
    SCALE = 1.0 / 16.0
    with ExitStack() as st:
        def sb(name, shape, dt=F32):
            return st.enter_context(nc.sbuf_tensor(name, shape, dt))

        def sem(name):
            return st.enter_context(nc.semaphore(name))

        ctx_in_sb = sb("ctx_stage", [P, SLOTS, J * D])
        ctx_hi = sb("ctx_hi", [P, NCH * J * D], F32R)
        ctx_lo = sb("ctx_lo", [P, NCH * J * D], F32R)
        scores = sb("scores", [P, QT, NCTX])
        ctxT_hi = sb("ctxT_hi", [P, 2, DH, CH], F32R)
        ctxT_lo = sb("ctxT_lo", [P, 2, DH, CH], F32R)
        probs = sb("probs", [P, 2, QT, CH])
        pT_hi = sb("pT_hi", [P, 2, QT, CH], F32R)
        pT_lo = sb("pT_lo", [P, 2, QT, CH], F32R)
        qk_hi = sb("qk_hi", [P, DH, B * S], F32R)
        qk_lo = sb("qk_lo", [P, DH, B * S], F32R)
        h_nat = sb("h_nat", [P, TT, D])
        hT = sb("hT", [P, DH, B * S])
        qT = scores[:, 0, 0:DH * B * S].rearrange("p (a t) -> p a t", a=DH)
        w_nat = {w: scores[:, 1, k * DH * D:(k + 1) * DH * D].rearrange("p (a d) -> p a d", a=DH)
                 for k, w in enumerate("qkvo")}
        qk_hi_b = sb("qk_hi_b", [P, DH, S], F32R)
        qk_lo_b = sb("qk_lo_b", [P, DH, S], F32R)
        wT = {w: sb(f"wT_{w}", [P, DH, D]) for w in "qvo"}
        bias = {w: sb(f"b_{w}", [P, DH]) for w in "qkv"}
        bo_all = sb("bo_all", [P, D])
        stats = sb("stats", [P, TT, 6])
        mv = sb("mv", [P, TT, 2])
        ve = sb("ve", [P, TT])
        rstd = sb("rstd", [P, TT])
        power = sb("power", [P, TT])
        qbk = sb("qbk", [P, TT])
        cmax = sb("cmax", [P, QT, NCH])
        rowmax = sb("rowmax", [P, QT])
        negmax = sb("negmax", [P, QT])
        csum = sb("csum", [P, QT, NCH])
        rowsum = sb("rowsum", [P, QT])
        rinv = sb("rinv", [P, QT])
        att = h_nat
        attT = qT
        zT = hT

        bank = [st.enter_context(nc.psum_tensor(f"ps{i}", [P, 512], F32)) for i in range(8)]
        pT, pS, pE, pO = bank[0:2], bank[2:4], bank[4:6], bank[6:8]

        def ctx_banks(c, alone):
            return pE if alone and c % 2 else pT

        def probs_banks(c, alone):
            return pT if alone and c % 2 else pE

        x_in, w_in, ident_ok = sem("x_in"), sem("w_in"), sem("ident_ok")
        st_v, mv_v, ve_v, rstd_g, h_v, pow_g = sem("st_v"), sem("mv_v"), sem("ve_v"), sem("rstd_g"), sem("h_v"), sem("pow_g")
        xbo_g = sem("xbo_g")
        pro_mm, pro_v, pro_a, qklo_v = sem("pro_mm"), sem("pro_v"), sem("pro_a"), sem("qklo_v")
        ctx_in = [sem(f"ctx_in{k}") for k in range(SLOTS)]
        ctxhi_v, split_g, qkb_v = sem("ctxhi_v"), sem("split_g"), sem("qkb_v")
        ctxT_mm, ctxThi_a, ctxTlo_v = sem("ctxT_mm"), sem("ctxThi_a"), sem("ctxTlo_v")
        scores_mm, scores_v = sem("scores_mm"), sem("scores_v")
        max_v, negmax_v = sem("max_v"), sem("negmax_v")
        exp_a = sem("exp_a")
        probsT_mm, probsThi_a, probsTlo_v = sem("probsT_mm"), sem("probsThi_a"), sem("probsTlo_v")
        pv_mm = sem("pv_mm")
        sum_v, rinv_v, att_v = sem("sum_v"), sem("rinv_v"), sem("att_v")
        epi_mm, epi_v, epi_a = sem("epi_mm"), sem("epi_v"), sem("epi_a")
        xst_v, xmv_v = sem("xst_v"), sem("xmv_v")

        ST_W = 0
        ST_H = ST_W + 3
        ST_Q = ST_H + 4
        ST_QK = ST_Q + 4
        ST_QB = ST_QK + 4
        HALF = B * S // 2

        def arrivals(b, c):
            return 16 * (NCH // SLOTS * b + c // SLOTS + 1)

        block = st.enter_context(nc.Block())

        @block.sync
        def _(sp):
            sp.dma_start(x_sb[:], x.rearrange("b (q p) d -> p (b q) d", p=P)).then_inc(x_in, 16)
            for w, a in (("q", Wq), ("k", Wk), ("v", Wv), ("o", Wo)):
                sp.dma_start(w_nat[w][:], a.rearrange("(j p) d -> p j d", p=P)).then_inc(w_in, 16)
            for w, a in (("q", bq), ("k", bk), ("v", bv)):
                sp.dma_start(bias[w][:], a.rearrange("(j p) -> p j", p=P),
                             allow_slow_non_contiguous=True).then_inc(w_in, 16)
            sp.dma_start(bo_all[:], bo.rearrange("(a d) -> a d", a=1).broadcast_to([P, D])).then_inc(w_in, 16)

            chunks = ctx.rearrange("b s d -> (b s) d").rearrange("(g s p j) d -> p g s (j d)", s=SLOTS, p=P, j=J)

            def load(g, s):
                n = SLOTS * g + s
                at_least(sp, split_g, n - SLOTS + 1)
                sp.dma_start(ctx_in_sb[:, s, :],
                             chunks[:, bass.ds(g, 1), s, :].rearrange("p g e -> p (g e)")).then_inc(ctx_in[s], 16)

            for s in range(SLOTS):
                load(0, s)
            with sp.Fori(1, B * NCH // SLOTS) as g:
                for s in range(SLOTS):
                    load(g, s)

        @block.gpsimd
        def _(pool):
            nc.gpsimd.memset(ident[:], 0.0).then_inc(ident_ok, 1)
            nc.gpsimd.memset(power[:], -0.5).then_inc(pow_g, 1)
            pool.wait_ge(ident_ok, 1)
            nc.gpsimd.affine_select(out=ident[:], in_=ident[:], compare_op=ALU.not_equal, fill=1.0, base=0,
                                    pattern=[[-1, P]], channel_multiplier=1).then_inc(ident_ok, 1)
            pool.wait_ge(pow_g, 1)
            pool.wait_ge(ve_v, 1)
            nc.gpsimd.tensor_tensor(rstd[:], ve[:], power[:], ALU.pow).then_inc(rstd_g, 1)
            pool.wait_ge(w_in, 128)
            pool.wait_ge(h_v, TT)
            nc.gpsimd.tensor_tensor(x_sb[:], x_sb[:], bo_all[:].unsqueeze(1).broadcast_to([P, TT, D]),
                                    ALU.add).then_inc(xbo_g, 1)

            with pool.Fori(0, B) as b:
                for c in range(NCH):
                    cols = slice(c * J * D, (c + 1) * J * D)
                    pool.wait_ge(ctxhi_v, NCH * b + c + 1)
                    pool.wait_ge(ctxT_mm, DH * (NCH * b + c + 1))
                    nc.gpsimd.tensor_tensor(ctx_lo[:, cols], ctx_in_sb[:, c % SLOTS, :], ctx_hi[:, cols].bitcast(F32),
                                            ALU.subtract).then_inc(split_g, 1)

        @block.tensor
        def _(pe):
            def bank_free(k):
                if k >= 4:
                    pe.wait_ge(pro_a if k % 2 else pro_v, half_wait(k - 4))

            pe.wait_ge(w_in, 128)
            pe.wait_ge(ident_ok, 2)
            for k, w in enumerate("qvo"):
                for ci in range(DH):
                    for co in range(DH):
                        last = nc.tensor.transpose(bank[k][:, ci * D + co * P:][:, :P],
                                                   w_nat[w][:, co, ci * P:(ci + 1) * P], ident[:])
                last.then_inc(pro_mm, 1)
            pe.wait_ge(h_v, TT)
            for s in range(4):
                k = ST_H + s
                bank_free(k)
                for t in range(4):
                    last = nc.tensor.transpose(bank[k % 4][:, t * P:(t + 1) * P],
                                               h_nat[:, (s % 2) * 4 + t, (s // 2) * P:(s // 2 + 1) * P], ident[:])
                last.then_inc(pro_mm, 1)
            pe.wait_ge(pro_v, half_wait(ST_Q - 1 if (ST_Q - 1) % 2 == 0 else ST_Q - 2))
            pe.wait_ge(pro_a, half_wait(ST_Q - 1 if (ST_Q - 1) % 2 else ST_Q - 2))
            for s in range(4):
                k = ST_Q + s
                for c in range(DH):
                    last = nc.tensor.matmul(bank[k % 4][:], wT["q"][:, c, (s // 2) * P:(s // 2 + 1) * P],
                                            hT[:, c, (s % 2) * HALF:(s % 2 + 1) * HALF], start=c == 0, stop=c == 1)
                last.then_inc(pro_mm, 1)
            pe.wait_ge(pro_v, half_wait(ST_QK - 1 if (ST_QK - 1) % 2 == 0 else ST_QK - 2))
            pe.wait_ge(pro_a, half_wait(ST_QK - 1 if (ST_QK - 1) % 2 else ST_QK - 2))
            for s in range(4):
                k = ST_QK + s
                for c in range(DH):
                    last = nc.tensor.matmul(bank[k % 4][:], w_nat["k"][:, c, (s // 2) * P:(s // 2 + 1) * P],
                                            qT[:, c, (s % 2) * HALF:(s % 2 + 1) * HALF], start=c == 0, stop=c == 1)
                last.then_inc(pro_mm, 1)
            for t in range(TT):
                for c in range(DH):
                    last = nc.tensor.matmul(pO[0][:, t:t + 1], qT[:, c, t * P:(t + 1) * P], bias["k"][:, c:c + 1],
                                            start=c == 0, stop=c == 1)
            last.then_inc(pro_mm, 1)
            pe.wait_ge(qklo_v, 4)
            pe.wait_ge(pro_v, 1 + half_wait(ST_Q - 1))

            def transpose_ctx(b, c, alone):
                n = NCH * b + c
                to = ctx_banks(c, alone)
                pe.wait_ge(ctx_in[c % SLOTS], arrivals(b, c))
                for dh in range(DH):
                    at_least(pe, ctxTlo_v, 2 * n + dh - (3 if alone else 1))
                    for j in range(J):
                        last = nc.tensor.transpose(to[dh][:, j * P:(j + 1) * P],
                                                   ctx_in_sb[:, c % SLOTS, j * D + dh * P:][:, :P], ident[:])
                    last.then_inc(ctxT_mm, 1)

            def score(b, c):
                n = NCH * b + c
                pe.wait_ge(ctxTlo_v, 2 * n + 2)
                for q in range(QT):
                    at_least(pe, scores_v, 2 * n + q - 1)
                    step = 0
                    for a, k in ((qk_hi_b, ctxT_hi), (qk_lo_b, ctxT_hi), (qk_hi_b, ctxT_lo)):
                        for dh in range(DH):
                            last = nc.tensor.matmul(pS[q][:], a[:, dh, q * P:(q + 1) * P], k[:, c % 2, dh, :],
                                                    start=step == 0, stop=step == 5)
                            step += 1
                    last.then_inc(scores_mm, 1)

            def transpose_probs(b, c, alone):
                m = NCH * b + c
                to = probs_banks(c, alone)
                for q in range(QT):
                    pe.wait_ge(exp_a, 2 * m + q + 1)
                    if c >= (2 if alone else 1):
                        pe.wait_ge(probsTlo_v, 2 * m + q - (3 if alone else 1))
                    for j in range(J):
                        last = nc.tensor.transpose(to[q][:, j * P:(j + 1) * P],
                                                   probs[:, c % 2, q, j * P:(j + 1) * P], ident[:])
                    last.then_inc(probsT_mm, 1)

            def mix(b, c, scoring):
                m = NCH * b + c
                pe.wait_ge(probsTlo_v, 2 * m + 2)
                pe.wait_ge(split_g, m + 1)
                if c == 0 and not scoring:
                    pe.wait_ge(att_v, QT * b)
                for q in range(QT):
                    for j in range(J):
                        hi = ctx_hi[:, (c * J + j) * D:(c * J + j + 1) * D]
                        lo = ctx_lo[:, (c * J + j) * D:(c * J + j + 1) * D]
                        cols = slice(j * P, (j + 1) * P)
                        nc.tensor.matmul(pO[q][:, 0:D], pT_hi[:, c % 2, q, cols], hi, start=c == 0 and j == 0, stop=False)
                        nc.tensor.matmul(pO[q][:, 0:D], pT_hi[:, c % 2, q, cols], lo, start=False, stop=False)
                        last = nc.tensor.matmul(pO[q][:, 0:D], pT_lo[:, c % 2, q, cols], hi, start=False,
                                                stop=c == NCH - 1 and j == J - 1)
                last.then_inc(pv_mm, 1)

            def batch(b, more):
                pe.wait_ge(qkb_v, 2 * b + 2)
                for c in range(NCH):
                    score(b, c)
                    if c == 0:
                        transpose_probs(b - 1, 0, False)
                    if c < NCH - 1:
                        transpose_ctx(b, c + 1, False)
                    elif more:
                        transpose_ctx(b + 1, 0, False)
                    mix(b - 1, c, True)
                    if c < NCH - 1:
                        transpose_probs(b - 1, c + 1, False)

            transpose_ctx(0, 0, True)
            transpose_ctx(0, 1, True)
            pe.wait_ge(qkb_v, 2)
            for c in range(NCH):
                score(0, c)
                if c < NCH - 2:
                    transpose_ctx(0, c + 2, True)
            transpose_ctx(1, 0, False)
            with pe.Fori(1, B - 1) as b:
                batch(b, True)
            batch(B - 1, False)
            transpose_probs(B - 1, 0, True)
            transpose_probs(B - 1, 1, True)
            for c in range(NCH):
                mix(B - 1, c, False)
                if c < NCH - 2:
                    transpose_probs(B - 1, c + 2, True)

            pe.wait_ge(att_v, TT)
            for k in range(4):
                for t in range(4):
                    last = nc.tensor.transpose(bank[k][:, t * P:(t + 1) * P],
                                               att[:, (k % 2) * 4 + t, (k // 2) * P:(k // 2 + 1) * P], ident[:])
                last.then_inc(epi_mm, 1)
            pe.wait_ge(epi_v, 2)
            pe.wait_ge(epi_a, 2)
            for k in range(4):
                for c in range(DH):
                    last = nc.tensor.matmul(bank[k][:], wT["v"][:, c, (k // 2) * P:(k // 2 + 1) * P],
                                            attT[:, c, (k % 2) * HALF:(k % 2 + 1) * HALF], start=c == 0, stop=c == 1)
                last.then_inc(epi_mm, 1)
            pe.wait_ge(epi_v, 2 + 4)
            for k in range(TT):
                for c in range(DH):
                    last = nc.tensor.matmul(bank[k][:, 0:D], zT[:, c, k * P:(k + 1) * P], wT["o"][:, c, :],
                                            start=c == 0, stop=c == 1)
                last.then_inc(epi_mm, 1)

        @block.scalar
        def _(act):
            act.wait_ge(w_in, 128)
            nc.scalar.wait_ge(pro_mm, 2)
            nc.scalar.copy(wT["v"][:].rearrange("p a b -> p (a b)"), bank[1][:]).then_inc(pro_a, 1)
            for s in range(4):
                k = ST_H + s
                if k % 2:
                    act.wait_ge(pro_mm, k + 1)
                    nc.scalar.copy(hT[:, s // 2, (s % 2) * HALF:(s % 2 + 1) * HALF], bank[k % 4][:]).then_inc(pro_a, 1)
            for s in range(4):
                k = ST_Q + s
                if k % 2:
                    act.wait_ge(pro_mm, k + 1)
                    nc.scalar.activation(qT[:, s // 2, (s % 2) * HALF:(s % 2 + 1) * HALF], bank[k % 4][:], ACT.Identity,
                                         bias=bias["q"][:, s // 2:s // 2 + 1]).then_inc(pro_a, 1)
            for s in range(4):
                k = ST_QK + s
                act.wait_ge(pro_mm, k + 1)
                nc.scalar.copy(qk_hi[:, s // 2, (s % 2) * HALF:(s % 2 + 1) * HALF], bank[k % 4][:]).then_inc(pro_a, 1)

            def ctx_high(b, c, alone):
                n = NCH * b + c
                at_least(act, scores_mm, 2 * n - 2)
                for dh in range(DH):
                    act.wait_ge(ctxT_mm, 2 * n + dh + 1)
                    nc.scalar.copy(ctxT_hi[:, c % 2, dh, :], ctx_banks(c, alone)[dh][:]).then_inc(ctxThi_a, 1)

            def exps(b, c):
                m = NCH * b + c
                act.wait_ge(negmax_v, b + 1)
                if c == 0:
                    act.wait_ge(sum_v, b + 1)
                for q in range(QT):
                    if c >= 2:
                        act.wait_ge(probsT_mm, 2 * m + q - 3)
                    nc.scalar.activation(probs[:, c % 2, q, :], scores[:, q, c * CH:(c + 1) * CH], ACT.Exp,
                                         bias=negmax[:, q:q + 1], scale=SCALE,
                                         accum_out=csum[:, q, c:c + 1]).then_inc(exp_a, 1)

            def probs_high(b, c, alone):
                m = NCH * b + c
                for q in range(QT):
                    act.wait_ge(probsT_mm, 2 * m + q + 1)
                    nc.scalar.copy(pT_hi[:, c % 2, q, :], probs_banks(c, alone)[q][:]).then_inc(probsThi_a, 1)

            def batch(b, more):
                exps(b - 1, 0)
                probs_high(b - 1, 0, False)
                for c in range(NCH - 1):
                    ctx_high(b, c + 1, False)
                    exps(b - 1, c + 1)
                    probs_high(b - 1, c + 1, False)
                if more:
                    ctx_high(b + 1, 0, False)

            for c in range(NCH):
                ctx_high(0, c, True)
            ctx_high(1, 0, False)
            with act.Fori(1, B - 1) as b:
                batch(b, True)
            batch(B - 1, False)
            exps(B - 1, 0)
            exps(B - 1, 1)
            for c in range(NCH):
                probs_high(B - 1, c, True)
                if c < NCH - 2:
                    exps(B - 1, c + 2)

            for k in (1, 3):
                act.wait_ge(epi_mm, k + 1)
                nc.scalar.copy(attT[:, k // 2, (k % 2) * HALF:(k % 2 + 1) * HALF], bank[k][:]).then_inc(epi_a, 1)

        @block.vector
        def _(dve):
            dve.wait_ge(x_in, 16)
            for t in range(TT):
                nc.vector.bn_stats(stats[:, t, :], x_sb[:, t, :]).then_inc(st_v, 1)
            for t in range(TT):
                dve.wait_ge(st_v, t + 1)
                nc.vector.bn_aggr(mv[:, t, :], stats[:, t, :]).then_inc(mv_v, 1)
            dve.wait_ge(mv_v, TT)
            nc.vector.tensor_scalar(ve[:], mv[:, :, 1], LN_EPS, None, ALU.add).then_inc(ve_v, 1)
            dve.wait_ge(rstd_g, 1)
            for t in range(TT):
                nc.vector.tensor_scalar(h_nat[:, t, :], x_sb[:, t, :], mv[:, t, 0:1], rstd[:, t:t + 1],
                                        ALU.subtract, ALU.mult).then_inc(h_v, 1)
            for k, w in ((0, "q"), (2, "o")):
                dve.wait_ge(pro_mm, k + 1)
                nc.vector.tensor_copy(wT[w][:].rearrange("p a b -> p (a b)"), bank[k][:]).then_inc(pro_v, 1)
            for s in range(4):
                k = ST_H + s
                if k % 2 == 0:
                    dve.wait_ge(pro_mm, k + 1)
                    nc.vector.tensor_copy(hT[:, s // 2, (s % 2) * HALF:(s % 2 + 1) * HALF], bank[k % 4][:]).then_inc(pro_v, 1)
            dve.wait_ge(w_in, 128)
            for s in range(4):
                k = ST_Q + s
                if k % 2 == 0:
                    dve.wait_ge(pro_mm, k + 1)
                    nc.vector.tensor_scalar(qT[:, s // 2, (s % 2) * HALF:(s % 2 + 1) * HALF], bank[k % 4][:],
                                            bias["q"][:, s // 2:s // 2 + 1], None, ALU.add).then_inc(pro_v, 1)
            for s in range(4):
                cols = slice((s % 2) * HALF, (s % 2 + 1) * HALF)
                dve.wait_ge(pro_a, half_wait(ST_Q - 1 if (ST_Q - 1) % 2 else ST_Q - 2) + 2 + s + 1)
                nc.vector.tensor_tensor(qk_lo[:, s // 2, cols], bank[(ST_QK + s) % 4][:],
                                        qk_hi[:, s // 2, cols].bitcast(F32), ALU.subtract).then_inc(qklo_v, 1)
            dve.wait_ge(pro_mm, ST_QB + 1)
            nc.vector.tensor_copy(qbk[:], pO[0][:, 0:TT]).then_inc(pro_v, 1)
            dve.wait_ge(pro_v, 1 + half_wait(ST_Q - 1))
            dve.wait_ge(qklo_v, 4)
            nc.vector.memset(rowsum[:], 0.0).then_inc(sum_v, 1)

            def ctx_low(b, c, alone):
                n = NCH * b + c
                for dh in range(DH):
                    dve.wait_ge(ctxThi_a, 2 * n + dh + 1)
                    nc.vector.tensor_tensor(ctxT_lo[:, c % 2, dh, :], ctx_banks(c, alone)[dh][:], ctxT_hi[:, c % 2, dh, :].bitcast(F32),
                                            ALU.subtract).then_inc(ctxTlo_v, 1)

            def ctx_high(b, c):
                n = NCH * b + c
                dve.wait_ge(ctx_in[c % SLOTS], arrivals(b, c))
                at_least(dve, pv_mm, n - NCH + 1)
                nc.vector.tensor_copy(ctx_hi[:, c * J * D:(c + 1) * J * D], ctx_in_sb[:, c % SLOTS, :]).then_inc(ctxhi_v, 1)

            def scores_out(b, c):
                n = NCH * b + c
                for q in range(QT):
                    dve.wait_ge(scores_mm, 2 * n + q + 1)
                    at_least(dve, exp_a, 2 * n + q + 1 - QT * NCH)
                    nc.vector.tensor_scalar(scores[:, q, c * CH:(c + 1) * CH], pS[q][:], qbk[:, bass.ds(b * QT + q, 1)], None,
                                            ALU.add, ALU.max,
                                            accum_out=cmax[:, q, c:c + 1]).then_inc(scores_v, 1)

            def probs_low(b, c, alone):
                m = NCH * b + c
                for q in range(QT):
                    dve.wait_ge(probsThi_a, 2 * m + q + 1)
                    nc.vector.tensor_tensor(pT_lo[:, c % 2, q, :], probs_banks(c, alone)[q][:], pT_hi[:, c % 2, q, :].bitcast(F32),
                                            ALU.subtract).then_inc(probsTlo_v, 1)

            def maxima(b):
                dve.wait_ge(scores_v, QT * NCH * (b + 1))
                nc.vector.reduce_max(rowmax[:], cmax[:], axis=AX.X).then_inc(max_v, 1)
                dve.wait_ge(max_v, b + 1)
                nc.vector.tensor_scalar(negmax[:], rowmax[:], -SCALE, None, ALU.mult).then_inc(negmax_v, 1)

            def normalise(b):
                dve.wait_ge(exp_a, QT * NCH * (b + 1))
                nc.vector.reduce_sum(rowsum[:], csum[:], axis=AX.X).then_inc(sum_v, 1)
                dve.wait_ge(sum_v, b + 2)
                nc.vector.reciprocal(rinv[:], rowsum[:]).then_inc(rinv_v, 1)
                dve.wait_ge(rinv_v, b + 1)
                dve.wait_ge(pv_mm, NCH * (b + 1))
                for q in range(QT):
                    nc.vector.tensor_scalar(att[:].rearrange("p t d -> p (t d)")[:, bass.ds((b * QT + q) * D, D)], pO[q][:, 0:D],
                                            rinv[:, q:q + 1], None, ALU.mult).then_inc(att_v, 1)

            def batch_queries(b):
                at_least(dve, scores_mm, QT * NCH * b)
                for part, of_all in ((qk_hi_b, qk_hi), (qk_lo_b, qk_lo)):
                    nc.vector.tensor_copy(part[:], of_all[:, :, bass.ds(b * S, S)].bitcast(F32)).then_inc(qkb_v, 1)

            def batch(b, more):
                for c in range(NCH):
                    scores_out(b, c)
                    if c == 0:
                        probs_low(b - 1, 0, False)
                    if c < NCH - 1:
                        ctx_low(b, c + 1, False)
                    else:
                        maxima(b)
                        if more:
                            batch_queries(b + 1)
                            ctx_low(b + 1, 0, False)
                    if c:
                        ctx_high(b, c - 1)
                    if c < NCH - 1:
                        probs_low(b - 1, c + 1, False)
                ctx_high(b, NCH - 1)
                normalise(b - 1)

            batch_queries(0)
            ctx_low(0, 0, True)
            for c in range(NCH):
                if c < NCH - 1:
                    ctx_low(0, c + 1, True)
                scores_out(0, c)
                if c == NCH - 1:
                    maxima(0)
                    batch_queries(1)
                    ctx_low(1, 0, False)
                ctx_high(0, c)
            with dve.Fori(1, B - 1) as b:
                batch(b, True)
            batch(B - 1, False)
            for c in range(NCH):
                probs_low(B - 1, c, True)
            normalise(B - 1)

            for k in (0, 2):
                dve.wait_ge(epi_mm, k + 1)
                nc.vector.tensor_copy(attT[:, k // 2, (k % 2) * HALF:(k % 2 + 1) * HALF], bank[k][:]).then_inc(epi_v, 1)
            for k in range(4):
                cols = slice((k % 2) * HALF, (k % 2 + 1) * HALF)
                dve.wait_ge(epi_mm, 4 + k + 1)
                nc.vector.scalar_tensor_tensor(out=zT[:, k // 2, cols], in0=bank[k][:], scalar=bias["v"][:, k // 2:k // 2 + 1],
                                               in1=hT[:, k // 2, cols], op0=ALU.add, op1=ALU.add).then_inc(epi_v, 1)
            dve.wait_ge(xbo_g, 1)
            for k in range(TT):
                dve.wait_ge(epi_mm, 8 + k + 1)
                nc.vector.tensor_tensor(x_sb[:, k, :], bank[k][:, 0:D], x_sb[:, k, :], ALU.add).then_inc(epi_v, 1)
                if k:
                    row_statistics(dve, nc, x_sb, x_stats, x_mv, k - 1, epi_v, 6 + k, xst_v, xmv_v)
            row_statistics(dve, nc, x_sb, x_stats, x_mv, TT - 1, epi_v, 6 + TT, xst_v, xmv_v)


def phi_places(disp):
    flat = disp[:].rearrange("p t s -> p (t s)")
    SL = disp.shape[2]
    phi_size = SL // P * D
    return (flat[:, 0:phi_size].rearrange("p (k d) -> p k d", k=SL // P), flat[:, phi_size:phi_size + SL],
            flat[:, phi_size + SL:])


def self_attention(nc, x_sb, x_stats, x_mv, ident, disp, ones, phib, qk_dram, c_attn_w, c_attn_b, c_proj_w, c_proj_b, phi_w, phi_b):
    NH = 16
    HD = D // NH
    GH = 4
    NG = NH // GH
    HPH = P // HD
    FIRST_END = S // 3
    SECOND_END = 2 * S // 3
    FOCUS = 1.6
    SCALE = HD ** -0.5
    MASKED = -3.0e38
    HALF = B * S // 2
    NPART = 3
    Q_STACK = (0, 0, 1, 0, 2, 1)
    K_STACK = (0, 1, 0, 2, 0, 1)
    STACK = len(Q_STACK)
    RING = 4
    with ExitStack() as st:
        def sb(name, shape, dt=F32):
            return st.enter_context(nc.sbuf_tensor(name, shape, dt))

        def sem(name):
            return st.enter_context(nc.semaphore(name))

        w_qkv = sb("w_qkv", [P, DH, 3 * D])
        w_proj = sb("w_proj", [P, DH, D])
        b_qk = sb("b_qk2", [P, 2 * DH])
        b_v = sb("b_v2", [P, D])
        b_proj = sb("b_proj2", [P, D])
        ve = sb("ve2", [P, TT])
        rstd = sb("rstd2", [P, TT])
        power = sb("power2", [P, TT])
        h_nat = sb("h2_nat", [P, TT, D])
        hT = sb("h2T", [P, DH, B * S])
        parts = sb("qk_parts", [P, RING, NPART, HALF], BF16)
        rest = sb("qk_rest", [P, 2, HALF])
        q_rows = sb("q_rows", [STACK * HD, NH, B * S], BF16)
        v_all = sb("v_all", [P, TT, D])
        v_pad = sb("v_pad", [P, QT, NH, P])
        ident_bf = sb("ident_bf", [P, P], BF16)
        causal = sb("causal", [P, P], BF16)
        focus = sb("focus", [P, 3, S])
        eA = sb("eA", [P, 2, GH, P])
        eB = sb("eB", [P, 2, GH, S])
        gmax = sb("gmax", [P, 2, 2 * GH])
        nmax = sb("nmax", [P, 2, 2 * GH])
        esum = sb("esum", [P, 2, 2 * GH])
        rinv = sb("rinv2", [P, 2, 2 * GH])
        pT = sb("pT2", [P, 2, 3, 512])
        oT = h_nat[:].rearrange("p t d -> p (t d)").rearrange("p (c t) -> p c t", c=DH)

        bank = [st.enter_context(nc.psum_tensor(f"pq{i}", [P, 512], F32)) for i in range(8)]
        psS, psT, psO = bank[0:4], bank[4:7], bank[7]

        HEADS_DONE = (0, GH, GH + 2)

        def following(b, g, n):
            return (b + (g + n) // NG, (g + n) % NG) if g + n >= NG else (b, g + n)

        def before(b, g):
            return (b, g - 1) if g else (b - 1, NG - 1)

        def is_first(b, g):
            return isinstance(b, int) and b == 0 and g == 0

        def columns(g, part):
            return psS[(3 * g + part) % 4]

        w_in = sem("w2_in")
        ve_v, rstd_g, h_v = sem("ve2_v"), sem("rstd2_g"), sem("h2_v")
        const_g, vzero_g, consts_g, xb_g = sem("const2_g"), sem("vzero_g"), sem("consts2_g"), sem("xb2_g")
        pro_mm, pro_v, pro_a = sem("pro2_mm"), sem("pro2_v"), sem("pro2_a")
        high_a, rest_v, middle_a, low_g = sem("high_a"), sem("rest_v"), sem("middle_a"), sem("low_g")
        parts_out, rows_in = [sem(f"parts_out{k}") for k in range(2)], [sem(f"rows_in{k}") for k in range(8)]
        vpad_g = sem("vpad_g")
        s_mm, gmax_v, nmax_v, exp_a = sem("s2_mm"), sem("gmax_v"), sem("nmax_v"), sem("exp2_a")
        focus_v, fsum_v, rinv_v, norm_g = sem("focus_v"), sem("fsum_v"), sem("rinv2_v"), sem("norm_g")
        t_mm, pT_a, pT_v, av_mm, o_a = sem("t2_mm"), sem("pT_a"), sem("pT_v"), sem("av_mm"), sem("o_a")
        out_mm, out_v, xst_v, xmv_v = sem("out2_mm"), sem("out2_v"), sem("xst2_v"), sem("xmv2_v")
        phi_in, ones_v, phib_v, left_v = sem("phi_in"), sem("ones_v"), sem("phib_v"), sem("left_v")

        phi_nat, phi_b_rest, free = phi_places(disp)
        k_rows = free[0:STACK * HD, 0:NH * B * S // 2].bitcast(BF16).rearrange("p (h t) -> p h t", h=NH)

        ST_H = 0
        ST_QK = 4
        ST_V = 8
        QK_FIRST = 6
        QK_TILES = (0, 2, 1, 3)

        def stage_bank(k):
            return bank[k] if k < ST_QK else bank[4 + k % 4]

        def qk_number(s):
            return ST_QK + s if s < 4 else ST_V + s

        def qk_stage(s):
            return QK_TILES[s % 4], slice(s // 4 * HALF, (s // 4 + 1) * HALF)

        block = st.enter_context(nc.Block())

        @block.sync
        def _(sp):
            sp.dma_start(w_qkv[:], c_attn_w.rearrange("(j p) n -> p j n", p=P)).then_inc(w_in, 16)
            sp.dma_start(w_proj[:], c_proj_w.rearrange("(j p) n -> p j n", p=P)).then_inc(w_in, 16)
            sp.dma_start(b_qk[:], c_attn_b[0:2 * D].rearrange("(j p) -> p j", p=P),
                         allow_slow_non_contiguous=True).then_inc(w_in, 16)
            sp.dma_start(b_v[:], c_attn_b[2 * D:3 * D].rearrange("(a d) -> a d", a=1).broadcast_to([P, D])).then_inc(w_in, 16)
            sp.dma_start(b_proj[:], c_proj_b.rearrange("(a d) -> a d", a=1).broadcast_to([P, D])).then_inc(w_in, 16)

            def store_parts(s):
                rows, tokens = qk_stage(s)
                sp.wait_ge(low_g, s + 1)
                sp.dma_start(qk_dram[rows, :, :, tokens].rearrange("c p t -> p c t"), parts[:, s % RING, :, :]).then_inc(parts_out[s % 2], 16)

            def stack_rows(s):
                rows, tokens = qk_stage(s)
                heads = slice((rows % DH) * HPH, (rows % DH + 1) * HPH)
                sp.wait_ge(parts_out[s % 2], 16 * (s // 2 + 1))
                for r in range(STACK):
                    to, part = (q_rows, Q_STACK[r]) if rows < DH else (k_rows, K_STACK[r])
                    sp.dma_start(to[r * HD:(r + 1) * HD, heads, tokens],
                                 qk_dram[rows, part, :, tokens].rearrange("(h i) t -> i h t", i=HD)).then_inc(rows_in[s], 16)

            for s in range(8):
                store_parts(s)
                if s:
                    stack_rows(s - 1)
            stack_rows(7)
            sp.dma_start(phi_b_rest, phi_b.rearrange("(a s) -> a s", a=1).broadcast_to([P, phi_b.shape[0]])).then_inc(phi_in, 16)
            sp.wait_ge(phi_in, 16)
            sp.dma_start(phi_nat, phi_w.rearrange("(k p) d -> p k d", p=P)).then_inc(phi_in, 16)
            sp.wait_ge(phi_in, 32)

        @block.gpsimd
        def _(pool):
            nc.gpsimd.memset(power[:], -0.5).then_inc(const_g, 1)
            nc.gpsimd.memset(causal[:], 0.0).then_inc(const_g, 1)
            nc.gpsimd.memset(focus[:], 1.0).then_inc(const_g, 1)
            pool.wait_ge(const_g, 1)
            pool.wait_ge(ve_v, 1)
            nc.gpsimd.tensor_tensor(rstd[:], ve[:], power[:], ALU.pow).then_inc(rstd_g, 1)
            pool.wait_ge(const_g, 3)
            nc.gpsimd.affine_select(out=causal[:], in_=causal[:], compare_op=ALU.is_ge, fill=MASKED, base=0,
                                    pattern=[[-1, P]], channel_multiplier=1).then_inc(consts_g, 1)
            nc.gpsimd.tensor_copy(ident_bf[:], ident[:]).then_inc(consts_g, 1)
            nc.gpsimd.memset(focus[:, 0, 0:FIRST_END], FOCUS).then_inc(consts_g, 1)
            nc.gpsimd.memset(focus[:, 1, FIRST_END:SECOND_END], FOCUS).then_inc(consts_g, 1)
            nc.gpsimd.memset(focus[:, 2, SECOND_END:S], FOCUS).then_inc(consts_g, 1)
            nc.gpsimd.memset(v_pad[:], 0.0).then_inc(vzero_g, 1)
            pool.wait_ge(w_in, 80)
            pool.wait_ge(h_v, TT)
            nc.gpsimd.tensor_tensor(x_sb[:], x_sb[:], b_proj[:].unsqueeze(1).broadcast_to([P, TT, D]),
                                    ALU.add).then_inc(xb_g, 1)

            def pad_values(b, half):
                for kt in range(QT):
                    first = (half * HPH) * P
                    diagonal = v_pad[:, kt, :, :].rearrange("p h c -> p (h c)")[:, first:first + HPH * P]
                    diagonal = bass.AP(diagonal.tensor, diagonal.offset, [diagonal.ap[0], [P + HD, HPH], [1, HD]])
                    nc.gpsimd.tensor_copy(diagonal, v_all[:].rearrange("p t d -> p (t d)")[
                        :, bass.ds((b * QT + kt) * D + half * P, P)].rearrange("p (h c) -> p h c", h=HPH)).then_inc(vpad_g, 1)

            def normalise(b, g):
                pool.wait_ge(rinv_v, 2 * (NG * b + g) + 1)
                nc.gpsimd.tensor_tensor(eA[:, g % 2, :, :], eA[:, g % 2, :, :],
                                        rinv[:, g % 2, 0:GH].unsqueeze(2).broadcast_to([P, GH, P]), ALU.mult).then_inc(norm_g, 1)
                pool.wait_ge(rinv_v, 2 * (NG * b + g) + 2)
                nc.gpsimd.tensor_tensor(eB[:, g % 2, :, :], eB[:, g % 2, :, :],
                                        rinv[:, g % 2, GH:].unsqueeze(2).broadcast_to([P, GH, S]), ALU.mult).then_inc(norm_g, 1)

            def low_part(s):
                pool.wait_ge(middle_a, s + 1)
                nc.gpsimd.tensor_tensor(parts[:, s % RING, 2, :], rest[:, s % 2, :], parts[:, s % RING, 1, :],
                                        ALU.subtract).then_inc(low_g, 1)

            for s in range(QK_FIRST):
                low_part(s)
            normalise(0, 0)
            for s in range(QK_FIRST, 8):
                low_part(s)
            pool.wait_ge(vzero_g, 1)
            pool.wait_ge(pro_v, 6)
            for half in range(DH):
                pad_values(0, half)

            def batch(b, last):
                for g in range(NG):
                    if g + 1 < NG or not last:
                        normalise(*following(b, g, 1))
                    if g == 1 and not (isinstance(b, int) and b == 0):
                        pool.wait_ge(av_mm, NG * b)
                        pad_values(b, 1)
                    if g == 3 and not last:
                        pool.wait_ge(av_mm, NG * b + NG // 2)
                        pad_values(b + 1, 0)

            batch(0, False)
            with pool.Fori(1, B - 1) as b:
                batch(b, False)
            batch(B - 1, True)

        @block.tensor
        def _(pe):
            for s in range(4):
                k = ST_H + s
                pe.wait_ge(h_v, (s // 2 + 1) * 4)
                for t in range(4):
                    last = nc.tensor.transpose(stage_bank(k)[:, t * P:(t + 1) * P],
                                               h_nat[:, (s // 2) * 4 + t, (s % 2) * P:(s % 2 + 1) * P], ident[:])
                last.then_inc(pro_mm, 1)

            def project_qk(s):
                k = qk_number(s)
                rows, tokens = qk_stage(s)
                if s >= 4:
                    pe.wait_ge(pro_v, 2 + s - 3)
                for c in range(DH):
                    last = nc.tensor.matmul(stage_bank(k)[:], w_qkv[:, c, rows * P:(rows + 1) * P], hT[:, c, tokens],
                                            start=c == 0, stop=c == 1)
                last.then_inc(pro_mm, 1)

            def project_v(s):
                k = ST_V + s
                pe.wait_ge(rest_v, s + 1)
                for t in range(2):
                    for c in range(DH):
                        last = nc.tensor.matmul(stage_bank(k)[:, t * D:(t + 1) * D],
                                                hT[:, c, (2 * s + t) * P:(2 * s + t + 1) * P], w_qkv[:, c, 2 * D:3 * D],
                                                start=c == 0, stop=c == 1)
                last.then_inc(pro_mm, 1)

            def score(b, g, part):
                G = NG * b + g
                to = columns(g, part)
                if part == 0:
                    at_least(pe, exp_a, 2 * GH * (G - 1))
                    for h in range(GH):
                        first = bass.ds(b * S, P)
                        nc.tensor.matmul(to[:, h * P:(h + 1) * P], q_rows[:, g * GH + h, first], k_rows[:, g * GH + h, first],
                                         start=h == 0, stop=False)
                    last = nc.tensor.matmul(to[:], ident_bf[:], causal[:].unsqueeze(1).broadcast_to([P, GH, P]), start=False, stop=True)
                else:
                    at_least(pe, exp_a, 2 * GH * (G - 1) + HEADS_DONE[part])
                    for i in range(2):
                        head = g * GH + 2 * (part - 1) + i
                        nc.tensor.matmul(to[:, i * S:(i + 1) * S], q_rows[:, head, bass.ds(b * S + P, P)],
                                         k_rows[:, head, bass.ds(b * S, S)], start=i == 0, stop=False)
                    last = nc.tensor.matmul(to[:].rearrange("p (h k) -> p h k", h=2)[:, :, P:S], ident_bf[:],
                                            causal[:].unsqueeze(1).broadcast_to([P, 2, P]), start=False, stop=True)
                last.then_inc(s_mm, 1)

            def transpose(b, g):
                G = NG * b + g
                pe.wait_ge(norm_g, 2 * G + 2)
                at_least(pe, pT_a, G)
                at_least(pe, pT_v, 2 * G)
                for h in range(GH):
                    to = psT[h // 2][:, (h % 2) * S:(h % 2 + 1) * S]
                    nc.tensor.transpose(to[:, 0:P], eA[:, g % 2, h, :], ident[:])
                    last = nc.tensor.transpose(to[:, P:S], eB[:, g % 2, h, 0:P], ident[:])
                    if h % 2:
                        last.then_inc(t_mm, 1)
                for h in range(GH):
                    last = nc.tensor.transpose(psT[2][:, h * P:(h + 1) * P], eB[:, g % 2, h, P:S], ident[:])
                last.then_inc(t_mm, 1)

            def mix(b, g):
                G = NG * b + g
                half = g * GH // HPH
                if g * GH % HPH == 0:
                    pe.wait_ge(vpad_g, 4 * b + 2 * half + 2)
                    at_least(pe, o_a, DH * b + half)
                pe.wait_ge(pT_a, G + 1)
                pe.wait_ge(pT_v, 2 * G + 2)
                for h in range(GH):
                    head = g * GH + h
                    nc.tensor.matmul(psO[:, half * S:(half + 1) * S], v_pad[:, 0, head, :], pT[:, g % 2, h // 2, (h % 2) * S:(h % 2 + 1) * S],
                                     start=head % HPH == 0, stop=False)
                    last = nc.tensor.matmul(psO[:, half * S + P:(half + 1) * S], v_pad[:, 1, head, :], pT[:, g % 2, 2, h * P:(h + 1) * P],
                                            start=False, stop=head % HPH == HPH - 1)
                last.then_inc(av_mm, 1)

            pe.wait_ge(w_in, 80)
            pe.wait_ge(pro_v, 2)
            pe.wait_ge(pro_a, 2)
            for s in range(4):
                project_qk(s)
            for s in range(4):
                project_v(s)
            for s in range(4, QK_FIRST):
                project_qk(s)
            pe.wait_ge(consts_g, 5)
            for s in range(2):
                pe.wait_ge(rows_in[s], 16 * STACK)
            for part in range(3):
                score(0, 0, part)
            score(0, 1, 0)
            for s in range(QK_FIRST, 8):
                project_qk(s)
            pe.wait_ge(rest_v, 7)

            def batch(b, last):
                for g in range(NG):
                    if is_first(b, g):
                        for s in (2, 3):
                            pe.wait_ge(rows_in[s], 16 * STACK)
                    if is_first(b, g - 1):
                        pe.wait_ge(rest_v, 8)
                    if is_first(b, g - (NG - 1)):
                        for s in range(4, 8):
                            pe.wait_ge(rows_in[s], 16 * STACK)
                    if g + 1 < NG or not last:
                        score(*following(b, g, 1), 1)
                        score(*following(b, g, 1), 2)
                    if g == 0 and not is_first(b, g):
                        mix(*before(b, g))
                    transpose(b, g)
                    if g + 2 < NG or not last:
                        score(*following(b, g, 2), 0)
                    if g:
                        mix(*before(b, g))

            batch(0, False)
            with pe.Fori(1, B - 1) as b:
                batch(b, False)
            batch(B - 1, True)
            mix(B - 1, NG - 1)
            pe.wait_ge(o_a, DH * B)
            for t in range(TT):
                for c in range(DH):
                    last = nc.tensor.matmul(bank[t][:, 0:D], oT[:, c, t * P:(t + 1) * P], w_proj[:, c, :], start=c == 0, stop=c == 1)
                last.then_inc(out_mm, 1)

        @block.scalar
        def _(act):
            def high_part(s):
                rows, tokens = qk_stage(s)
                act.wait_ge(pro_mm, qk_number(s) + 1)
                if s >= RING:
                    act.wait_ge(parts_out[s % 2], 16 * ((s - RING) // 2 + 1))
                nc.scalar.activation(parts[:, s % RING, 0, :], stage_bank(qk_number(s))[:], ACT.Identity,
                                     bias=b_qk[:, rows:rows + 1]).then_inc(high_a, 1)

            def middle_part(s):
                act.wait_ge(rest_v, s + 1)
                nc.scalar.copy(parts[:, s % RING, 1, :], rest[:, s % 2, :]).then_inc(middle_a, 1)

            for s in (1, 3):
                act.wait_ge(pro_mm, ST_H + s + 1)
                nc.scalar.copy(hT[:, s % 2, (s // 2) * HALF:(s // 2 + 1) * HALF], stage_bank(s)[:]).then_inc(pro_a, 1)
            act.wait_ge(w_in, 80)
            for s in range(QK_FIRST):
                high_part(s)
                middle_part(s)

            def exps(b, g, part):
                act.wait_ge(nmax_v, 3 * (NG * b + g) + part + 1)
                if part == 0:
                    for h in range(GH):
                        nc.scalar.activation(eA[:, g % 2, h, :], columns(g, part)[:, h * P:(h + 1) * P], ACT.Exp,
                                             bias=nmax[:, g % 2, h:h + 1], scale=SCALE,
                                             accum_out=esum[:, g % 2, h:h + 1]).then_inc(exp_a, 1)
                else:
                    for i in range(2):
                        h = 2 * (part - 1) + i
                        nc.scalar.activation(eB[:, g % 2, h, :], columns(g, part)[:, i * S:(i + 1) * S], ACT.Exp,
                                             bias=nmax[:, g % 2, GH + h:GH + h + 1], scale=SCALE,
                                             accum_out=esum[:, g % 2, GH + h:GH + h + 1]).then_inc(exp_a, 1)

            def transposed(b, g):
                act.wait_ge(t_mm, 3 * (NG * b + g) + 1)
                nc.scalar.copy(pT[:, g % 2, 0, :], psT[0][:]).then_inc(pT_a, 1)

            for part in range(3):
                exps(0, 0, part)
            high_part(6)
            middle_part(6)
            exps(0, 1, 0)
            high_part(7)
            middle_part(7)

            def output(b, half):
                act.wait_ge(av_mm, NG * b + (half + 1) * NG // 2)
                nc.scalar.copy(oT[:, half, bass.ds(b * S, S)], psO[:, half * S:(half + 1) * S]).then_inc(o_a, 1)

            def batch(b, last):
                for g in range(NG):
                    if g + 1 < NG or not last:
                        exps(*following(b, g, 1), 1)
                        exps(*following(b, g, 1), 2)
                    transposed(b, g)
                    if g + 2 < NG or not last:
                        exps(*following(b, g, 2), 0)
                    if g == 0 and not is_first(b, g):
                        output(b - 1, 1)
                    if g == 2:
                        output(b, 0)

            batch(0, False)
            with act.Fori(1, B - 1) as b:
                batch(b, False)
            batch(B - 1, True)
            output(B - 1, 1)

        @block.vector
        def _(dve):
            nc.vector.tensor_scalar(ve[:], x_mv[:, :, 1], LN_EPS, None, ALU.add).then_inc(ve_v, 1)
            dve.wait_ge(rstd_g, 1)
            for t in range(TT):
                nc.vector.tensor_scalar(h_nat[:, t, :], x_sb[:, t, :], x_mv[:, t, 0:1], rstd[:, t:t + 1],
                                        ALU.subtract, ALU.mult).then_inc(h_v, 1)
            def rest_of(s):
                rows, tokens = qk_stage(s)
                dve.wait_ge(high_a, s + 1)
                at_least(dve, low_g, s - 1)
                nc.vector.scalar_tensor_tensor(out=rest[:, s % 2, :], in0=stage_bank(qk_number(s))[:], scalar=b_qk[:, rows:rows + 1],
                                               in1=parts[:, s % RING, 0, :], op0=ALU.add, op1=ALU.subtract).then_inc(rest_v, 1)

            for s in (0, 2):
                dve.wait_ge(pro_mm, ST_H + s + 1)
                nc.vector.tensor_copy(hT[:, s % 2, (s // 2) * HALF:(s // 2 + 1) * HALF], stage_bank(s)[:]).then_inc(pro_v, 1)
            dve.wait_ge(w_in, 80)

            def maxima(b, g, part):
                unit = 3 * (NG * b + g) + part
                heads = GH if part == 0 else 2
                first = (0, GH, GH + 2)[part]
                dve.wait_ge(s_mm, unit + 1)
                nc.vector.reduce_max(gmax[:, g % 2, first:first + heads], columns(g, part)[:].rearrange("p (h k) -> p h k", h=heads),
                                     axis=AX.X).then_inc(gmax_v, 1)
                dve.wait_ge(gmax_v, unit + 1)
                nc.vector.tensor_scalar(nmax[:, g % 2, first:first + heads], gmax[:, g % 2, first:first + heads], -SCALE, None,
                                        ALU.mult).then_inc(nmax_v, 1)

            def invert_sums(b, g, late):
                G = NG * b + g
                e = (eA, eB)[late]
                first = late * GH
                dve.wait_ge(exp_a, 2 * GH * G + (late + 1) * GH)
                if g == 0:
                    dve.wait_ge(consts_g, 5)
                    nc.vector.tensor_tensor(e[:, 0, 0:3, :], e[:, 0, 0:3, :], focus[:, :, 0:(late + 1) * P], ALU.mult).then_inc(focus_v, 1)
                    dve.wait_ge(focus_v, 2 * b + late + 1)
                    nc.vector.reduce_sum(esum[:, 0, first:first + 3], e[:, 0, 0:3, :], axis=AX.X).then_inc(fsum_v, 1)
                    dve.wait_ge(fsum_v, 2 * b + late + 1)
                nc.vector.reciprocal(rinv[:, g % 2, first:first + GH], esum[:, g % 2, first:first + GH]).then_inc(rinv_v, 1)

            def transposed(b, g):
                G = NG * b + g
                for r in range(1, 3):
                    dve.wait_ge(t_mm, 3 * G + r + 1)
                    nc.vector.tensor_copy(pT[:, g % 2, r, :], psT[r][:]).then_inc(pT_v, 1)

            def values(s):
                dve.wait_ge(pro_mm, ST_V + s + 1)
                nc.vector.tensor_tensor(v_all[:, 2 * s:2 * s + 2, :], stage_bank(ST_V + s)[:].rearrange("p (t d) -> p t d", t=2),
                                        b_v[:].unsqueeze(1).broadcast_to([P, 2, D]), ALU.add).then_inc(pro_v, 1)

            for s in range(4):
                rest_of(s)
            for s in range(4):
                values(s)
            for s in range(4, QK_FIRST):
                rest_of(s)
            for part in range(3):
                maxima(0, 0, part)
            invert_sums(0, 0, 0)
            maxima(0, 1, 0)
            rest_of(6)
            invert_sums(0, 0, 1)
            rest_of(7)

            def phi_bias_part(r):
                rows = slice(0, 96 - 32 * r)
                if r:
                    dve.wait_ge(left_v, r)
                nc.vector.tensor_copy(phib[rows, :], phi_b_rest[rows, :]).then_inc(phib_v, 1)

            def phi_bias_rest(r):
                rows = slice(0, 64 - 32 * r)
                dve.wait_ge(phib_v, r + 1)
                nc.vector.tensor_tensor(phi_b_rest[rows, :], phi_b_rest[rows, :], phib[rows, :], ALU.subtract).then_inc(left_v, 1)

            def batch(b, last):
                for g in range(NG):
                    more = g + 1 < NG or not last
                    if more:
                        if g + 1 == NG:
                            invert_sums(*following(b, g, 1), 0)
                        maxima(*following(b, g, 1), 1)
                        if g + 1 < NG:
                            invert_sums(*following(b, g, 1), 0)
                        maxima(*following(b, g, 1), 2)
                    transposed(b, g)
                    if more:
                        invert_sums(*following(b, g, 1), 1)
                    if g + 2 < NG or not last:
                        maxima(*following(b, g, 2), 0)
                    if last and g == 0:
                        phi_bias_rest(0)

            batch(0, False)
            nc.vector.memset(ones[:], 0.0).then_inc(ones_v, 1)
            dve.wait_ge(ones_v, 1)
            for r in range(3):
                nc.vector.memset(ones[32 * r:32 * r + 1, :], 1.0).then_inc(ones_v, 1)
            dve.wait_ge(phi_in, 16)
            phi_bias_part(0)
            with dve.Fori(1, B - 1) as b:
                batch(b, False)
            batch(B - 1, True)
            for r in range(1, 3):
                phi_bias_part(r)
                if r < 2:
                    phi_bias_rest(r)
            dve.wait_ge(xb_g, 1)
            for t in range(TT):
                dve.wait_ge(out_mm, t + 1)
                nc.vector.tensor_tensor(x_sb[:, t, :], bank[t][:, 0:D], x_sb[:, t, :], ALU.add).then_inc(out_v, 1)
                if t:
                    row_statistics(dve, nc, x_sb, x_stats, x_mv, t - 1, out_v, t, xst_v, xmv_v)
            row_statistics(dve, nc, x_sb, x_stats, x_mv, TT - 1, out_v, TT, xst_v, xmv_v)


def soft_moe(nc, x_sb, x_mv, ident, disp, disp_at, ones, phib, expert_w, expert_b, out):
    NE, HID = expert_w.shape[0], expert_w.shape[2]
    SL = disp.shape[2]
    NS = SL // NE
    ST = SL // P
    EPT = P // NS
    LB = SL // 512
    LR = 3
    WS = 4
    DE = 3 * NE // 8
    EARLY = 4
    LOW, HIGH = -33000.0, 65000.0
    HALF = B * S // 2
    with ExitStack() as st:
        def sb(name, shape, dt=F32):
            return st.enter_context(nc.sbuf_tensor(name, shape, dt))

        def sem(name):
            return st.enter_context(nc.semaphore(name))

        combT_at = next_address(nc)
        combT = sb("combT", [P, ST, B * S])
        phiT_at = next_address(nc)
        phiT = sb("phiT", [P, DH, SL])
        logits_at = next_address(nc)
        logits = sb("logits", [P, LR, SL])
        dwork = sb("dwork", [P, SL])
        h_nat = sb("h3_nat", [P, TT, D])
        xc = sb("xc", [P, 2, D])
        xh = sb("xh", [P, 2, D])
        xhT = sb("xhT", [P, 2, DH, P])
        ve = sb("ve3", [P, TT])
        rstd = sb("rstd3", [P, TT])
        power = sb("power3", [P, TT])
        sstats = sb("sstats", [P, 2, 6])
        smv = sb("smv", [P, 2, 2])
        sve = sb("sve", [P, 2])
        srstd = sb("srstd", [P, 2])
        snmr = sb("snmr", [P, 2])
        dmax = sb("dmax", [P, NE])
        dsum = sb("dsum", [P, NE])
        dinv = sb("dinv", [P, NE])
        cmax = sb("cmax3", [P, NS])
        csum = sb("csum3", [P, NS])
        cinv = sb("cinv", [P, NS])

        hT = disp[:, TT - 1, :].rearrange("p (a t) -> p a t", a=DH)
        phi_nat, _, _ = phi_places(disp)
        mixed = phiT[:].rearrange("p a s -> p (a s)").rearrange("p (k d) -> p k d", k=ST)
        comb_hi = nc.alloc_sbuf_tensor_at("comb_hi", [P, TT, SL], F32R, offset=disp_at)
        comb_lo = nc.alloc_sbuf_tensor_at("comb_lo", [P, ST, B * S], F32R, offset=combT_at)
        mixed_lo = nc.alloc_sbuf_tensor_at("mixed_lo", [P, ST, HID], F32R, offset=phiT_at)
        mixed_hi = nc.alloc_sbuf_tensor_at("mixed_hi", [P, ST, HID], F32R, offset=logits_at + 2 * SL * 4)
        MC = 4
        w_exp = [a.rearrange("p (n c h) -> p n c h", n=EPT, c=DH)
                 for a in (logits[:, 2, :], dwork[:], logits[:, 0, :], logits[:, 1, :])]

        bank = [st.enter_context(nc.psum_tensor(f"pf{i}", [P, 512], F32)) for i in range(8)]
        psL, psC = bank[0:4], bank[4:6]
        psE, psT = bank[2:4], bank[4:6]

        def psX(s):
            return bank[6 + s // 2][:, (s % 2) * D:(s % 2 + 1) * D] if s < EARLY else bank[s % 2][:, 0:D]

        psY = bank[6:8] + bank[0:6]

        w_in, eb_in = [sem(f"w3_in{k}") for k in range(WS)], sem("eb_in")
        ve_v, rstd_g, h_v = sem("ve3_v"), sem("rstd3_g"), sem("h3_v")
        const_g = sem("const3_g")
        pro_mm, pro_v, pro_a = sem("pro3_mm"), sem("pro3_v"), sem("pro3_a")
        L_mm, L_a = sem("L_mm"), sem("L_a")
        cmax_v, csub_g, cexp_a, csum_v, cinv_v, cmul_g = (sem(n) for n in ("cmax3_v", "csub_g", "cexp_a", "csum3_v", "cinv_v", "cmul_g"))
        dmax_v, dsub_v, dexp_a, dsum_v, dinv_v, dmul_v, dmul_g = (sem(n) for n in ("dmax_v", "dsub_v", "dexp_a", "dsum_v", "dinv_v", "dmul_v", "dmul_g"))
        cT_mm, cT_a = sem("cT_mm"), sem("cT_a")
        xs_mm, clip_v, sst_v, smv_v, sve_v, srstd_g, snmr_v, tanh_a = (sem(n) for n in (
            "xs_mm", "clip_v", "sst_v", "smv_v", "sve_v", "srstd_g", "snmr_v", "tanh_a"))
        xT_mm, xT_a, e_mm, mixed_v = sem("xT_mm"), sem("xT_a"), sem("e_mm"), sem("mixed_v")
        chigh_a, clow_v, mhigh_a, mlow_v = (sem(n) for n in ("chigh_a", "clow_v", "mhigh_a", "mlow_v"))
        y_mm, y_v, out_done = sem("y_mm"), sem("y_v"), sem("out_done")

        NPHI = DH * LB
        NH = 4

        def cut_at(s):
            return () if s < 4 else (2 * s - 8, 2 * s - 7) if s < 8 else (s,)

        def by_expert(a):
            return a.rearrange("p (n s) -> p n s", s=NS)

        def by_slot(a):
            return a.rearrange("p (n s) -> p s n", s=NS)

        block = st.enter_context(nc.Block())

        @block.sync
        def _(sp):
            experts = expert_w.rearrange("(k n) (c p) h -> k p n c h", n=EPT, p=P)

            def load(k):
                sp.dma_start(w_exp[k % WS], experts[k]).then_inc(w_in[k % WS], 16)

            sp.wait_ge(L_mm, LB * TT)
            for j in range(EPT):
                sp.dma_start(mixed[j * NS:(j + 1) * NS, :, :],
                             expert_b.rearrange("(k n) h -> n k h", n=EPT)[j:j + 1].broadcast_to([NS, ST, HID])).then_inc(eb_in, 16)
            sp.wait_ge(dmul_v, TT)
            freed = [(cT_mm, LB * (TT - 2)), (dmul_g, TT), (cT_mm, LB * (TT - 1)), (cT_mm, LB * TT)]
            for k in range(ST):
                if k < WS:
                    sp.wait_ge(*freed[k])
                else:
                    sp.wait_ge(e_mm, k - WS + 1)
                load(k)
            rows = out.rearrange("b (q p) d -> (b q) p d", p=P)
            for t in range(TT):
                sp.wait_ge(y_v, t + 1)
                sp.dma_start(rows[t], x_sb[:, t, :]).then_inc(out_done, 16)
            sp.wait_ge(out_done, 16 * TT)

        @block.gpsimd
        def _(pool):
            nc.gpsimd.memset(power[:], -0.5).then_inc(const_g, 1)
            pool.wait_ge(const_g, 1)
            pool.wait_ge(ve_v, 1)
            nc.gpsimd.tensor_tensor(rstd[:], ve[:], power[:], ALU.pow).then_inc(rstd_g, 1)

            def subtract(t):
                c = by_slot(logits[:, t % LR, :])
                pool.wait_ge(cmax_v, t + 1)
                pool.wait_ge(dsub_v, t + 1)
                nc.gpsimd.tensor_tensor(c, c, cmax[:].unsqueeze(2).broadcast_to([P, NS, NE]), ALU.subtract).then_inc(csub_g, 1)

            def divide(t):
                c = by_slot(logits[:, t % LR, :])
                pool.wait_ge(cinv_v, t + 1)
                nc.gpsimd.tensor_tensor(c, c, cinv[:].unsqueeze(2).broadcast_to([P, NS, NE]), ALU.mult).then_inc(cmul_g, 1)

            def divide_dispatch(t):
                pool.wait_ge(dinv_v, t + 1)
                nc.gpsimd.tensor_tensor(by_expert(disp[:, t, :])[:, DE:, :], by_expert(dwork[:])[:, DE:, :],
                                        dinv[:, DE:].unsqueeze(2).broadcast_to([P, NE - DE, NS]), ALU.mult).then_inc(dmul_g, 1)

            for t in range(TT):
                subtract(t)
                divide_dispatch(t)
                if t:
                    divide(t - 1)
            divide(TT - 1)
            for s in range(ST):
                pool.wait_ge(sve_v, s + 1)
                nc.gpsimd.tensor_tensor(srstd[:, s % 2:s % 2 + 1], sve[:, s % 2:s % 2 + 1], power[:, 0:1], ALU.pow).then_inc(srstd_g, 1)

        @block.tensor
        def _(pe):
            for s in range(NPHI):
                for j in range(4):
                    last = nc.tensor.transpose(bank[s][:, j * P:(j + 1) * P],
                                               phi_nat[:, (s % LB) * 4 + j, (s // LB) * P:(s // LB + 1) * P], ident[:])
                last.then_inc(pro_mm, 1)
            for s in range(NH):
                pe.wait_ge(pro_a, s + 1)
                pe.wait_ge(h_v, (s // 2 + 1) * 4)
                for t in range(4):
                    last = nc.tensor.transpose(bank[s][:, t * P:(t + 1) * P],
                                               h_nat[:, (s // 2) * 4 + t, (s % 2) * P:(s % 2 + 1) * P], ident[:])
                last.then_inc(pro_mm, 1)
            pe.wait_ge(pro_v, 2)
            pe.wait_ge(pro_a, NPHI + 2)

            def logit(t, first, end):
                for j in range(first, end):
                    if t:
                        pe.wait_ge(L_a, LB * (t - 1) + j + 1)
                    cols = slice(j * 512, (j + 1) * 512)
                    nc.tensor.matmul(psL[j][:], ones[0:96, :], phib[0:96, cols], start=True, stop=False)
                    for c in range(DH):
                        last = nc.tensor.matmul(psL[j][:], hT[:, c, t * P:(t + 1) * P], phiT[:, c, cols],
                                                start=False, stop=c == DH - 1)
                    last.then_inc(L_mm, 1)

            def transpose_combine(t):
                pe.wait_ge(cmul_g, t + 1)
                for k in range(LB):
                    at_least(pe, cT_a, LB * t + k - 1)
                    for j in range(4):
                        last = nc.tensor.transpose(psC[k % 2][:, j * P:(j + 1) * P],
                                                   logits[:, t % LR, (4 * k + j) * P:(4 * k + j + 1) * P], ident[:])
                    last.then_inc(cT_mm, 1)

            def early_inputs(t):
                pe.wait_ge(dmul_v, t + 1)
                pe.wait_ge(dmul_g, t + 1)
                for s in range(EARLY):
                    last = nc.tensor.matmul(psX(s), disp[:, t, s * P:(s + 1) * P], h_nat[:, t, :],
                                            start=t == 0 and s % 2 == 0, stop=t == TT - 1, skip_group_check=True)
                if t == TT - 1:
                    last.then_inc(xs_mm, EARLY)

            logit(0, 0, LB)
            for t in range(TT):
                if t + 1 < TT:
                    logit(t + 1, 0, LB)
                if t >= 2:
                    transpose_combine(t - 2)
                if t:
                    early_inputs(t - 1)

            def slot_inputs(s):
                if s >= EARLY + 2:
                    pe.wait_ge(clip_v, s - 1)
                for t in range(TT):
                    last = nc.tensor.matmul(psX(s), disp[:, t, s * P:(s + 1) * P], h_nat[:, t, :],
                                            start=t == 0, stop=t == TT - 1)
                last.then_inc(xs_mm, 1)

            def transpose_inputs(s):
                pe.wait_ge(tanh_a, s + 1)
                at_least(pe, xT_a, s - 1)
                for c in range(DH):
                    last = nc.tensor.transpose(psT[s % 2][:, c * P:(c + 1) * P], xh[:, s % 2, c * P:(c + 1) * P], ident[:])
                last.then_inc(xT_mm, 1)

            def experts(s):
                pe.wait_ge(xT_a, s + 1)
                pe.wait_ge(w_in[s % WS], 16 * (s // WS + 1))
                at_least(pe, mixed_v, s - 1)
                for n in range(EPT):
                    rows = slice(n * NS, (n + 1) * NS)
                    for c in range(DH):
                        last = nc.tensor.matmul(psE[s % 2][rows, 0:HID], xhT[:, s % 2, c, rows], w_exp[s % WS][:, n, c, :],
                                                start=c == 0, stop=c == 1)
                last.then_inc(e_mm, 1)

            early_inputs(TT - 1)
            pe.wait_ge(L_a, LB * TT)
            slot_inputs(EARLY)
            transpose_combine(TT - 2)
            slot_inputs(EARLY + 1)
            transpose_combine(TT - 1)
            pe.wait_ge(cT_a, LB * TT)
            for s in range(ST):
                if EARLY + 2 <= s + 1 < ST:
                    slot_inputs(s + 1)
                transpose_inputs(s)
                if s:
                    experts(s - 1)
            experts(ST - 1)
            for t in range(TT):
                for s in range(ST):
                    if t == 0 and s % MC == 0:
                        pe.wait_ge(clow_v, s + MC)
                        pe.wait_ge(mlow_v, s // MC + 1)
                    if t == 1 and s == 0:
                        pe.wait_ge(mixed_v, ST)
                    hi, lo = comb_hi[:, t, s * P:(s + 1) * P], comb_lo[:, s, t * P:(t + 1) * P]
                    nc.tensor.matmul(psY[t][:, 0:HID], hi, mixed_hi[:, s, :], start=s == 0, stop=False)
                    nc.tensor.matmul(psY[t][:, 0:HID], hi, mixed_lo[:, s, :], start=False, stop=False)
                    last = nc.tensor.matmul(psY[t][:, 0:HID], lo, mixed_hi[:, s, :], start=False, stop=s == ST - 1)
                last.then_inc(y_mm, 1)

        @block.scalar
        def _(act):
            for s in range(NPHI):
                act.wait_ge(pro_mm, s + 1)
                nc.scalar.copy(phiT[:, s // LB, (s % LB) * 512:(s % LB + 1) * 512], bank[s][:]).then_inc(pro_a, 1)
            for s in (1, 3):
                act.wait_ge(pro_mm, NPHI + s + 1)
                nc.scalar.copy(hT[:, s % 2, (s // 2) * HALF:(s // 2 + 1) * HALF], bank[s][:]).then_inc(pro_a, 1)

            def logits_out(t):
                if t >= LR:
                    act.wait_ge(cT_mm, LB * (t - LR + 1))
                for j in range(LB):
                    act.wait_ge(L_mm, LB * t + j + 1)
                    nc.scalar.copy(logits[:, t % LR, j * 512:(j + 1) * 512], psL[j][:]).then_inc(L_a, 1)

            def combine_out(t, first, end):
                for k in range(first, end):
                    act.wait_ge(cT_mm, LB * t + k + 1)
                    nc.scalar.copy(combT[:, 4 * k:4 * k + 4, t * P:(t + 1) * P],
                                   psC[k % 2][:].rearrange("p (j q) -> p j q", j=4)).then_inc(cT_a, 1)

            logits_out(0)
            for t in range(TT):
                act.wait_ge(dsub_v, t + 1)
                nc.scalar.activation(dwork[:], dwork[:], ACT.Exp).then_inc(dexp_a, 1)
                if t >= 2:
                    combine_out(t - 2, 0, LB)
                if t + 1 < TT:
                    logits_out(t + 1)
                act.wait_ge(csub_g, t + 1)
                nc.scalar.activation(logits[:, t % LR, :], logits[:, t % LR, :], ACT.Exp).then_inc(cexp_a, 1)
            for t in range(TT - 2, TT):
                combine_out(t, 0, LB)

            for s in range(ST):
                act.wait_ge(snmr_v, s + 1)
                at_least(act, xT_mm, s - 1)
                nc.scalar.activation(xh[:, s % 2, :], xc[:, s % 2, :], ACT.Tanh, bias=snmr[:, s % 2:s % 2 + 1],
                                     scale=srstd[:, s % 2:s % 2 + 1]).then_inc(tanh_a, 1)
                act.wait_ge(xT_mm, s + 1)
                at_least(act, e_mm, s - 1)
                nc.scalar.copy(xhT[:, s % 2, :, :].rearrange("p c s -> p (c s)"), psT[s % 2][:, 0:DH * P]).then_inc(xT_a, 1)
                for k in cut_at(s):
                    if k == 0:
                        act.wait_ge(cT_a, LB * TT)
                    act.wait_ge(xs_mm, k + 1)
                    nc.scalar.copy(comb_hi[:, :, k * P:(k + 1) * P],
                                   combT[:, k, :].rearrange("p (t q) -> p t q", t=TT)).then_inc(chigh_a, 1)
            act.wait_ge(e_mm, ST - 2)
            for j in range(ST // MC):
                act.wait_ge(mixed_v, MC * (j + 1))
                nc.scalar.copy(mixed_hi[:, j * MC:(j + 1) * MC, :], mixed[:, j * MC:(j + 1) * MC, :]).then_inc(mhigh_a, 1)

        @block.vector
        def _(dve):
            nc.vector.tensor_scalar(ve[:], x_mv[:, :, 1], LN_EPS, None, ALU.add).then_inc(ve_v, 1)
            dve.wait_ge(rstd_g, 1)
            for t in range(TT):
                nc.vector.tensor_scalar(h_nat[:, t, :], x_sb[:, t, :], x_mv[:, t, 0:1], rstd[:, t:t + 1],
                                        ALU.subtract, ALU.mult).then_inc(h_v, 1)
            for s in (0, 2):
                dve.wait_ge(pro_mm, NPHI + s + 1)
                nc.vector.tensor_copy(hT[:, s % 2, (s // 2) * HALF:(s // 2 + 1) * HALF], bank[s][:]).then_inc(pro_v, 1)

            def combine_sum(t):
                dve.wait_ge(cexp_a, t + 1)
                nc.vector.reduce_sum(csum[:], by_slot(logits[:, t % LR, :]), axis=AX.X).then_inc(csum_v, 1)
                dve.wait_ge(csum_v, t + 1)
                at_least(dve, cmul_g, t)
                nc.vector.reciprocal(cinv[:], csum[:]).then_inc(cinv_v, 1)

            for t in range(TT):
                row = logits[:, t % LR, :]
                work = by_expert(dwork[:])
                dve.wait_ge(L_a, LB * (t + 1))
                nc.vector.reduce_max(dmax[:], by_expert(row), axis=AX.X).then_inc(dmax_v, 1)
                at_least(dve, csub_g, t)
                nc.vector.reduce_max(cmax[:], by_slot(row), axis=AX.X).then_inc(cmax_v, 1)
                dve.wait_ge(dmax_v, t + 1)
                at_least(dve, dmul_v, t)
                at_least(dve, dmul_g, t)
                nc.vector.tensor_tensor(work, by_expert(row), dmax[:].unsqueeze(2).broadcast_to([P, NE, NS]),
                                        ALU.subtract).then_inc(dsub_v, 1)
                if t:
                    combine_sum(t - 1)
                dve.wait_ge(dexp_a, t + 1)
                nc.vector.reduce_sum(dsum[:], work, axis=AX.X).then_inc(dsum_v, 1)
                dve.wait_ge(dsum_v, t + 1)
                nc.vector.reciprocal(dinv[:], dsum[:]).then_inc(dinv_v, 1)
                dve.wait_ge(dinv_v, t + 1)
                nc.vector.tensor_tensor(by_expert(disp[:, t, :])[:, 0:DE, :], work[:, 0:DE, :],
                                        dinv[:, 0:DE].unsqueeze(2).broadcast_to([P, DE, NS]),
                                        ALU.mult).then_inc(dmul_v, 1)
            combine_sum(TT - 1)

            def inputs(s):
                r = s % 2
                dve.wait_ge(xs_mm, s + 1)
                at_least(dve, tanh_a, s - 1)
                nc.vector.tensor_scalar(xc[:, r, :], psX(s), LOW, HIGH, ALU.max, ALU.min).then_inc(clip_v, 1)
                dve.wait_ge(clip_v, s + 1)
                nc.vector.bn_stats(sstats[:, r, :], xc[:, r, :]).then_inc(sst_v, 1)
                dve.wait_ge(sst_v, s + 1)
                nc.vector.bn_aggr(smv[:, r, :], sstats[:, r, :]).then_inc(smv_v, 1)
                dve.wait_ge(smv_v, s + 1)
                nc.vector.tensor_scalar(sve[:, r:r + 1], smv[:, r, 1:2], LN_EPS, None, ALU.add).then_inc(sve_v, 1)
                dve.wait_ge(srstd_g, s + 1)
                nc.vector.tensor_scalar(snmr[:, r:r + 1], smv[:, r, 0:1], -1.0, srstd[:, r:r + 1],
                                        ALU.mult, ALU.mult).then_inc(snmr_v, 1)

            def outputs(s):
                dve.wait_ge(e_mm, s + 1)
                nc.vector.tensor_tensor(mixed[:, s, :], psE[s % 2][:, 0:HID], mixed[:, s, :], ALU.add).then_inc(mixed_v, 1)

            def combine_low(k):
                dve.wait_ge(chigh_a, k + 1)
                nc.vector.tensor_tensor(comb_lo[:, k, :].rearrange("p (t q) -> p t q", t=TT),
                                        combT[:, k, :].rearrange("p (t q) -> p t q", t=TT),
                                        comb_hi[:, :, k * P:(k + 1) * P].bitcast(F32), ALU.subtract).then_inc(clow_v, 1)

            def mixed_low(j):
                tiles = slice(j * MC, (j + 1) * MC)
                dve.wait_ge(mhigh_a, j + 1)
                nc.vector.tensor_tensor(mixed_lo[:, tiles, :], mixed[:, tiles, :], mixed_hi[:, tiles, :].bitcast(F32),
                                        ALU.subtract).then_inc(mlow_v, 1)

            dve.wait_ge(eb_in, 16 * EPT)
            for s in range(ST):
                inputs(s)
                if s >= 2:
                    outputs(s - 2)
                for k in cut_at(s - 1):
                    combine_low(k)
            combine_low(ST - 1)
            outputs(ST - 2)
            mixed_low(0)
            mixed_low(1)
            outputs(ST - 1)
            mixed_low(2)
            mixed_low(3)
            for t in range(TT):
                dve.wait_ge(y_mm, t + 1)
                nc.vector.tensor_tensor(x_sb[:, t, :], psY[t][:, 0:HID], x_sb[:, t, :], ALU.add).then_inc(y_v, 1)


def perceiver_block(nc, x, ctx, Wq, bq, Wk, bk, Wv, bv, Wo, bo, c_attn_w, c_attn_b, c_proj_w, c_proj_b,
                    phi_w, phi_b, expert_w, expert_b, out):
    with ExitStack() as st:
        x_sb = st.enter_context(nc.sbuf_tensor("x_sb", [P, TT, D], F32))
        x_stats = st.enter_context(nc.sbuf_tensor("x_stats", [P, TT, 6], F32))
        x_mv = st.enter_context(nc.sbuf_tensor("x_mv", [P, TT, 2], F32))
        ident = st.enter_context(nc.sbuf_tensor("ident", [P, P], F32))
        cross_attention(nc, x_sb, x_stats, x_mv, ident, x, ctx, Wq, bq, Wk, bk, Wv, bv, Wo, bo)
        SL = phi_w.shape[0]
        disp_at = next_address(nc)
        disp = st.enter_context(nc.sbuf_tensor("disp", [P, TT, SL], F32))
        ones = st.enter_context(nc.sbuf_tensor("ones", [P, P], BF16))
        phib = st.enter_context(nc.sbuf_tensor("phib", [P, SL], BF16))
        qk_dram = nc.dram_tensor("qk_parts_dram", (4, 3, P, B * S), BF16).ap()
        self_attention(nc, x_sb, x_stats, x_mv, ident, disp, ones, phib, qk_dram, c_attn_w, c_attn_b, c_proj_w, c_proj_b, phi_w, phi_b)
        soft_moe(nc, x_sb, x_mv, ident, disp, disp_at, ones, phib, expert_w, expert_b, out)


_INS = ["x", "ctx_1024", "L0_xattn_Wq", "L0_xattn_bq", "L0_xattn_Wk", "L0_xattn_bk", "L0_xattn_Wv", "L0_xattn_bv",
        "L0_xattn_Wo", "L0_xattn_bo", "L0_attn_c_attn_w", "L0_attn_c_attn_b", "L0_attn_c_proj_w", "L0_attn_c_proj_b",
        "L0_ffn_phi_w", "L0_ffn_phi_b", "L0_ffn_expert_w", "L0_ffn_expert_b"]


def kernel(**inputs):
    import numpy as np
    import concourse.bacc as bacc
    from concourse.bass_utils import run_bass_kernel_spmd

    nc = bacc.Bacc("TRN2", target_bir_lowering=False, num_devices=1)
    arrays, args = {}, []
    for name in _INS:
        a = np.ascontiguousarray(inputs[name])
        arrays[f"in_{name}_dram"] = a
        args.append(nc.dram_tensor(f"in_{name}_dram", a.shape, mybir.dt.from_np(a.dtype), kind="ExternalInput").ap())
    out = nc.dram_tensor("out_dram", (B, S, D), F32, kind="ExternalOutput").ap()
    perceiver_block(nc, *args, out)
    r = run_bass_kernel_spmd(nc, [arrays], core_ids=[0])
    return r.results[0]["out_dram"]
```
